# Optimizing a Trainium2 kernel written in Bass

```python
import numpy as np
import jax
import jax.numpy as jnp

def _softmax(x, axis=-1):
    return jax.nn.softmax(x, axis=axis)

def _gelu(x):
    return jax.nn.gelu(x, approximate=True)

def _silu(x):
    return jax.nn.silu(x)

def _sigmoid(x):
    return jax.nn.sigmoid(x)

def _layernorm(x, axis=-1, eps=1e-05):
    m = jnp.mean(x, axis=axis, keepdims=True)
    v = jnp.var(x, axis=axis, keepdims=True)
    return (x - m) / jnp.sqrt(v + eps)

def _scatter_add(tgt, idx, src, axis=0):
    return tgt.at[idx].add(src)

def _segment_sum(src, seg, n):
    return jax.ops.segment_sum(src, seg, n)
kernel_name = 'mk_decoder_postln_d1_seqx_r4_a7d312'

def setup_inputs(seed: int=0):
    np.random.seed(seed)
    _w = jnp.asarray

    def _rec_inputs():
        import jax
        import jax.numpy as jnp
        _rk = jax.random.key(seed)
        x = 7.22e-05 + 1 * jax.random.normal(jax.random.fold_in(_rk, 1), (16, 128, 256), jnp.float32)
        _lenS = 128 - jax.random.randint(jax.random.fold_in(_rk, 7), (16,), 0, max(1, 128 // 4) + 1, jnp.int32)
        _lenS2 = 128 - jax.random.randint(jax.random.fold_in(_rk, 8), (16,), 0, max(1, 128 // 4) + 1, jnp.int32)
        _ctx_1024P = jax.random.normal(jax.random.fold_in(_rk, 11), (16, 16, 256), jnp.float32)
        _ctx_1024c = jax.random.dirichlet(jax.random.fold_in(_rk, 511), 0.3 * jnp.ones((16,), jnp.float32), (16, 128))
        _ctx_1024t = jnp.einsum('bsk,bkd->bsd', _ctx_1024c, _ctx_1024P)
        _ctx_1024t = _ctx_1024t * jax.lax.rsqrt(jnp.mean(jnp.square(_ctx_1024t)) + 1e-12) * 0.953939
        ctx_1024 = 4.13588e-05 + 0.999923 * (_ctx_1024t + 0.3 * jax.random.normal(jax.random.fold_in(_rk, 611), (16, 128, 256), jnp.float32))
        return (x, ctx_1024)
    x, ctx_1024 = _rec_inputs()

    def _L0_attn_setup():
        import jax, jax.numpy as jnp
        import numpy as np
        DIM, SSM, RNN = (256, 64, 128)
        key = jax.random.key(seed)
        ks = jax.random.split(key, 16)
        s = 0.02
        B, N = (8, 512)
        return {'x': jax.random.normal(ks[0], (B, N, DIM), jnp.float32), 'A': jax.random.normal(ks[1], (SSM, SSM), jnp.float32) * s, 'Bw': jax.random.normal(ks[2], (SSM, DIM), jnp.float32) * s, 'Bb': jnp.zeros((SSM,), jnp.float32), 'Cw': jax.random.normal(ks[3], (DIM, SSM), jnp.float32) * s, 'Cb': jnp.zeros((DIM,), jnp.float32), 'Dw': jax.random.normal(ks[4], (DIM, DIM), jnp.float32) * s, 'Db': jnp.zeros((DIM,), jnp.float32), 'W_ih': jax.random.normal(ks[5], (3 * RNN, DIM), jnp.float32) * s, 'b_ih': jnp.zeros((3 * RNN,), jnp.float32), 'W_hh': jax.random.normal(ks[6], (3 * RNN, RNN), jnp.float32) * s, 'b_hh': jnp.zeros((3 * RNN,), jnp.float32), 'proj_w': jax.random.normal(ks[7], (DIM, RNN), jnp.float32) * s, 'proj_b': jnp.zeros((DIM,), jnp.float32), 'gate_w': jax.random.normal(ks[8], (2, DIM), jnp.float32) * s, 'gate_b': jnp.zeros((2,), jnp.float32)}
    _L0_attn_all = _L0_attn_setup()
    _L0_attn_in = {k: v for k, v in _L0_attn_all.items() if k in ('A', 'Bw', 'Bb', 'Cw', 'Cb', 'Dw', 'Db', 'W_ih', 'b_ih', 'W_hh', 'b_hh', 'proj_w', 'proj_b', 'gate_w', 'gate_b')}
    del _L0_attn_all

    def _L0_xattn_setup():
        import jax, jax.numpy as jnp
        import numpy as np
        THETA = 10000.0
        SCALE_BASE = 512.0
        GAMMA = 0.96875

        def _dup_interleave(x):
            return jnp.repeat(x, 2, axis=-1)

        def _xpos(x, offset, inverse_scale):
            L, d = (x.shape[-2], x.shape[-1])
            half = d // 2
            base = (jnp.arange(0, d, 2, dtype=x.dtype) + 0.4 * d) / (1.4 * d)
            pos = jnp.arange(offset, offset + L, dtype=x.dtype)
            scale = base[None, :] ** (pos[:, None] / SCALE_BASE)
            freqs = 1.0 / THETA ** (jnp.arange(half, dtype=x.dtype) / half)
            sin_in = pos[:, None] * freqs[None, :]
            if inverse_scale:
                scale = 1.0 / scale
            sin = _dup_interleave(jnp.sin(sin_in) * scale)
            cos = _dup_interleave(jnp.cos(sin_in) * scale)
            rot = jnp.stack((-x[..., 1::2], x[..., ::2]), axis=-1).reshape(x.shape)
            return x * cos + rot * sin

        def _decay_mask(L, gamma, dtype):
            u = jnp.arange(L, dtype=dtype)[:, None]
            v = jnp.arange(L, dtype=dtype)[None, :]
            return jnp.where(u >= v, gamma ** (u - v), jnp.zeros((), dtype))
        key = jax.random.key(seed)
        ks = jax.random.split(key, 6)
        B, L, E = (2, 1024, 256)
        query = jax.random.normal(ks[0], (B, L, E), jnp.float32)
        k_in = jax.random.normal(ks[1], (B, L, E), jnp.float32)
        value = jax.random.normal(ks[2], (B, L, E), jnp.float32)
        s = 1.0 / np.sqrt(E)
        Wq = jax.random.normal(ks[3], (E, E), jnp.float32) * s
        Wk = jax.random.normal(ks[4], (E, E), jnp.float32) * s
        Wv = jax.random.normal(ks[5], (E, E), jnp.float32) * s
        return {'query': query, 'key': k_in, 'value': value, 'Wq': Wq, 'Wk': Wk, 'Wv': Wv}
    _L0_xattn_all = _L0_xattn_setup()
    _L0_xattn_in = {k: v for k, v in _L0_xattn_all.items() if k in ('Wq', 'Wk', 'Wv')}
    del _L0_xattn_all

    def _L0_ffn_setup():
        import jax, jax.numpy as jnp
        import numpy as np
        D_MODEL = 256
        FF = 1024
        E = 8
        TOP_K = 2
        CAP_FACTOR = 1.25
        B, T = (4, 512)

        def _moe_forward(x, gate_w, gate_b, w1, b1, w2, b2):
            Bb, Tt, d = x.shape
            S = Bb * Tt
            C = int(CAP_FACTOR * S / E)
            xf = x.reshape(S, d)
            logits = xf @ gate_w + gate_b
            probs = jax.nn.softmax(logits, axis=1)
            topk_p, topk_i = jax.lax.top_k(probs, TOP_K)
            topk_pn = topk_p / jnp.sum(topk_p, axis=1, keepdims=True)
            rows = jnp.arange(S)
            w_te = jnp.zeros((S, E), xf.dtype).at[rows[:, None], topk_i].set(topk_pn)
            mask = jnp.zeros((S, E), bool).at[rows[:, None], topk_i].set(True)
            rank = jnp.cumsum(mask.astype(jnp.int32), axis=0)
            slot = jnp.where(mask & (rank <= C), rank - 1, C)
            e_grid = jnp.broadcast_to(jnp.arange(E), (S, E))
            t_grid = jnp.broadcast_to(rows[:, None], (S, E))
            buf = jnp.full((E, C + 1), S, jnp.int32).at[e_grid, slot].set(t_grid)
            idx = buf[:, :C]
            valid = idx < S
            x_pad = jnp.concatenate([xf, jnp.zeros((1, d), xf.dtype)], axis=0)
            xin = x_pad[idx]
            h = jax.nn.relu(jnp.einsum('ecd,edh->ech', xin, w1) + b1[:, None, :])
            out = jnp.einsum('ech,ehd->ecd', h, w2) + b2[:, None, :]
            w_pad = jnp.concatenate([w_te, jnp.zeros((1, E), xf.dtype)], axis=0)
            tok_w = w_pad[idx, jnp.arange(E)[:, None]]
            out = out * jnp.where(valid, tok_w, 0.0)[:, :, None]
            final = jnp.zeros((S + 1, d), xf.dtype).at[idx.reshape(-1)].add(out.reshape(-1, d))[:S]
            return final.reshape(Bb, Tt, d)
        key = jax.random.key(seed)
        ks = jax.random.split(key, 7)
        s = 0.02
        return {'x': jax.random.normal(ks[0], (B, T, D_MODEL), jnp.float32), 'gate_w': jax.random.normal(ks[1], (D_MODEL, E), jnp.float32) * s, 'gate_b': jnp.zeros((E,), jnp.float32), 'w1': jax.random.normal(ks[2], (E, D_MODEL, FF), jnp.float32) * s, 'b1': jnp.zeros((E, FF), jnp.float32), 'w2': jax.random.normal(ks[3], (E, FF, D_MODEL), jnp.float32) * s, 'b2': jnp.zeros((E, D_MODEL), jnp.float32)}
    _L0_ffn_all = _L0_ffn_setup()
    _L0_ffn_in = {k: v for k, v in _L0_ffn_all.items() if k in ('gate_w', 'gate_b', 'w1', 'b1', 'w2', 'b2')}
    del _L0_ffn_all
    return {'x': x, 'ctx_1024': ctx_1024, 'L0_attn_A': _L0_attn_in['A'], 'L0_attn_Bw': _L0_attn_in['Bw'], 'L0_attn_Bb': _L0_attn_in['Bb'], 'L0_attn_Cw': _L0_attn_in['Cw'], 'L0_attn_Cb': _L0_attn_in['Cb'], 'L0_attn_Dw': _L0_attn_in['Dw'], 'L0_attn_Db': _L0_attn_in['Db'], 'L0_attn_W_ih': _L0_attn_in['W_ih'], 'L0_attn_b_ih': _L0_attn_in['b_ih'], 'L0_attn_W_hh': _L0_attn_in['W_hh'], 'L0_attn_b_hh': _L0_attn_in['b_hh'], 'L0_attn_proj_w': _L0_attn_in['proj_w'], 'L0_attn_proj_b': _L0_attn_in['proj_b'], 'L0_attn_gate_w': _L0_attn_in['gate_w'], 'L0_attn_gate_b': _L0_attn_in['gate_b'], 'L0_xattn_Wq': _L0_xattn_in['Wq'], 'L0_xattn_Wk': _L0_xattn_in['Wk'], 'L0_xattn_Wv': _L0_xattn_in['Wv'], 'L0_ffn_gate_w': _L0_ffn_in['gate_w'], 'L0_ffn_gate_b': _L0_ffn_in['gate_b'], 'L0_ffn_w1': _L0_ffn_in['w1'], 'L0_ffn_b1': _L0_ffn_in['b1'], 'L0_ffn_w2': _L0_ffn_in['w2'], 'L0_ffn_b2': _L0_ffn_in['b2']}

def reference(x, ctx_1024, L0_attn_A, L0_attn_Bw, L0_attn_Bb, L0_attn_Cw, L0_attn_Cb, L0_attn_Dw, L0_attn_Db, L0_attn_W_ih, L0_attn_b_ih, L0_attn_W_hh, L0_attn_b_hh, L0_attn_proj_w, L0_attn_proj_b, L0_attn_gate_w, L0_attn_gate_b, L0_xattn_Wq, L0_xattn_Wk, L0_xattn_Wv, L0_ffn_gate_w, L0_ffn_gate_b, L0_ffn_w1, L0_ffn_b1, L0_ffn_w2, L0_ffn_b2):
    import jax
    import jax.numpy as jnp

    def _L0_attn_ref(x, A, Bw, Bb, Cw, Cb, Dw, Db, W_ih, b_ih, W_hh, b_hh, proj_w, proj_b, gate_w, gate_b):
        import jax, jax.numpy as jnp
        import numpy as np
        DIM, SSM, RNN = (256, 64, 128)
        B, N, D = x.shape
        R = W_hh.shape[1]
        bx = jnp.einsum('bnd,sd->bns', x, Bw) + Bb
        dx = jnp.einsum('bnd,ed->bne', x, Dw) + Db
        gx = jax.nn.sigmoid(jnp.einsum('bnd,gd->bng', x, gate_w) + gate_b)
        ih = jnp.einsum('bnd,rd->bnr', x, W_ih) + b_ih
        bx_t = jnp.swapaxes(bx, 0, 1)
        dx_t = jnp.swapaxes(dx, 0, 1)
        gx_t = jnp.swapaxes(gx, 0, 1)
        ih_t = jnp.swapaxes(ih, 0, 1)
        h_ssm0 = jnp.zeros((B, A.shape[0]), x.dtype)
        h_rnn0 = jnp.zeros((B, R), x.dtype)

        def step(carry, inp):
            h_ssm, h_rnn = carry
            bxt, dxt, gxt, iht = inp
            h_ssm = jax.nn.silu(h_ssm @ A.T + bxt)
            y_ssm = h_ssm @ Cw.T + Cb + dxt
            hh = h_rnn @ W_hh.T + b_hh
            i_r, i_z, i_n = jnp.split(iht, 3, axis=-1)
            h_r, h_z, h_n = jnp.split(hh, 3, axis=-1)
            r = jax.nn.sigmoid(i_r + h_r)
            z = jax.nn.sigmoid(i_z + h_z)
            n = jnp.tanh(i_n + r * h_n)
            h_rnn = (1.0 - z) * n + z * h_rnn
            y_rnn = h_rnn @ proj_w.T + proj_b
            fused = gxt[:, :1] * y_ssm + gxt[:, 1:2] * y_rnn
            return ((h_ssm, h_rnn), fused)
        _, out = jax.lax.scan(step, (h_ssm0, h_rnn0), (bx_t, dx_t, gx_t, ih_t))
        return jnp.swapaxes(out, 0, 1)

    def _L0_xattn_ref(query, key, value, Wq, Wk, Wv):
        import jax, jax.numpy as jnp
        import numpy as np
        THETA = 10000.0
        SCALE_BASE = 512.0
        GAMMA = 0.96875

        def _dup_interleave(x):
            return jnp.repeat(x, 2, axis=-1)

        def _xpos(x, offset, inverse_scale):
            L, d = (x.shape[-2], x.shape[-1])
            half = d // 2
            base = (jnp.arange(0, d, 2, dtype=x.dtype) + 0.4 * d) / (1.4 * d)
            pos = jnp.arange(offset, offset + L, dtype=x.dtype)
            scale = base[None, :] ** (pos[:, None] / SCALE_BASE)
            freqs = 1.0 / THETA ** (jnp.arange(half, dtype=x.dtype) / half)
            sin_in = pos[:, None] * freqs[None, :]
            if inverse_scale:
                scale = 1.0 / scale
            sin = _dup_interleave(jnp.sin(sin_in) * scale)
            cos = _dup_interleave(jnp.cos(sin_in) * scale)
            rot = jnp.stack((-x[..., 1::2], x[..., ::2]), axis=-1).reshape(x.shape)
            return x * cos + rot * sin

        def _decay_mask(L, gamma, dtype):
            u = jnp.arange(L, dtype=dtype)[:, None]
            v = jnp.arange(L, dtype=dtype)[None, :]
            return jnp.where(u >= v, gamma ** (u - v), jnp.zeros((), dtype))
        q = jnp.einsum('ble,de->bld', query, Wq)
        k = jnp.einsum('ble,de->bld', key, Wk)
        v = jnp.einsum('ble,de->bld', value, Wv)
        q = _xpos(q, 0, False)
        k = _xpos(k, 0, True)
        L = q.shape[-2]
        mask = _decay_mask(L, jnp.asarray(GAMMA, q.dtype), q.dtype)
        retention = jnp.einsum('bqd,bkd->bqk', q, k) * mask[None, :, :]
        out = jnp.einsum('bqk,bkv->bqv', retention, v)
        return out

    def _L0_ffn_ref(x, gate_w, gate_b, w1, b1, w2, b2):
        import jax, jax.numpy as jnp
        import numpy as np
        D_MODEL = 256
        FF = 1024
        E = 8
        TOP_K = 2
        CAP_FACTOR = 1.25
        B, T = (4, 512)

        def _moe_forward(x, gate_w, gate_b, w1, b1, w2, b2):
            Bb, Tt, d = x.shape
            S = Bb * Tt
            C = int(CAP_FACTOR * S / E)
            xf = x.reshape(S, d)
            logits = xf @ gate_w + gate_b
            probs = jax.nn.softmax(logits, axis=1)
            topk_p, topk_i = jax.lax.top_k(probs, TOP_K)
            topk_pn = topk_p / jnp.sum(topk_p, axis=1, keepdims=True)
            rows = jnp.arange(S)
            w_te = jnp.zeros((S, E), xf.dtype).at[rows[:, None], topk_i].set(topk_pn)
            mask = jnp.zeros((S, E), bool).at[rows[:, None], topk_i].set(True)
            rank = jnp.cumsum(mask.astype(jnp.int32), axis=0)
            slot = jnp.where(mask & (rank <= C), rank - 1, C)
            e_grid = jnp.broadcast_to(jnp.arange(E), (S, E))
            t_grid = jnp.broadcast_to(rows[:, None], (S, E))
            buf = jnp.full((E, C + 1), S, jnp.int32).at[e_grid, slot].set(t_grid)
            idx = buf[:, :C]
            valid = idx < S
            x_pad = jnp.concatenate([xf, jnp.zeros((1, d), xf.dtype)], axis=0)
            xin = x_pad[idx]
            h = jax.nn.relu(jnp.einsum('ecd,edh->ech', xin, w1) + b1[:, None, :])
            out = jnp.einsum('ech,ehd->ecd', h, w2) + b2[:, None, :]
            w_pad = jnp.concatenate([w_te, jnp.zeros((1, E), xf.dtype)], axis=0)
            tok_w = w_pad[idx, jnp.arange(E)[:, None]]
            out = out * jnp.where(valid, tok_w, 0.0)[:, :, None]
            final = jnp.zeros((S + 1, d), xf.dtype).at[idx.reshape(-1)].add(out.reshape(-1, d))[:S]
            return final.reshape(Bb, Tt, d)
        return _moe_forward(x, gate_w, gate_b, w1, b1, w2, b2)
    x = _layernorm(x + _L0_attn_ref(x, L0_attn_A, L0_attn_Bw, L0_attn_Bb, L0_attn_Cw, L0_attn_Cb, L0_attn_Dw, L0_attn_Db, L0_attn_W_ih, L0_attn_b_ih, L0_attn_W_hh, L0_attn_b_hh, L0_attn_proj_w, L0_attn_proj_b, L0_attn_gate_w, L0_attn_gate_b), axis=-1)
    x = _layernorm(x + _L0_xattn_ref(x, ctx_1024, ctx_1024, L0_xattn_Wq, L0_xattn_Wk, L0_xattn_Wv), axis=-1)
    x = _layernorm(x + _L0_ffn_ref(x, L0_ffn_gate_w, L0_ffn_gate_b, L0_ffn_w1, L0_ffn_b1, L0_ffn_w2, L0_ffn_b2), axis=-1)
    return x

_drawn_inputs = setup_inputs


def setup_inputs(seed=0):
    import zlib

    import numpy as np

    out = dict(_drawn_inputs(seed))
    spreads = {'L0_attn_Bb': (0.0, 0.716),
     'L0_attn_Cb': (0.0, 0.1),
     'L0_attn_Db': (0.0, 0.1),
     'L0_attn_b_ih': (0.0, 0.406),
     'L0_attn_b_hh': (0.0, 0.757),
     'L0_attn_proj_b': (0.0, 0.1),
     'L0_attn_gate_b': (0.0, 0.739),
     'L0_ffn_gate_b': (0.0, 0.1),
     'L0_ffn_b1': (0.0, 0.321),
     'L0_ffn_b2': (0.0, 0.1)}
    factors = {'L0_attn_A': 8.0, 'L0_attn_Bw': 2.976, 'L0_attn_Cw': 2.896, 'L0_attn_W_hh': 8.0}
    for name, (base, spread) in spreads.items():
        noise = np.random.default_rng([zlib.crc32(name.encode()), seed]).standard_normal(out[name].shape)
        drawn = base * np.exp(spread * noise) if base else spread * noise
        out[name] = jnp.asarray(drawn.astype(out[name].dtype))
    for name, factor in factors.items():
        out[name] = (out[name] * factor).astype(out[name].dtype)
    return out
```

```python
from contextlib import ExitStack

import concourse.bass as bass
from concourse import mybir

F32 = mybir.dt.float32
U32 = mybir.dt.uint32
ALU = mybir.AluOpType
ACT = mybir.ActivationFunctionType
AX = mybir.AxisListType

B, N, D = 16, 128, 256
SSM, RNN = 64, 128
FF, E = 1024, 8
S = B * N
CAP = int(1.25 * S / E)
SLOTS = E * CAP
P = 128
ST = P // B
TILES = S // P
CH = 2 * ST
CHUNKS = N // CH
HD = D // P
FK = FF // P
EPS = 1e-5
NRM_STEPS = TILES

CC = {}
_at = 0
for _name, _w in (("ident", P), ("cosq", N), ("sinq", N), ("cosk", N), ("sink", N), ("mask", N),
                  ("le", P), ("diag", P), ("lt", P), ("slot0", E * TILES), ("keep", E * TILES),
                  ("iota", E), ("bsel", 512)):
    CC[_name] = (_at, _at + _w)
    _at += _w
CW = _at


def mk_decoder_kernel(nc, xtok, xT, ctxT, consts, AT, BwT, Bb, CwE, DwT, W_ihT, b_gates, W_hhT, projT,
                      proj_b, gateT, gate_b, WqT, WkT, WvT, rgwT, rgb, w1, b1, w2, b2, out):
    xin = nc.dram_tensor("xin", (SLOTS, D), F32, kind="Internal").ap()
    yout = nc.dram_tensor("yout", (SLOTS + 1, D), F32, kind="Internal").ap()

    with ExitStack() as ctx:
        def sb(name, shape, dt=F32):
            return ctx.enter_context(nc.sbuf_tensor(name, shape, dt))

        def sem(name):
            return ctx.enter_context(nc.semaphore(name))

        cst = sb("cst", [P, CW])

        def con(name):
            return cst[:, CC[name][0]:CC[name][1]]

        ident = con("ident")
        whh = sb("whh", [RNN, 3 * RNN])
        wih = sb("wih", [P, HD, 3 * RNN])
        at_w = sb("at_w", [SSM, SSM])
        bw = sb("bw", [P, HD, SSM])
        bb = sb("bb", [SSM, 1])
        cwe = sb("cwe", [SSM + 2, D])
        dw = sb("dw", [P, HD, D])
        pw = sb("pw", [RNN, D])
        pb = sb("pb", [1, D])
        bg = sb("bg", [6, RNN])
        gw = sb("gw", [P, HD, 2])
        gb = sb("gb", [P, 2])
        wq = sb("wq", [P, HD, D])
        wk = sb("wk", [P, HD, D])
        wv = sb("wv", [P, HD, D])
        rgw = sb("rgw", [P, HD, E])
        rgc = sb("rgc", [P, HD, E])
        rgbt = sb("rgbt", [P, E])
        b1t = sb("b1t", [P, E * FK])
        b2t = sb("b2t", [P, E * HD])
        ones = sb("ones", [P, P])
        mhalf = sb("mhalf", [P, 2])
        epst = sb("epst", [P, 2])
        xin_t = [sb(f"xin_t{j}", [P, HD, P]) for j in range(2)]
        xfin_t = [sb(f"xfin_t{j}", [P, HD, P]) for j in range(2)]
        xres = [sb(f"xres{j}", [P, D]) for j in range(2)]
        hist = [sb(f"hist{j}", [RNN, ST * 2 * B]) for j in range(2)]
        hsb = [sb(f"hsb{j}", [SSM + 2, P]) for j in range(2)]
        rzb = sb("rzb", [RNN, 4 * B])
        nb = sb("nb", [RNN, 2 * B])
        ub = sb("ub", [RNN, 2 * B])
        mb = sb("mb", [RNN, 2 * B])
        sgb = sb("sgb", [SSM, B])
        ctxb = sb("ctxb", [P, HD, S])
        kT = sb("kT", [P, HD, S])
        vt = sb("vt", [P, B, D])
        ktm = sb("ktm", [P, 4, 512])
        gxs = sb("gxs", [P, 2])
        s1a = sb("s1a", [P, D])
        s1b = sb("s1b", [P, D])
        st1 = sb("st1", [P, 6])
        mv1 = sb("mv1", [P, 2])
        ve1 = sb("ve1", [P, 1])
        rs1 = sb("rs1", [P, 1])
        x1 = [sb(f"x1_{j}", [P, D]) for j in range(2)]
        x1T = sb("x1T", [P, HD, 2 * P])
        tm = sb("tm", [P, 4, 2 * P])
        qr = sb("qr", [P, HD, 2 * P])
        ret = sb("ret", [P, B, CH])
        sT = sb("sT", [P, HD, 2 * P])
        st2 = sb("st2", [P, 2, 6])
        mv2 = sb("mv2", [P, 2, 2])
        ve2 = sb("ve2", [P, 2])
        rs2 = sb("rs2", [P, 2])
        x2 = sb("x2", [P, TILES, D])
        lg = sb("lg", [P, TILES, E])
        mx = sb("mx", [P, TILES])
        pe_ = sb("pe_", [P, TILES, E])
        top = sb("top", [P, TILES, 8])
        topi = sb("topi", [P, TILES, 8], U32)
        topf = sb("topf", [P, TILES, 2])
        oh = [sb(f"oh{j}", [P, E, TILES]) for j in range(2)]
        msk = sb("msk", [P, E, TILES])
        cum = sb("cum", [P, E, TILES])
        pre = sb("pre", [P, E, TILES])
        suf = sb("suf", [P, E, TILES])
        rk = sb("rk", [P, E, TILES])
        ov = sb("ov", [P, E, TILES])
        slf = sb("slf", [P, 2, TILES])
        slu = sb("slu", [P, 2, TILES], U32)
        wt = sb("wt", [P, 2, TILES])
        wsum = sb("wsum", [P, TILES])
        w1t = [sb(f"w1t{j}", [P, HD, FF]) for j in range(2)]
        w2t = [sb(f"w2t{j}", [P, FK, D]) for j in range(2)]
        xe = [sb(f"xe{j}", [P, 3, D]) for j in range(2)]
        xeT = [sb(f"xeT{j}", [P, HD, CAP]) for j in range(2)]
        hT = sb("hT", [P, FK, CAP])
        yT = sb("yT", [P, HD, CAP])
        yt = [sb(f"yt{j}", [P, 3, D]) for j in range(2)]
        RG = 4
        yg = [[sb(f"yg{r}_{j}", [P, D]) for j in range(2)] for r in range(RG)]
        c1 = sb("c1", [P, D])
        c2 = sb("c2", [P, D])
        st3 = sb("st3", [P, 6])
        mv3 = [sb(f"mv3_{r}", [P, 2]) for r in range(2)]
        ve3 = sb("ve3", [P, 1])
        rs3 = [sb(f"rs3_{r}", [P, 1]) for r in range(2)]
        ot = [sb(f"ot{r}", [P, D]) for r in range(RG)]

        bank = [ctx.enter_context(nc.psum_tensor(f"bank{i}", [P, 512], F32)) for i in range(8)]
        RZ = bank[0:2]
        NS = bank[2:4]
        FB = bank[4]
        QB = bank[5]
        TB = bank[6]
        SC = bank[7]
        NW = 2 * ST * B

        names = ("w_load k_load a_load c_load z_load e_load ctx_load0 ctx_load1 ctx_load2 ctx_load3 xin0 xin1 xfin0 xfin1 xres0 xres1 "
                 "init_v init_p kv_mm k_mul k_rot kv_copy gsum gcent "
                 "in_done rz_ready ns_ready r_ready sg_ready npre_ready n_ready zh_ready h_done hs_done "
                 "fin_ready gx_ready fuse_a fuse_b stat1 var1 eps1 rstd1 x1_ready x1tr_ready x1T_ready "
                 "q_ready qmul_ready qr_ready sc_ready ret_ready pv_ready res_ready back_ready "
                 "stat2 var2 eps2 rstd2 x2_ready rt ract rmm "
                 "scat xe0 xe1 w1l0 w1l1 w2l0 w2l1 xtr_ready xeT_ready h_mm h_even h_odd y_mm yT_ready ytr_ready yt_ready yst0 yst1 zrow "
                 "ga0 ga1 ga2 ga3 c_a c_b stat3 var3 eps3 rstd3 o_ready ost0 ost1 ost2 ost3 g_done")
        q = {n: sem(n) for n in names.split()}

        def ev(ap):
            return ap.rearrange("p (c two) -> p c two", two=2)[:, :, 0]

        def od(ap):
            return ap.rearrange("p (c two) -> p c two", two=2)[:, :, 1]

        def h_of(j, s):
            return od(hist[j][:, s * 2 * B:(s + 1) * 2 * B])

        def prev(j, s):
            return (j, s - 1) if s else (1 - j, ST - 1)

        xT_d = xT.rearrange("(h p) c -> p h c", p=P)
        ctxT_d = ctxT.rearrange("(h p) c -> p h c", p=P)
        w1_d = w1.rearrange("e (h p) f -> p e h f", p=P)
        w2_d = w2.rearrange("e (k p) d -> p e k d", p=P)
        n_w = 17

        block = ctx.enter_context(nc.Block())

        @block.sync
        def _(sp):
            def load_in(k, j, first=False):
                if not first:
                    sp.wait_ge(q["in_done"], k - 1)
                sp.dma_start(xin_t[j][:], xT_d[:, :, bass.ts(k, P)]).then_inc(q[f"xin{j}"], 16)

            def load_fin(k, j, first=False):
                if not first:
                    sp.wait_ge(q["fuse_b"], k - 1)
                sp.dma_start(xfin_t[j][:], xT_d[:, :, bass.ts(k, P)]).then_inc(q[f"xfin{j}"], 16)
                sp.dma_start(xres[j][:], xtok[bass.ts(k, P), :]).then_inc(q[f"xres{j}"], 16)

            load_in(0, 0, True)
            sp.dma_start(wih[:], W_ihT.rearrange("(h p) r -> p h r", p=P)).then_inc(q["w_load"], 16)
            sp.dma_start(bg[:], b_gates).then_inc(q["w_load"], 16)
            sp.dma_start(whh[:], W_hhT).then_inc(q["w_load"], 16)
            sp.dma_start(at_w[:], AT).then_inc(q["w_load"], 16)
            sp.dma_start(bw[:], BwT.rearrange("(h p) r -> p h r", p=P)).then_inc(q["w_load"], 16)
            sp.dma_start(bb[:], Bb).then_inc(q["w_load"], 16)
            load_in(1, 1, True)
            sp.dma_start(dw[:], DwT.rearrange("(h p) r -> p h r", p=P)).then_inc(q["w_load"], 16)
            sp.dma_start(pw[:], projT).then_inc(q["w_load"], 16)
            sp.dma_start(pb[:], proj_b).then_inc(q["w_load"], 16)
            sp.dma_start(cwe[:], CwE).then_inc(q["w_load"], 16)
            sp.dma_start(gw[:], gateT.rearrange("(h p) r -> p h r", p=P)).then_inc(q["w_load"], 16)
            sp.dma_start(gb[:], gate_b.to_broadcast([P, 2])).then_inc(q["w_load"], 16)
            sp.dma_start(wq[:], WqT.rearrange("(h p) r -> p h r", p=P)).then_inc(q["w_load"], 16)
            load_fin(0, 0, True)
            load_fin(1, 1, True)
            sp.dma_start(rgw[:], rgwT.rearrange("(h p) r -> p h r", p=P)).then_inc(q["w_load"], 16)
            sp.dma_start(rgbt[:], rgb.to_broadcast([P, E])).then_inc(q["w_load"], 16)
            sp.dma_start(b1t[:], b1).then_inc(q["w_load"], 16)
            sp.dma_start(b2t[:], b2).then_inc(q["w_load"], 16)
            for e in range(2):
                sp.dma_start(w1t[e][:], w1_d[:, e]).then_inc(q[f"w1l{e}"], 16)
                sp.dma_start(w2t[e][:], w2_d[:, e]).then_inc(q[f"w2l{e}"], 16)
            with sp.Fori(0, CHUNKS - 1) as g:
                load_in(2 * g + 2, 0)
                load_fin(2 * g + 2, 0)
                load_in(2 * g + 3, 1)
                load_fin(2 * g + 3, 1)
            sp.wait_ge(q["scat"], 16 * 2 * TILES)

            def load_xe(e, j):
                sp.dma_start(xe[j][:, 0:2, :], xin[bass.ds(e * CAP, 2 * P), :].rearrange("(c p) d -> p c d", p=P)).then_inc(q[f"xe{j}"], 16)
                sp.dma_start(xe[j][0:CAP - 2 * P, 2, :], xin[bass.ds(e * CAP + 2 * P, CAP - 2 * P), :]).then_inc(q[f"xe{j}"], 16)

            def store_y(e, j):
                sp.wait_ge(q["yt_ready"], e + 1)
                sp.dma_start(yout[bass.ds(e * CAP, 2 * P), :].rearrange("(c p) d -> p c d", p=P), yt[j][:, 0:2, :]).then_inc(q[f"yst{j}"], 16)
                sp.dma_start(yout[bass.ds(e * CAP + 2 * P, CAP - 2 * P), :], yt[j][0:CAP - 2 * P, 2, :]).then_inc(q[f"yst{j}"], 16)

            load_xe(0, 0)
            load_xe(1, 1)
            with sp.Fori(0, E // 2 - 1) as i:
                for j in range(2):
                    e = 2 * i + j
                    sp.wait_ge(q["xtr_ready"], e + 1)
                    load_xe(e + 2, j)
                    sp.wait_ge(q["h_mm"], FK * (e + 1))
                    sp.dma_start(w1t[j][:], w1_d[:, e + 2]).then_inc(q[f"w1l{j}"], 16)
                    sp.wait_ge(q["y_mm"], e + 1)
                    sp.dma_start(w2t[j][:], w2_d[:, e + 2]).then_inc(q[f"w2l{j}"], 16)
                    store_y(e, j)
            store_y(E - 2, 0)
            store_y(E - 1, 1)
            with sp.Fori(0, TILES // RG) as i:
                for r in range(RG):
                    sp.wait_ge(q["o_ready"], RG * i + (r + 1))
                    sp.dma_start(out[bass.ts(RG * i + r, P), :], ot[r][:]).then_inc(q[f"ost{r}"], 16)
            for r in range(RG):
                sp.wait_ge(q[f"ost{r}"], 16 * (TILES // RG))

        @block.gpsimd
        def _(pool):
            def rot_k(i):
                pool.wait_ge(q["k_mul"], 4 * (i + 1))
                pool.tensor_tensor(kT[:, 0, bass.ts(i, 512)], ktm[:, 0, :], ktm[:, 1, :], ALU.subtract).then_inc(q["k_rot"], 1)
                pool.tensor_tensor(kT[:, 1, bass.ts(i, 512)], ktm[:, 2, :], ktm[:, 3, :], ALU.add).then_inc(q["k_rot"], 1)

            def rstd(var, eps, out_, ready, done, scratch, n):
                pool.wait_ge(var, n)
                pool.tensor_tensor(scratch[0], scratch[1], epst[:, 0:scratch[0].shape[-1]], ALU.add).then_inc(eps, 1)
                pool.wait_ge(eps, n)
                pool.tensor_tensor(out_, scratch[0], mhalf[:, 0:scratch[0].shape[-1]], ALU.pow).then_inc(done, 1)

            def rstd_1(n):
                rstd(q["var1"], q["eps1"], rs1[:], None, q["rstd1"], (ve1[:], mv1[:, 1:2]), n + 1)

            def rot_q(c):
                pool.wait_ge(q["qmul_ready"], c + 1)
                pool.tensor_tensor(qr[:, 0, :], tm[:, 0, :], tm[:, 1, :], ALU.subtract).then_inc(q["qr_ready"], 1)
                pool.tensor_tensor(qr[:, 1, :], tm[:, 2, :], tm[:, 3, :], ALU.add).then_inc(q["qr_ready"], 1)

            def rstd_2(c):
                rstd(q["var2"], q["eps2"], rs2[:], None, q["rstd2"], (ve2[:], mv2[:, :, 1]), c + 1)

            def iteration(g, has_prev):
                if has_prev:
                    rstd_1(2 * g - 1)
                    rot_q(g - 1)
                rstd_1(2 * g)
                if has_prev:
                    rstd_2(g - 1)

            pool.memset(ones[:], 1.0).then_inc(q["init_p"], 1)
            pool.memset(mhalf[:], -0.5).then_inc(q["init_p"], 1)
            pool.memset(epst[:], EPS).then_inc(q["init_p"], 1)
            pool.wait_ge(q["init_v"], INIT_V)
            pool.wait_ge(q["init_p"], INIT_P)
            for i in range(SLOTS // P):
                pool.dma_start(xin[i * P:(i + 1) * P, :], c1[:]).then_inc(q["zrow"], 16)
            pool.dma_start(yout[SLOTS:SLOTS + 1, :], c1[0:1, :]).then_inc(q["zrow"], 16)
            for i in range(4):
                rot_k(i)
            iteration(0, False)
            with pool.Fori(1, CHUNKS) as g:
                iteration(g, True)
            rstd_1(TILES - 1)
            rot_q(CHUNKS - 1)
            rstd_2(CHUNKS - 1)
            pool.wait_ge(q["zrow"], 16 * (SLOTS // P + 1))
            pool.wait_ge(q["rt"], RT_SLOT)
            for k in range(TILES):
                for j in range(2):
                    pool.indirect_dma_start(
                        xin[:, :], bass.IndirectOffsetOnAxis(ap=slu[:, j, k:k + 1], axis=0), x2[:, k, :], None,
                        bounds_check=SLOTS - 1, oob_is_err=False).then_inc(q["scat"], 16)
            for j in range(2):
                pool.wait_ge(q[f"yst{j}"], 32 * (E // 2))

            def gather(k):
                if k >= RG:
                    pool.wait_ge(q["c_b"], k - RG + 1)
                for j in range(2):
                    pool.indirect_dma_start(
                        yg[k % RG][j][:], None, yout[:, :], bass.IndirectOffsetOnAxis(ap=slu[:, j, k:k + 1], axis=0),
                        bounds_check=SLOTS, oob_is_err=False).then_inc(q[f"ga{k % RG}"], 16)

            def rstd_3(k):
                rstd(q["var3"], q["eps3"], rs3[k % 2][:], None, q["rstd3"], (ve3[:], mv3[k % 2][:, 1:2]), k + 1)

            gather(0)
            gather(1)
            gather(2)
            gather(3)
            for k in range(TILES):
                rstd_3(k)
                if k + RG < TILES:
                    gather(k + RG)

        @block.scalar
        def _(act):
            def rec(g, j, s):
                t = CH * g + ST * j + s
                act.wait_ge(q["rz_ready"], t + 1)
                nc.scalar.activation(od(rzb[:]), RZ[j][:, s * 2 * B:(s + 1) * 2 * B], ACT.Sigmoid).then_inc(q["r_ready"], 1)
                act.wait_ge(q["npre_ready"], t + 1)
                nc.scalar.activation(od(nb[:]), od(ub[:]), ACT.Tanh).then_inc(q["n_ready"], 1)
                nc.scalar.activation(sgb[:], NS[j][0:SSM, NW + s * B:NW + (s + 1) * B], ACT.Sigmoid, bias=bb[:]).then_inc(q["sg_ready"], 1)

            def gates(n):
                act.wait_ge(q["fin_ready"], n + 1)
                for i in range(2):
                    nc.scalar.activation(gxs[:, i:i + 1], TB[:, i:i + 1], ACT.Sigmoid, bias=gb[:, i:i + 1]).then_inc(q["gx_ready"], 1)

            def x1T_copy(c):
                act.wait_ge(q["x1tr_ready"], c + 1)
                for h in range(HD):
                    nc.scalar.copy(x1T[:, h, :], TB[:, h * 256:(h + 1) * 256]).then_inc(q["x1T_ready"], 1)

            def iteration(g, has_prev):
                for s in range(CH):
                    rec(g, s // ST, s % ST)
                    if has_prev and s == 1:
                        gates(2 * g - 1)
                    if has_prev and s == 4:
                        x1T_copy(g - 1)
                    if s == 9:
                        gates(2 * g)

            act.dma_start(cst[:], consts).then_inc(q["c_load"], 16)
            act.dma_start(wk[:], WkT.rearrange("(h p) r -> p h r", p=P)).then_inc(q["k_load"], 16)
            act.dma_start(wv[:], WvT.rearrange("(h p) r -> p h r", p=P)).then_inc(q["k_load"], 16)
            for i in range(4):
                act.dma_start(ctxb[:, :, bass.ts(i, 512)], ctxT_d[:, :, bass.ts(i, 512)]).then_inc(q[f"ctx_load{i}"], 16)
            act.wait_ge(q["w_load"], 16 * n_w)
            for b in range(B):
                act.wait_ge(q["kv_mm"], 4 + b + 1)
                nc.scalar.copy(vt[:, b, :], bank[4 + b % 4][:, 0:D]).then_inc(q["kv_copy"], 1)
            act.wait_ge(q["init_v"], INIT_V)
            iteration(0, False)
            with act.Fori(1, CHUNKS) as g:
                iteration(g, True)
            gates(TILES - 1)
            x1T_copy(CHUNKS - 1)
            act.wait_ge(q["rt"], 2)
            nc.scalar.activation(pe_[:], pe_[:], ACT.Exp).then_inc(q["ract"], 1)

            def expert(i, j):
                e = 2 * i + j
                act.wait_ge(q["xtr_ready"], e + 1)
                for h in range(HD):
                    nc.scalar.copy(xeT[j][:, h, :], bank[h][:, 0:CAP]).then_inc(q["xeT_ready"], 1)
                for f in range(0, FK, 2):
                    act.wait_ge(q["h_mm"], FK * e + f + 1)
                    nc.scalar.activation(hT[:, f, :], bank[2 + f % 4][:, 0:CAP], ACT.Relu,
                                         bias=b1t[:, bass.ds(e * FK + f, 1)]).then_inc(q["h_even"], 1)
                act.wait_ge(q["y_mm"], e + 1)
                for h in range(HD):
                    nc.scalar.activation(yT[:, h, :], bank[6 + h][:, 0:CAP], ACT.Identity,
                                         bias=b2t[:, bass.ds(e * HD + h, 1)]).then_inc(q["yT_ready"], 1)

            with act.Fori(0, E // 2) as i:
                for j in range(2):
                    expert(i, j)

        @block.tensor
        def _(pe):
            def mm(out_, lhsT, rhs, start=True, stop=True):
                return nc.tensor.matmul(out_, lhsT, rhs, start=start, stop=stop, skip_group_check=True)

            def project_in(n, j):
                pe.wait_ge(q[f"xin{j}"], 16 * ((n - j) // 2 + 1) if isinstance(n, int) else 8 * n + (16 - 8 * j))
                mm(RZ[j][:, 0:NW], bg[:], con("bsel")[0:6, 0:NW], True, False)
                mm(NS[j][:, 0:NW], bg[:], con("bsel")[0:6, NW:2 * NW], True, False)
                for h in range(HD):
                    for i in range(3):
                        if i < 2:
                            o = RZ[j][:, 0:NW].rearrange("p (s i b) -> p i s b", i=2, b=B)[:, i]
                        else:
                            o = NS[j][:, 0:NW].rearrange("p (s b two) -> p two s b", two=2, b=B)[:, 1]
                        mm(o, wih[:, h, i * RNN:(i + 1) * RNN], xin_t[j][:, h, :].rearrange("p (s b) -> p s b", b=B), False, False)
                for h in range(HD):
                    last = mm(NS[j][0:SSM, NW:NW + P], bw[:, h, :], xin_t[j][:, h, :], False, False)
                last.then_inc(q["in_done"], 1)

            def rec(g, j, s):
                t = CH * g + ST * j + s
                pj, ps = prev(j, s)
                h = h_of(pj, ps)
                pe.wait_ge(q["h_done"], t + 1)
                mm(RZ[j][:, s * 32:s * 32 + 16], whh[:, 0:RNN], h, False, False)
                mm(RZ[j][:, s * 32 + 16:s * 32 + 32], whh[:, RNN:2 * RNN], h, False, False).then_inc(q["rz_ready"], 1)
                pe.wait_ge(q["hs_done"], t + 1)
                mm(ev(NS[j][:, s * 32:s * 32 + 32]), whh[:, 2 * RNN:3 * RNN], h, False, False)
                mm(NS[j][0:SSM, NW + s * B:NW + (s + 1) * B], at_w[:], hsb[pj][0:SSM, ps * B:(ps + 1) * B], False, False).then_inc(q["ns_ready"], 1)

            def fin_a(n, j):
                pe.wait_ge(q[f"xfin{j}"], 16 * ((n - j) // 2 + 1) if isinstance(n, int) else 8 * n + (16 - 8 * j))
                if not isinstance(n, int) or n >= 1:
                    pe.wait_ge(q["fuse_b"], n)
                mm(FB[:, 0:D], hsb[j][:], cwe[:], True, False)
                for h in range(HD):
                    mm(FB[:, 0:D], xfin_t[j][:, h, :], dw[:, h, :], False, h == 1)

            def fin_b(n, j):
                if j == 1:
                    pe.wait_ge(q["x2_ready"], n)
                mm(FB[:, D:2 * D], h_hist(j), pw[:], False, False)
                mm(FB[:, D:2 * D], ones[0:1, :], pb[:], False, True)
                for h in range(HD):
                    last = mm(TB[:, 0:2], xfin_t[j][:, h, :], gw[:, h, :], h == 0, h == 1)
                last.then_inc(q["fin_ready"], 1)

            def h_hist(j):
                return od(hist[j][:])

            def x1_tr(c):
                pe.wait_ge(q["x1_ready"], 2 * c + 2)
                pe.wait_ge(q["x2_ready"], 2 * c + 1)
                for j in range(2):
                    for h in range(HD):
                        last = nc.tensor.transpose(TB[:, h * 256 + j * P:h * 256 + (j + 1) * P], x1[j][:, h * P:(h + 1) * P], ident)
                last.then_inc(q["x1tr_ready"], 1)

            def q_proj(c):
                pe.wait_ge(q["x1T_ready"], 2 * c + 2)
                for o in range(HD):
                    for h in range(HD):
                        last = mm(QB[:, o * 256:(o + 1) * 256], wq[:, h, o * P:(o + 1) * P], x1T[:, h, :], h == 0, h == 1)
                last.then_inc(q["q_ready"], 1)

            def scores(c, r, n):
                if r == 0:
                    pe.wait_ge(q["qr_ready"], 2 * c + 2)
                for b in range(r, r + n):
                    for h in range(HD):
                        last = mm(SC[:, b * CH:(b + 1) * CH], kT[:, h, b * N:(b + 1) * N],
                                  qr[:, h, :].rearrange("p (t b) -> p t b", b=B)[:, :, b], h == 0, h == 1)
                if r + n == B:
                    last.then_inc(q["sc_ready"], 1)

            def mix(c, r, n):
                if r == 0:
                    pe.wait_ge(q["ret_ready"], c + 1)
                for b in range(r, r + n):
                    for h in range(HD):
                        last = mm(QB[:, h * 256:(h + 1) * 256].rearrange("p (t b) -> p t b", b=B)[:, :, b],
                                  vt[:, b, h * P:(h + 1) * P], ret[:, b, :])
                if r + n == B:
                    last.then_inc(q["pv_ready"], 1)

            def back(c, back_gates):
                pe.wait_ge(q["res_ready"], 2 * c + 2)
                pe.wait_ge(q["gx_ready"], back_gates)
                for j in range(2):
                    for h in range(HD):
                        nc.tensor.transpose(TB[:, j * 256 + h * P:j * 256 + (h + 1) * P], sT[:, h, j * P:(j + 1) * P], ident)
                for j in range(2):
                    for h in range(HD):
                        last = mm(SC[:, 264 + j * 8:272 + j * 8], sT[:, h, j * P:(j + 1) * P], rgc[:, h, :], h == 0, h == 1)
                last.then_inc(q["back_ready"], 1)

            def iteration(g, has_prev, has_next):
                for s in range(CH):
                    rec(g, s // ST, s % ST)
                    if has_prev:
                        if s == 0:
                            fin_a(2 * g - 1, 1)
                        if s == 1:
                            fin_b(2 * g - 1, 1)
                    if s == 2:
                        project_in(2 * g + 1, 1)
                    if has_prev:
                        if s == 4:
                            x1_tr(g - 1)
                        if s == 5:
                            q_proj(g - 1)
                        if s in (7, 8, 9, 10):
                            scores(g - 1, 4 * (s - 7), 4)
                    if s == 8:
                        fin_a(2 * g, 0)
                    if s == 9:
                        fin_b(2 * g, 0)
                    if has_next and s == 11:
                        project_in(2 * g + 2, 0)
                    if has_prev:
                        if s in (12, 13, 14, 15):
                            mix(g - 1, 4 * (s - 12), 4)
                if has_prev:
                    back(g - 1, 4 * g + 2)

            pe.wait_ge(q["w_load"], 16 * n_w)
            pe.wait_ge(q["init_p"], INIT_P)
            pe.wait_ge(q["init_v"], INIT_V)
            for h in range(HD):
                last = mm(bank[2][:, 0:E], ones[:], rgw[:, h, :], h == 0, h == 1)
            last.then_inc(q["gsum"], 1)
            pe.wait_ge(q["k_load"], 32)
            pe.wait_ge(q["c_load"], 16)
            for i in range(4):
                pe.wait_ge(q[f"ctx_load{i}"], 16)
                if i >= 2:
                    pe.wait_ge(q["k_mul"], 4 * (i - 1))
                for o in range(HD):
                    for h in range(HD):
                        last = mm(bank[4 + 2 * (i % 2) + o][:], wk[:, h, o * P:(o + 1) * P], ctxb[:, h, bass.ts(i, 512)], h == 0, h == 1)
                last.then_inc(q["kv_mm"], 1)
            pe.wait_ge(q["k_mul"], 16)
            for b in range(B):
                if b >= 4:
                    pe.wait_ge(q["kv_copy"], b - 3)
                for h in range(HD):
                    last = mm(bank[4 + b % 4][:, 0:D], ctxb[:, h, b * N:(b + 1) * N], wv[:, h, :], h == 0, h == 1)
                last.then_inc(q["kv_mm"], 1)
            pe.wait_ge(q["kv_copy"], B)
            pe.wait_ge(q["gcent"], 1)
            project_in(0, 0)
            iteration(0, False, True)
            with pe.Fori(1, CHUNKS - 1) as g:
                iteration(g, True, True)
            iteration(CHUNKS - 1, True, False)
            c = CHUNKS - 1
            fin_a(TILES - 1, 1)
            fin_b(TILES - 1, 1)
            x1_tr(c)
            q_proj(c)
            scores(c, 0, 8)
            scores(c, 8, 8)
            mix(c, 0, 8)
            mix(c, 8, 8)
            back(c, 2 * TILES)
            pe.wait_ge(q["rt"], RT_CUM)
            flat = [x[:].rearrange("p e k -> p (e k)") for x in (pre, msk, suf)]
            for i, name in enumerate(("le", "diag", "lt")):
                last = mm(bank[0][:, 0:E * TILES], con(name), flat[i], i == 0, i == 2)
            last.then_inc(q["rmm"], 1)
            pe.wait_ge(q["rt"], RT_SLOT)

            def expert(i, j, first):
                e = 2 * i + j
                pe.wait_ge(q[f"xe{j}"], 32 * i + 32)
                if not first:
                    pe.wait_ge(q["xeT_ready"], 2 * e)
                for c3 in range(3):
                    m = min(P, CAP - c3 * P)
                    for h in range(HD):
                        last = nc.tensor.transpose(bank[h][:, c3 * P:c3 * P + m], xe[j][0:m, c3, h * P:(h + 1) * P], ident[0:m, 0:m])
                last.then_inc(q["xtr_ready"], 1)
                pe.wait_ge(q["xeT_ready"], 2 * e + 2)
                pe.wait_ge(q[f"w1l{j}"], 16 * i + 16)
                for f in range(FK):
                    if f >= 4:
                        pe.wait_ge(q["h_odd" if f % 2 else "h_even"], FK // 2 * e + (f - 4) // 2 + 1)
                    for h in range(HD):
                        last = mm(bank[2 + f % 4][:, 0:CAP], w1t[j][:, h, f * P:(f + 1) * P], xeT[j][:, h, :], h == 0, h == 1)
                    last.then_inc(q["h_mm"], 1)
                pe.wait_ge(q["h_even"], FK // 2 * (e + 1))
                pe.wait_ge(q["h_odd"], FK // 2 * (e + 1))
                pe.wait_ge(q[f"w2l{j}"], 16 * i + 16)
                if not first:
                    pe.wait_ge(q["yt_ready"], e)
                for h in range(HD):
                    for f in range(FK):
                        last = mm(bank[6 + h][:, 0:CAP], w2t[j][:, f, h * P:(h + 1) * P], hT[:, f, :], f == 0, f == FK - 1)
                last.then_inc(q["y_mm"], 1)
                pe.wait_ge(q["yT_ready"], 2 * e + 2)
                for c3 in range(3):
                    m = min(P, CAP - c3 * P)
                    for h in range(HD):
                        w = c3 * D + h * P
                        last = nc.tensor.transpose(bank[6 + w // 512][0:m, w % 512:w % 512 + P], yT[:, h, c3 * P:c3 * P + m], ident)
                last.then_inc(q["ytr_ready"], 1)

            expert(0, 0, True)
            expert(0, 1, False)
            with pe.Fori(1, E // 2) as i:
                for j in range(2):
                    expert(i, j, False)

        @block.vector
        def _(dve):
            def rec(g, j, s):
                t = CH * g + ST * j + s
                pj, ps = prev(j, s)
                dve.wait_ge(q["ns_ready"], t + 1)
                dve.wait_ge(q["r_ready"], t + 1)
                nc.vector.tensor_tensor_scan(ub[:], rzb[:, 0:2 * B], NS[j][:, s * 32:s * 32 + 32], 0.0,
                                             ALU.mult, ALU.add).then_inc(q["npre_ready"], 1)
                nc.vector.tensor_scalar(ev(mb[:]), od(rzb[:, 2 * B:4 * B]), -1.0, 1.0, ALU.mult, ALU.add).then_inc(q["zh_ready"], 1)
                nc.vector.tensor_tensor(od(mb[:]), od(rzb[:, 2 * B:4 * B]), h_of(pj, ps), ALU.mult).then_inc(q["zh_ready"], 1)
                dve.wait_ge(q["zh_ready"], 2 * t + 2)
                dve.wait_ge(q["n_ready"], t + 1)
                nc.vector.tensor_tensor_scan(hist[j][:, s * 32:(s + 1) * 32], nb[:], mb[:], 0.0, ALU.mult, ALU.add).then_inc(q["h_done"], 1)
                dve.wait_ge(q["sg_ready"], t + 1)
                nc.vector.scalar_tensor_tensor(hsb[j][0:SSM, s * B:(s + 1) * B], NS[j][0:SSM, NW + s * B:NW + (s + 1) * B], bb[:], sgb[:],
                                               ALU.add, ALU.mult).then_inc(q["hs_done"], 1)

            def fuse(n, j, part):
                if part == 0:
                    dve.wait_ge(q["gx_ready"], 2 * n + 2)
                    dve.wait_ge(q[f"xres{j}"], 16 * ((n - j) // 2 + 1) if isinstance(n, int) else 8 * n + (16 - 8 * j))
                    nc.vector.scalar_tensor_tensor(s1a[:], FB[:, 0:D], gxs[:, 0:1], xres[j][:], ALU.mult, ALU.add).then_inc(q["fuse_a"], 1)
                else:
                    dve.wait_ge(q["fuse_a"], n + 1)
                    nc.vector.scalar_tensor_tensor(s1b[:], FB[:, D:2 * D], gxs[:, 1:2], s1a[:], ALU.mult, ALU.add).then_inc(q["fuse_b"], 1)

            def stats_1(n):
                dve.wait_ge(q["fuse_b"], n + 1)
                nc.vector.bn_stats(st1[:], s1b[:]).then_inc(q["stat1"], 1)
                dve.wait_ge(q["init_v"], INIT_V)
                dve.wait_ge(q["stat1"], n + 1)
                nc.vector.bn_aggr(mv1[:], st1[:]).then_inc(q["var1"], 1)

            def norm_1(n, j):
                dve.wait_ge(q["rstd1"], n + 1)
                nc.vector.tensor_scalar(x1[j][:], s1b[:], mv1[:, 0:1], rs1[:], ALU.subtract, ALU.mult).then_inc(q["x1_ready"], 1)

            def rotate(c):
                dve.wait_ge(q["q_ready"], c + 1)
                col = bass.ts(c, CH)
                cs = con("cosq")[:, col].unsqueeze(2).to_broadcast([P, CH, B])
                sn = con("sinq")[:, col].unsqueeze(2).to_broadcast([P, CH, B])
                for i, (half, tab) in enumerate(((0, cs), (1, sn), (1, cs), (0, sn))):
                    last = nc.vector.tensor_tensor(tm[:, i, :].rearrange("p (t b) -> p t b", b=B),
                                                   QB[:, half * 256:(half + 1) * 256].rearrange("p (t b) -> p t b", b=B), tab, ALU.mult)
                last.then_inc(q["qmul_ready"], 1)

            def decay(c):
                dve.wait_ge(q["sc_ready"], c + 1)
                m = con("mask")[:, bass.ts(c, CH)].unsqueeze(1).to_broadcast([P, B, CH])
                nc.vector.tensor_tensor(ret[:], SC[:, 0:B * CH].rearrange("p (b t) -> p b t", t=CH), m,
                                        ALU.mult).then_inc(q["ret_ready"], 1)

            def residual(c):
                dve.wait_ge(q["pv_ready"], c + 1)
                for h in range(HD):
                    nc.vector.tensor_tensor(sT[:, h, :], QB[:, h * 256:(h + 1) * 256], x1T[:, h, :], ALU.add).then_inc(q["res_ready"], 1)

            def stats_2(c):
                dve.wait_ge(q["back_ready"], c + 1)
                for j in range(2):
                    last = nc.vector.bn_stats(st2[:, j, :], TB[:, j * 256:(j + 1) * 256])
                last.then_inc(q["stat2"], 1)
                dve.wait_ge(q["init_v"], INIT_V)
                dve.wait_ge(q["stat2"], c + 1)
                for j in range(2):
                    last = nc.vector.bn_aggr(mv2[:, j, :], st2[:, j, :])
                last.then_inc(q["var2"], 1)

            def norm_2(c):
                dve.wait_ge(q["rstd2"], c + 1)
                for j in range(2):
                    nc.vector.scalar_tensor_tensor(lg[:, bass.ds(2 * c + j, 1), :].rearrange("p o e -> p (o e)"), SC[:, 264 + j * 8:272 + j * 8], rs2[:, j:j + 1],
                                                   rgbt[:], ALU.mult, ALU.add)
                    nc.vector.tensor_scalar(x2[:, bass.ds(2 * c + j, 1), :].rearrange("p o d -> p (o d)"), TB[:, j * 256:(j + 1) * 256], mv2[:, j, 0:1],
                                            rs2[:, j:j + 1], ALU.subtract, ALU.mult).then_inc(q["x2_ready"], 1)

            def iteration(g, has_prev):
                for s in range(CH):
                    rec(g, s // ST, s % ST)
                    if has_prev:
                        if s == 1:
                            fuse(2 * g - 1, 1, 0)
                        if s == 2:
                            fuse(2 * g - 1, 1, 1)
                            stats_1(2 * g - 1)
                        if s == 3:
                            norm_1(2 * g - 1, 1)
                        if s == 6:
                            rotate(g - 1)
                    if s == 9:
                        fuse(2 * g, 0, 0)
                    if s == 10:
                        fuse(2 * g, 0, 1)
                        stats_1(2 * g)
                    if s == 11:
                        norm_1(2 * g, 0)
                    if has_prev:
                        if s == 11:
                            decay(g - 1)
                if has_prev:
                    residual(g - 1)
                    stats_2(g - 1)
                    norm_2(g - 1)

            nc.vector.memset(rzb[:], 0.0).then_inc(q["init_v"], 1)
            nc.vector.memset(nb[:], 0.0).then_inc(q["init_v"], 1)
            nc.vector.memset(hist[1][:], 0.0).then_inc(q["init_v"], 1)
            nc.vector.memset(hsb[1][0:SSM, :], 0.0).then_inc(q["init_v"], 1)
            for j in range(2):
                nc.vector.memset(hsb[j][SSM:SSM + 2, :], 1.0).then_inc(q["init_v"], 1)
            nc.vector.memset(c1[:], 0.0).then_inc(q["init_v"], 1)
            dve.wait_ge(q["gsum"], 1)
            for h in range(HD):
                last = nc.vector.scalar_tensor_tensor(rgc[:, h, :], bank[2][:, 0:E], -1.0 / D, rgw[:, h, :], ALU.mult, ALU.add)
            last.then_inc(q["gcent"], 1)
            dve.wait_ge(q["c_load"], 16)
            for i in range(4):
                dve.wait_ge(q["kv_mm"], i + 1)
                if i >= 1:
                    dve.wait_ge(q["k_rot"], 2 * i)
                cs = con("cosk").unsqueeze(1).to_broadcast([P, 4, N])
                sn = con("sink").unsqueeze(1).to_broadcast([P, 4, N])
                for n, (half, tab) in enumerate(((0, cs), (1, sn), (1, cs), (0, sn))):
                    nc.vector.tensor_tensor(ktm[:, n, :].rearrange("p (b t) -> p b t", t=N),
                                            bank[4 + 2 * (i % 2) + half][:].rearrange("p (b t) -> p b t", t=N), tab,
                                            ALU.mult).then_inc(q["k_mul"], 1)
            dve.wait_ge(q["k_rot"], 8)
            dve.wait_ge(q["init_v"], INIT_V)
            dve.wait_ge(q["init_p"], INIT_P)
            nc.vector.memset(mb[:], 0.0).then_inc(q["h_done"], 1)
            nc.vector.memset(sgb[:], 0.0).then_inc(q["hs_done"], 1)
            nc.vector.memset(st2[:], 0.0).then_inc(q["x2_ready"], 1)
            iteration(0, False)
            with dve.Fori(1, CHUNKS) as g:
                iteration(g, True)
            n, c = TILES - 1, CHUNKS - 1
            fuse(n, 1, 0)
            fuse(n, 1, 1)
            stats_1(n)
            norm_1(n, 1)
            rotate(c)
            decay(c)
            residual(c)
            stats_2(c)
            norm_2(c)

            step = [0]

            def then(ins):
                step[0] += 1
                ins.then_inc(q["rt"], 1)
                dve.wait_ge(q["rt"], step[0])

            def bk(ap):
                return ap.unsqueeze(2).to_broadcast([P, TILES, E])

            dve.wait_ge(q["x2_ready"], TILES + 1)
            then(nc.vector.tensor_reduce(mx[:], lg[:], AX.X, ALU.max))
            then(nc.vector.tensor_tensor(pe_[:], lg[:], bk(mx[:]), ALU.subtract))
            dve.wait_ge(q["ract"], 1)
            then(nc.vector.tensor_reduce(mx[:], pe_[:], AX.X, ALU.add))
            then(nc.vector.reciprocal(mx[:], mx[:]))
            then(nc.vector.tensor_tensor(pe_[:], pe_[:], bk(mx[:]), ALU.mult))
            for k in range(TILES):
                last = nc.vector.max(top[:, k, :], pe_[:, k, :])
            then(last)
            for k in range(TILES):
                last = nc.vector.max_index(topi[:, k, :], top[:, k, :], pe_[:, k, :])
            then(last)
            then(nc.vector.tensor_copy(topf[:], topi[:, :, 0:2]))
            for j in range(2):
                last = nc.vector.tensor_tensor(oh[j][:], topf[:, :, j].unsqueeze(1).to_broadcast([P, E, TILES]),
                                               con("iota").unsqueeze(2).to_broadcast([P, E, TILES]), ALU.is_equal)
            then(last)
            then(nc.vector.tensor_tensor(msk[:], oh[0][:], oh[1][:], ALU.add))
            then(nc.vector.tensor_tensor_scan(cum[:].rearrange("p e k -> p (e k)"), con("keep"), msk[:].rearrange("p e k -> p (e k)"),
                                              0.0, ALU.mult, ALU.add))
            nc.vector.tensor_tensor(pre[:], cum[:], msk[:], ALU.subtract)
            then(nc.vector.tensor_tensor(suf[:], cum[:, :, TILES - 1:TILES].to_broadcast([P, E, TILES]), cum[:], ALU.subtract))
            assert step[0] == RT_CUM, step[0]
            then(nc.vector.tensor_tensor(wsum[:], top[:, :, 0], top[:, :, 1], ALU.add))
            then(nc.vector.reciprocal(wsum[:], wsum[:]))
            for j in range(2):
                nc.vector.tensor_tensor(wt[:, j, :], top[:, :, j], wsum[:], ALU.mult)
            dve.wait_ge(q["rmm"], 1)
            R = bank[0][:, 0:E * TILES].rearrange("p (e k) -> p e k", k=TILES)
            then(nc.vector.tensor_scalar(ov[:], R, float(CAP), 2.0 * SLOTS, ALU.is_gt, ALU.mult))
            then(nc.vector.tensor_tensor(rk[:], R, con("slot0").rearrange("p (e k) -> p e k", k=TILES), ALU.add))
            then(nc.vector.tensor_tensor(rk[:], rk[:], ov[:], ALU.add))
            for j in range(2):
                last = nc.vector.tensor_tensor(oh[j][:], oh[j][:], rk[:], ALU.mult)
            then(last)
            for j in range(2):
                last = nc.vector.tensor_reduce(slf[:, j, :], oh[j][:].rearrange("p e k -> p k e"), AX.X, ALU.add)
            then(last)
            then(nc.vector.tensor_scalar(slu[:], slf[:], float(SLOTS), None, ALU.min))
            assert step[0] == RT_SLOT, step[0]

            def expert(i, j, first):
                e = 2 * i + j
                for f in range(1, FK, 2):
                    dve.wait_ge(q["h_mm"], FK * e + f + 1)
                    nc.vector.tensor_scalar(hT[:, f, :], bank[2 + f % 4][:, 0:CAP], b1t[:, bass.ds(e * FK + f, 1)], 0.0,
                                            ALU.add, ALU.max).then_inc(q["h_odd"], 1)
                dve.wait_ge(q["ytr_ready"], e + 1)
                if not first:
                    dve.wait_ge(q[f"yst{j}"], 32 * i)
                nc.vector.tensor_copy(yt[j][:, 0:2, :], bank[6][:].rearrange("p (c d) -> p c d", c=2))
                nc.vector.tensor_copy(yt[j][0:CAP - 2 * P, 2, :], bank[7][0:CAP - 2 * P, 0:D]).then_inc(q["yt_ready"], 1)

            expert(0, 0, True)
            expert(0, 1, True)
            with dve.Fori(1, E // 2) as i:
                for j in range(2):
                    expert(i, j, False)

            for k in range(TILES):
                r = k % RG
                dve.wait_ge(q[f"ga{r}"], 32 * (k // RG + 1))
                nc.vector.scalar_tensor_tensor(c1[:], yg[r][0][:], wt[:, 0, k:k + 1], x2[:, k, :], ALU.mult, ALU.add).then_inc(q["c_a"], 1)
                dve.wait_ge(q["c_a"], k + 1)
                nc.vector.scalar_tensor_tensor(c2[:], yg[r][1][:], wt[:, 1, k:k + 1], c1[:], ALU.mult, ALU.add).then_inc(q["c_b"], 1)
                dve.wait_ge(q["c_b"], k + 1)
                nc.vector.bn_stats(st3[:], c2[:]).then_inc(q["stat3"], 1)
                dve.wait_ge(q["stat3"], k + 1)
                nc.vector.bn_aggr(mv3[k % 2][:], st3[:]).then_inc(q["var3"], 1)
                dve.wait_ge(q["rstd3"], k + 1)
                if k >= RG:
                    dve.wait_ge(q[f"ost{r}"], 16 * (k // RG))
                nc.vector.tensor_scalar(ot[r][:], c2[:], mv3[k % 2][:, 0:1], rs3[k % 2][:], ALU.subtract, ALU.mult).then_inc(q["o_ready"], 1)


INIT_V, INIT_P = 7, 3
RT_CUM = 12
RT_SLOT = 20


def _constants():
    import numpy as np
    f = np.float32
    c = np.zeros((P, CW), f)

    def put(name, a):
        c[:a.shape[0], CC[name][0]:CC[name][1]] = a

    put("ident", np.eye(P, dtype=f))
    d = D
    base = ((np.arange(0, d, 2, dtype=f) + f(0.4 * d)) / f(1.4 * d)).astype(f)
    pos = np.arange(N, dtype=f)
    freqs = (f(1.0) / np.power(f(10000.0), np.arange(d // 2, dtype=f) / f(d // 2))).astype(f)
    ang = (pos[:, None] * freqs[None, :]).astype(f).astype(np.float64)
    scale = base[None, :].astype(np.float64) ** (pos[:, None] / 512.0)
    put("cosq", (np.cos(ang) * scale).T)
    put("sinq", (np.sin(ang) * scale).T)
    put("cosk", (np.cos(ang) / scale).T)
    put("sink", (np.sin(ang) / scale).T)
    u, v = np.arange(N)[None, :], np.arange(N)[:, None]
    put("mask", np.where(u >= v, 0.96875 ** np.maximum(u - v, 0).astype(np.float64), 0.0))
    tl, b = np.arange(P) // B, np.arange(P) % B
    put("le", (b[:, None] <= b[None, :]).astype(f))
    put("diag", ((b[:, None] < b[None, :]) | ((b[:, None] == b[None, :]) & (tl[:, None] <= tl[None, :]))).astype(f))
    put("lt", (b[:, None] < b[None, :]).astype(f))
    put("slot0", np.tile(np.repeat(np.arange(E) * CAP - 1.0, TILES), (P, 1)))
    put("keep", np.tile(np.tile((np.arange(TILES) > 0).astype(f), E), (P, 1)))
    put("iota", np.tile(np.arange(E, dtype=f), (P, 1)))
    sel = np.zeros((6, 512), f)
    rz = sel[:, 0:256].reshape(6, ST, 2, B)
    rz[0, :, 0], rz[3, :, 0], rz[1, :, 1], rz[4, :, 1] = 1, 1, 1, 1
    hn = sel[:, 256:].reshape(6, ST, B, 2)
    hn[5, :, :, 0], hn[2, :, :, 1] = 1, 1
    put("bsel", sel)
    return c


def kernel(**inputs):
    import numpy as np
    import concourse.bacc as _bacc
    from concourse.bass_utils import run_bass_kernel_spmd as _run

    a = {k: np.asarray(v) for k, v in inputs.items()}
    p = "L0_attn_"
    order = np.concatenate([np.arange(0, D, 2), np.arange(1, D, 2)])
    arrays = {
        "xtok": a["x"].transpose(1, 0, 2).reshape(S, D),
        "xT": a["x"].transpose(2, 1, 0).reshape(D, S),
        "ctxT": a["ctx_1024"].transpose(2, 0, 1).reshape(D, S),
        "consts": _constants(),
        "AT": a[p + "A"].T,
        "BwT": a[p + "Bw"].T,
        "Bb": a[p + "Bb"].reshape(SSM, 1),
        "CwE": np.concatenate([a[p + "Cw"].T, a[p + "Cb"][None], a[p + "Db"][None]]),
        "DwT": a[p + "Dw"].T,
        "W_ihT": a[p + "W_ih"].T,
        "b_gates": np.concatenate([a[p + "b_ih"].reshape(3, RNN), a[p + "b_hh"].reshape(3, RNN)]),
        "W_hhT": a[p + "W_hh"].T,
        "projT": a[p + "proj_w"].T,
        "proj_b": a[p + "proj_b"].reshape(1, D),
        "gateT": a[p + "gate_w"].T,
        "gate_b": a[p + "gate_b"].reshape(1, 2),
        "WqT": a["L0_xattn_Wq"][order].T,
        "WkT": a["L0_xattn_Wk"][order].T,
        "WvT": a["L0_xattn_Wv"].T,
        "rgwT": a["L0_ffn_gate_w"],
        "rgb": a["L0_ffn_gate_b"].reshape(1, E),
        "w1": a["L0_ffn_w1"],
        "b1": a["L0_ffn_b1"].reshape(E, FK, P).transpose(2, 0, 1).reshape(P, E * FK),
        "w2": a["L0_ffn_w2"],
        "b2": a["L0_ffn_b2"].reshape(E, HD, P).transpose(2, 0, 1).reshape(P, E * HD),
    }
    nc = _bacc.Bacc("TRN2", target_bir_lowering=False, num_devices=1)
    feeds, args = {}, []
    for name, v in arrays.items():
        v = np.ascontiguousarray(v)
        feeds[f"in_{name}"] = v
        args.append(nc.dram_tensor(f"in_{name}", v.shape, mybir.dt.from_np(v.dtype), kind="ExternalInput").ap())
    args.append(nc.dram_tensor("out_tok", (S, D), F32, kind="ExternalOutput").ap())
    mk_decoder_kernel(nc, *args)
    r = _run(nc, [feeds], core_ids=[0])
    got = r.results[0]["out_tok"]
    return np.ascontiguousarray(got.reshape(N, B, D).transpose(1, 0, 2))
```

```python
from contextlib import ExitStack

import concourse.bass as bass
from concourse import mybir

F32 = mybir.dt.float32
U32 = mybir.dt.uint32
F16 = mybir.dt.float16
BF16 = mybir.dt.bfloat16
ALU = mybir.AluOpType
ACT = mybir.ActivationFunctionType
AX = mybir.AxisListType

B, N, D = 16, 128, 256
SSM, RNN = 64, 128
FF, E = 1024, 8
S = B * N
CAP = int(1.25 * S / E)
SLOTS = E * CAP
P = 128
ST = P // B
TILES = S // P
CH = 2 * ST
CHUNKS = N // CH
HD = D // P
FK = FF // P
EPS = 1e-5

Q_UP, K_UP, V_UP = 2.0 ** 7, 2.0 ** 12, 2.0 ** 12
TINY = 1e-24
PAIRS = ((0, 0), (1, 0), (0, 1))
V_STEP = 12
RET_DOWN = 2.0 ** -8

CC = {}
_at = 0
for _name, _w in (("ident", P), ("cosq", N), ("sinq", N), ("cosk", N), ("sink", N), ("mask", N),
                  ("le", P), ("diag", P), ("lt", P), ("slot0", E * TILES), ("keep", E * TILES),
                  ("iota", E)):
    CC[_name] = (_at, _at + _w)
    _at += _w
CW = _at


def mk_decoder_kernel(nc, xtok, xT, ctxT, consts, AT, BwT, Bb, CwE, DwT, W_ihT, b_rows, bsel, W_hhT, projT,
                      gateT, gate_b, WqT, WkT, WvT, rgwT, rgb, w1, b1, w2, b2, out):
    xin = nc.dram_tensor("xin", (SLOTS, D), F32, kind="Internal").ap()
    yout = nc.dram_tensor("yout", (SLOTS + 1, D), F32, kind="Internal").ap()

    with ExitStack() as ctx:
        def sb(name, shape, dt=F32):
            return ctx.enter_context(nc.sbuf_tensor(name, shape, dt))

        def sem(name):
            return ctx.enter_context(nc.semaphore(name))

        cst = sb("cst", [P, CW])

        def con(name):
            return cst[:, CC[name][0]:CC[name][1]]

        ident = con("ident")
        whh = sb("whh", [RNN, 3 * RNN])
        whp = [sb(f"whp{i}", [RNN, 3 * RNN], BF16) for i in range(3)]
        whr = sb("whr", [RNN, 3 * RNN])
        wih = sb("wih", [P, HD, 3 * RNN])
        at_w = sb("at_w", [SSM, SSM])
        bw = sb("bw", [P, HD, SSM])
        bb = sb("bb", [SSM, 1])
        cwe = sb("cwe", [SSM + 2, D])
        dw = sb("dw", [P, HD, D])
        pw = sb("pw", [RNN, D])
        bz = sb("bz", [3 * 32, RNN + D])
        bzp = sb("bzp", [3 * 32, RNN + D], BF16)
        bzr = sb("bzr", [3 * 32, RNN + D])
        bzq = sb("bzq", [3 * 32, RNN + D], BF16)
        bst = sb("bst", [3 * 32, 512], F16)
        ones16 = sb("ones16", [3 * 32, P], F16)
        gw = sb("gw", [P, HD, 2])
        gb = sb("gb", [P, 2])
        wq = sb("wq", [P, HD, D])
        wk = sb("wk", [P, HD, D])
        wv = sb("wv", [P, HD, D])
        rgw = sb("rgw", [P, HD, E])
        rgc = sb("rgc", [P, HD, E])
        rgbt = sb("rgbt", [P, E])
        b1t = sb("b1t", [P, E * FK])
        b2t = sb("b2t", [P, E * HD])
        ones = sb("ones", [P, P])
        mhalf = sb("mhalf", [P, 4])
        epst = sb("epst", [P, 2])
        xin_t = [sb(f"xin_t{j}", [P, HD, P]) for j in range(2)]
        xfin_t = [sb(f"xfin_t{j}", [P, HD, P]) for j in range(2)]
        xres = [sb(f"xres{j}", [P, D]) for j in range(2)]
        hist = [sb(f"hist{j}", [RNN, ST * 2 * B]) for j in range(2)]
        hsb = [sb(f"hsb{j}", [SSM + 2, P]) for j in range(2)]
        rzb = sb("rzb", [RNN, 4 * B])
        h1 = sb("h1", [RNN, 2 * B], F16)
        h2 = sb("h2", [RNN, B], F16)
        nb = sb("nb", [RNN, 2 * B])
        ub = sb("ub", [RNN, 2 * B])
        mb = sb("mb", [RNN, 2 * B])
        sgb = sb("sgb", [SSM, B])
        arena = [sb(f"arena{i}", [P, 4096]) for i in range(3)]
        arena3 = sb("arena3", [P, 2048])

        def view(a, at, *dims):
            w = 1
            for d_ in dims:
                w *= d_
            ap = a[:, at:at + w]
            return ap if len(dims) == 1 else ap.rearrange("p (a b) -> p a b", a=dims[0])

        ctxb = view(arena[0], 0, HD, S)
        kT = view(arena[1], 0, HD, S)
        vt = view(arena[2], 0, B, D)
        ktm = view(arena3, 0, 4, 512)
        kp = [sb(f"kp{i}", [P, HD, S], F16) for i in range(2)]
        vp = [sb(f"vp{i}", [P, B, D], F16) for i in range(2)]
        cmx = sb("cmx", [P, HD * 8])
        sq = sb("sq", [P, 3 + HD])
        cm1 = sb("cm1", [P, HD])
        nrm = sb("nrm", [P, 4])
        inv = sb("inv", [P, 4])
        scl = sb("scl", [P, 3])
        und = sb("und", [P, 3])
        cq = sb("cq", [P, 2 * N])
        gxs = sb("gxs", [P, 2])
        s1a = sb("s1a", [P, D])
        s1b = sb("s1b", [P, D])
        st1 = sb("st1", [P, 6])
        mv1 = sb("mv1", [P, 2])
        ve1 = sb("ve1", [P, 1])
        rs1 = sb("rs1", [P, 1])
        x1 = [sb(f"x1_{j}", [P, D]) for j in range(2)]
        x1T = sb("x1T", [P, HD, 2 * P])
        tm = sb("tm", [P, 4, 2 * P])
        wsq = tm[:, 0:HD, :]
        qr = sb("qr", [P, HD, 2 * P])
        qp = [sb(f"qp{i}", [P, HD, B, CH], F16) for i in range(2)]
        ret = sb("ret", [P, B, CH])
        rp = [sb(f"rp{i}", [P, B, CH], F16) for i in range(2)]
        sT = sb("sT", [P, HD, 2 * P])
        st2 = sb("st2", [P, 2, 6])
        mv2 = sb("mv2", [P, 2, 2])
        ve2 = sb("ve2", [P, 2])
        rs2 = sb("rs2", [P, 2])
        x2 = sb("x2", [P, TILES, D])
        lg = sb("lg", [P, TILES, E])
        mx = sb("mx", [P, TILES])
        pe_ = sb("pe_", [P, TILES, E])
        top = sb("top", [P, TILES, 8])
        topi = sb("topi", [P, TILES, 8], U32)
        topf = sb("topf", [P, TILES, 2])
        oh = [sb(f"oh{j}", [P, E, TILES]) for j in range(2)]
        msk = sb("msk", [P, E, TILES])
        cum = sb("cum", [P, E, TILES])
        pre = sb("pre", [P, E, TILES])
        suf = sb("suf", [P, E, TILES])
        rk = sb("rk", [P, E, TILES])
        ov = sb("ov", [P, E, TILES])
        slf = sb("slf", [P, 2, TILES])
        slu = sb("slu", [P, 2, TILES], U32)
        wt = sb("wt", [P, 2, TILES])
        wsum = sb("wsum", [P, TILES])
        w1t = [sb(f"w1t{j}", [P, HD, FF]) for j in range(2)]
        w2t = [sb(f"w2t{j}", [P, FK, D]) for j in range(2)]
        hT = view(arena[0], 0, FK, CAP)
        yT = view(arena[0], FK * CAP, HD, CAP)
        RG = 4
        yg = [[view(arena[1], (2 * r + j) * D, D) for j in range(2)] for r in range(RG)]
        ot = [view(arena[1], (8 + r) * D, D) for r in range(RG)]
        xe = [view(arena[2], j * 3 * D, 3, D) for j in range(2)]
        xeT = [view(arena[2], 6 * D + j * HD * CAP, HD, CAP) for j in range(2)]
        yt = [view(arena3, j * 3 * D, 3, D) for j in range(2)]
        c1 = sb("c1", [P, D])
        c2 = sb("c2", [P, D])
        st3 = sb("st3", [P, 6])
        mv3 = [sb(f"mv3_{r}", [P, 2]) for r in range(2)]
        ve3 = sb("ve3", [P, 1])
        rs3 = [sb(f"rs3_{r}", [P, 1]) for r in range(2)]

        bank = [ctx.enter_context(nc.psum_tensor(f"bank{i}", [P, 512], F32)) for i in range(8)]
        RZ = bank[0:2]
        NS = bank[2:4]
        FB = bank[4]
        QB = bank[5]
        TB = bank[6]
        SC = bank[7]
        NW = 2 * ST * B

        names = ("w_hh w_k w_rec w_fin w_att w_late c_load ctx_load0 ctx_load1 ctx_load2 ctx_load3 xin0 xin1 xfin0 xfin1 xres0 xres1 "
                 "init_v init_p wsplit bsplit k_mm k_mul k_rot v_mm v_copy cmax wsqs cstat nsum nrm_done inv_done scl_done gcent "
                 "kv_hi kv_lo "
                 "in_done rz_ready ns_ready r_ready sg_ready npre_ready n_ready zh_ready h1_done hist_done h2_done hs_done "
                 "fin_ready gx_ready fuse_a fuse_b stat1 var1 eps1 rstd1 x1_ready x1tr_ready x1T_ready "
                 "q_ready qmul_ready qr_ready qh_ready ql_ready sc_ready ret_ready rh_ready rl_ready pv_ready res_ready back_ready "
                 "stat2 var2 eps2 rstd2 x2_ready rt ract rmm "
                 "scat xe0 xe1 w1l0 w1l1 w2l0 w2l1 xtr_ready xeT_ready h_mm h_even h_odd y_mm yT_ready ytr_ready yt_ready yst0 yst1 zrow "
                 "ga0 ga1 ga2 ga3 c_a c_b stat3 var3 eps3 rstd3 o_ready ost0 ost1 ost2 ost3 g_done")
        q = {n: sem(n) for n in names.split()}

        def ev(ap):
            return ap.rearrange("p (c two) -> p c two", two=2)[:, :, 0]

        def od(ap):
            return ap.rearrange("p (c two) -> p c two", two=2)[:, :, 1]

        def h_of(j, s):
            return od(hist[j][:, s * 2 * B:(s + 1) * 2 * B])

        def prev(j, s):
            return (j, s - 1) if s else (1 - j, ST - 1)

        xT_d = xT.rearrange("(h p) c -> p h c", p=P)
        ctxT_d = ctxT.rearrange("(h p) c -> p h c", p=P)
        w1_d = w1.rearrange("e (h p) f -> p e h f", p=P)
        w2_d = w2.rearrange("e (k p) d -> p e k d", p=P)

        block = ctx.enter_context(nc.Block())

        @block.sync
        def _(sp):
            def load_in(k, j, first=False):
                if not first:
                    sp.wait_ge(q["in_done"], k - 1)
                sp.dma_start(xin_t[j][:], xT_d[:, :, bass.ts(k, P)]).then_inc(q[f"xin{j}"], 16)

            def load_fin(k, j, first=False):
                if not first:
                    sp.wait_ge(q["fuse_b"], k - 1)
                sp.dma_start(xfin_t[j][:], xT_d[:, :, bass.ts(k, P)]).then_inc(q[f"xfin{j}"], 16)
                sp.dma_start(xres[j][:], xtok[bass.ts(k, P), :]).then_inc(q[f"xres{j}"], 16)

            load_in(0, 0, True)
            sp.dma_start(whh[:], W_hhT).then_inc(q["w_hh"], 16)
            sp.dma_start(bz[:], b_rows).then_inc(q["w_hh"], 16)
            sp.dma_start(wih[:], W_ihT.rearrange("(h p) r -> p h r", p=P)).then_inc(q["w_rec"], 16)
            sp.dma_start(bst[:], bsel).then_inc(q["w_rec"], 16)
            sp.dma_start(at_w[:], AT).then_inc(q["w_rec"], 16)
            sp.dma_start(bw[:], BwT.rearrange("(h p) r -> p h r", p=P)).then_inc(q["w_rec"], 16)
            sp.dma_start(bb[:], Bb).then_inc(q["w_rec"], 16)
            load_in(1, 1, True)
            sp.dma_start(wk[:], WkT.rearrange("(h p) r -> p h r", p=P)).then_inc(q["w_k"], 16)
            for i in range(4):
                sp.dma_start(ctxb[:, :, bass.ts(i, 512)], ctxT_d[:, :, bass.ts(i, 512)]).then_inc(q[f"ctx_load{i}"], 16)
                if i == 0:
                    sp.dma_start(cst[:], consts).then_inc(q["c_load"], 16)
                if i == 1:
                    sp.dma_start(dw[:], DwT.rearrange("(h p) r -> p h r", p=P)).then_inc(q["w_fin"], 16)
                    sp.dma_start(pw[:], projT).then_inc(q["w_fin"], 16)
                    sp.dma_start(cwe[:], CwE).then_inc(q["w_fin"], 16)
                    sp.dma_start(gw[:], gateT.rearrange("(h p) r -> p h r", p=P)).then_inc(q["w_fin"], 16)
                    sp.dma_start(gb[:], gate_b.to_broadcast([P, 2])).then_inc(q["w_fin"], 16)
                    load_fin(0, 0, True)
            sp.dma_start(wq[:], WqT.rearrange("(h p) r -> p h r", p=P)).then_inc(q["w_att"], 16)
            sp.dma_start(wv[:], WvT.rearrange("(h p) r -> p h r", p=P)).then_inc(q["w_att"], 16)
            sp.dma_start(rgw[:], rgwT.rearrange("(h p) r -> p h r", p=P)).then_inc(q["w_late"], 16)
            sp.dma_start(rgbt[:], rgb.to_broadcast([P, E])).then_inc(q["w_late"], 16)
            load_fin(1, 1, True)
            sp.dma_start(b1t[:], b1).then_inc(q["w_late"], 16)
            sp.dma_start(b2t[:], b2).then_inc(q["w_late"], 16)
            for e in range(2):
                sp.dma_start(w1t[e][:], w1_d[:, e]).then_inc(q[f"w1l{e}"], 16)
                sp.dma_start(w2t[e][:], w2_d[:, e]).then_inc(q[f"w2l{e}"], 16)
            with sp.Fori(0, CHUNKS - 1) as g:
                load_in(2 * g + 2, 0)
                load_fin(2 * g + 2, 0)
                load_in(2 * g + 3, 1)
                load_fin(2 * g + 3, 1)
            sp.wait_ge(q["scat"], 16 * 2 * TILES)

            def load_xe(e, j):
                sp.dma_start(xe[j][:, 0:2, :], xin[bass.ds(e * CAP, 2 * P), :].rearrange("(c p) d -> p c d", p=P)).then_inc(q[f"xe{j}"], 16)
                sp.dma_start(xe[j][0:CAP - 2 * P, 2, :], xin[bass.ds(e * CAP + 2 * P, CAP - 2 * P), :]).then_inc(q[f"xe{j}"], 16)

            def store_y(e, j):
                sp.wait_ge(q["yt_ready"], e + 1)
                sp.dma_start(yout[bass.ds(e * CAP, 2 * P), :].rearrange("(c p) d -> p c d", p=P), yt[j][:, 0:2, :]).then_inc(q[f"yst{j}"], 16)
                sp.dma_start(yout[bass.ds(e * CAP + 2 * P, CAP - 2 * P), :], yt[j][0:CAP - 2 * P, 2, :]).then_inc(q[f"yst{j}"], 16)

            load_xe(0, 0)
            load_xe(1, 1)
            with sp.Fori(0, E // 2 - 1) as i:
                for j in range(2):
                    e = 2 * i + j
                    sp.wait_ge(q["xtr_ready"], e + 1)
                    load_xe(e + 2, j)
                    sp.wait_ge(q["h_mm"], FK * (e + 1))
                    sp.dma_start(w1t[j][:], w1_d[:, e + 2]).then_inc(q[f"w1l{j}"], 16)
                    sp.wait_ge(q["y_mm"], e + 1)
                    sp.dma_start(w2t[j][:], w2_d[:, e + 2]).then_inc(q[f"w2l{j}"], 16)
                    store_y(e, j)
            store_y(E - 2, 0)
            store_y(E - 1, 1)
            with sp.Fori(0, TILES // RG) as i:
                for r in range(RG):
                    sp.wait_ge(q["o_ready"], RG * i + (r + 1))
                    sp.dma_start(out[bass.ts(RG * i + r, P), :], ot[r][:]).then_inc(q[f"ost{r}"], 16)
            for r in range(RG):
                sp.wait_ge(q[f"ost{r}"], 16 * (TILES // RG))

        @block.gpsimd
        def _(pool):
            def rot_k(i):
                pool.wait_ge(q["k_mul"], 4 * (i + 1))
                pool.tensor_tensor(kT[:, 0, bass.ts(i, 512)], ktm[:, 0, :], ktm[:, 1, :], ALU.subtract).then_inc(q["k_rot"], 1)
                pool.tensor_tensor(kT[:, 1, bass.ts(i, 512)], ktm[:, 2, :], ktm[:, 3, :], ALU.add).then_inc(q["k_rot"], 1)

            def rstd(var, eps, out_, ready, done, scratch, n):
                pool.wait_ge(var, n)
                pool.tensor_tensor(scratch[0], scratch[1], epst[:, 0:scratch[0].shape[-1]], ALU.add).then_inc(eps, 1)
                pool.wait_ge(eps, n)
                pool.tensor_tensor(out_, scratch[0], mhalf[:, 0:scratch[0].shape[-1]], ALU.pow).then_inc(done, 1)

            def rstd_1(n):
                rstd(q["var1"], q["eps1"], rs1[:], None, q["rstd1"], (ve1[:], mv1[:, 1:2]), n + 1)

            def rot_q(c):
                pool.wait_ge(q["qmul_ready"], c + 1)
                pool.tensor_tensor(qr[:, 0, :], tm[:, 0, :], tm[:, 1, :], ALU.subtract).then_inc(q["qr_ready"], 1)
                pool.tensor_tensor(qr[:, 1, :], tm[:, 2, :], tm[:, 3, :], ALU.add).then_inc(q["qr_ready"], 1)

            def q_low(c):
                pool.wait_ge(q["qr_ready"], 2 * c + 2)
                for h in range(HD):
                    pool.wait_ge(q["qh_ready"], 2 * c + h + 1)
                    pool.tensor_tensor(qp[1][:, h].rearrange("p b t -> p t b"), qr[:, h, :].rearrange("p (t b) -> p t b", b=B),
                                       qp[0][:, h].rearrange("p b t -> p t b"), ALU.subtract).then_inc(q["ql_ready"], 1)

            def ret_low(c):
                pool.wait_ge(q["rh_ready"], c + 1)
                pool.tensor_tensor(rp[1][:], ret[:], rp[0][:], ALU.subtract).then_inc(q["rl_ready"], 1)

            def rstd_2(c):
                rstd(q["var2"], q["eps2"], rs2[:], None, q["rstd2"], (ve2[:], mv2[:, :, 1]), c + 1)

            def iteration(g, A, M):
                if M:
                    ret_low(g - 2)
                if A:
                    rstd_1(2 * g - 1)
                if M:
                    rstd_2(g - 2)
                if A:
                    rot_q(g - 1)
                    q_low(g - 1)
                rstd_1(2 * g)

            pool.memset(ones[:], 1.0).then_inc(q["init_p"], 1)
            pool.memset(mhalf[:], -0.5).then_inc(q["init_p"], 1)
            pool.memset(epst[:], EPS).then_inc(q["init_p"], 1)
            pool.wait_ge(q["init_v"], INIT_V)
            pool.wait_ge(q["init_p"], INIT_P)
            for i in range(SLOTS // P):
                pool.dma_start(xin[i * P:(i + 1) * P, :], c1[:]).then_inc(q["zrow"], 16)
            pool.dma_start(yout[SLOTS:SLOTS + 1, :], c1[0:1, :]).then_inc(q["zrow"], 16)
            for i in range(4):
                rot_k(i)
            pool.wait_ge(q["nrm_done"], 1)
            pool.tensor_tensor(inv[:], nrm[:], mhalf[:], ALU.pow).then_inc(q["inv_done"], 1)
            iteration(0, False, False)
            iteration(1, True, False)
            with pool.Fori(2, CHUNKS) as g:
                iteration(g, True, True)
            ret_low(CHUNKS - 2)
            rstd_1(TILES - 1)
            rstd_2(CHUNKS - 2)
            rot_q(CHUNKS - 1)
            q_low(CHUNKS - 1)
            ret_low(CHUNKS - 1)
            rstd_2(CHUNKS - 1)
            pool.wait_ge(q["zrow"], 16 * (SLOTS // P + 1))
            pool.wait_ge(q["rt"], RT_SLOT)
            for k in range(TILES):
                for j in range(2):
                    pool.indirect_dma_start(
                        xin[:, :], bass.IndirectOffsetOnAxis(ap=slu[:, j, k:k + 1], axis=0), x2[:, k, :], None,
                        bounds_check=SLOTS - 1, oob_is_err=False).then_inc(q["scat"], 16)
            for j in range(2):
                pool.wait_ge(q[f"yst{j}"], 32 * (E // 2))

            def gather(k):
                if k >= RG:
                    pool.wait_ge(q["c_b"], k - RG + 1)
                for j in range(2):
                    pool.indirect_dma_start(
                        yg[k % RG][j][:], None, yout[:, :], bass.IndirectOffsetOnAxis(ap=slu[:, j, k:k + 1], axis=0),
                        bounds_check=SLOTS, oob_is_err=False).then_inc(q[f"ga{k % RG}"], 16)

            def rstd_3(k):
                rstd(q["var3"], q["eps3"], rs3[k % 2][:], None, q["rstd3"], (ve3[:], mv3[k % 2][:, 1:2]), k + 1)

            gather(0)
            gather(1)
            gather(2)
            gather(3)
            for k in range(TILES):
                rstd_3(k)
                if k + RG < TILES:
                    gather(k + RG)

        @block.scalar
        def _(act):
            def rec(g, j, s):
                t = CH * g + ST * j + s
                act.wait_ge(q["rz_ready"], t + 1)
                nc.scalar.activation(od(rzb[:]), RZ[j][:, s * 2 * B:(s + 1) * 2 * B], ACT.Sigmoid).then_inc(q["r_ready"], 1)
                nc.scalar.activation(sgb[:], RZ[j][0:SSM, NW + s * B:NW + (s + 1) * B], ACT.Sigmoid, bias=bb[:]).then_inc(q["sg_ready"], 1)
                act.wait_ge(q["npre_ready"], t + 1)
                nc.scalar.activation(od(nb[:]), od(ub[:]), ACT.Tanh).then_inc(q["n_ready"], 1)

            def gates(n):
                act.wait_ge(q["fin_ready"], n + 1)
                for i in range(2):
                    nc.scalar.activation(gxs[:, i:i + 1], SC[:, 256 + i:257 + i], ACT.Sigmoid, bias=gb[:, i:i + 1]).then_inc(q["gx_ready"], 1)

            def x1T_copy(c, first=False):
                act.wait_ge(q["x1tr_ready"], c + 1)
                if not first:
                    act.wait_ge(q["res_ready"], 2 * c)
                for h in range(HD):
                    nc.scalar.copy(x1T[:, h, :], TB[:, h * 256:(h + 1) * 256]).then_inc(q["x1T_ready"], 1)

            def q_high(c):
                for h in range(HD):
                    act.wait_ge(q["qr_ready"], 2 * c + h + 1)
                    nc.scalar.copy(qp[0][:, h].rearrange("p b t -> p t b"),
                                   qr[:, h, :].rearrange("p (t b) -> p t b", b=B)).then_inc(q["qh_ready"], 1)

            def ret_high(c):
                act.wait_ge(q["ret_ready"], c + 1)
                nc.scalar.copy(rp[0][:], ret[:]).then_inc(q["rh_ready"], 1)

            def w_square(i):
                if i == 0:
                    act.wait_ge(q["w_k"], 16)
                    act.wait_ge(q["w_att"], 32)
                else:
                    act.wait_ge(q["wsqs"], i)
                nc.scalar.activation(wsq, (wq, wk, wv)[i][:], ACT.Square, accum_out=sq[:, i:i + 1]).then_inc(q["wsqs"], 1)

            def v_out(b):
                act.wait_ge(q["v_mm"], b + 1)
                nc.scalar.copy(vt[:, b, :], QB[:, 0:D]).then_inc(q["v_copy"], 1)

            def k_high(i):
                act.wait_ge(q["k_rot"], 8)
                nc.scalar.activation(kp[0][:, i // 4, bass.ts(i % 4, 512)], kT[:, i // 4, bass.ts(i % 4, 512)], ACT.Copy,
                                     scale=scl[:, 1:2]).then_inc(q["kv_hi"], 1)

            def v_high(i):
                act.wait_ge(q["v_copy"], 2 * i + 2)
                nc.scalar.activation(vp[0][:, 2 * i:2 * i + 2, :], vt[:, 2 * i:2 * i + 2, :], ACT.Copy,
                                     scale=scl[:, 2:3]).then_inc(q["kv_hi"], 1)

            def iteration(g, A, M):
                for s in range(CH):
                    rec(g, s // ST, s % ST)
                    if M and s == 0:
                        ret_high(g - 2)
                    if A and s == 1:
                        gates(2 * g - 1)
                    if A and s == 8:
                        x1T_copy(g - 1, not M)
                    if s == 11:
                        gates(2 * g)
                    if A and s == 12:
                        q_high(g - 1)
                    if not A and 8 <= s < 11:
                        w_square(s - 8)
                    if not A and s >= V_STEP:
                        v_out(s - V_STEP)
                    if A and not M:
                        if s + CH - V_STEP < B:
                            v_out(s + CH - V_STEP)
                        if s == 0:
                            act.wait_ge(q["scl_done"], 1)
                        if s < 8:
                            k_high(s)
                        elif s < 12:
                            v_high(2 * s - 16)
                            v_high(2 * s - 15)

            act.wait_ge(q["init_v"], INIT_V)
            act.wait_ge(q["init_p"], INIT_P)
            act.wait_ge(q["w_rec"], 16 * 5)
            iteration(0, False, False)
            iteration(1, True, False)
            with act.Fori(2, CHUNKS) as g:
                iteration(g, True, True)
            ret_high(CHUNKS - 2)
            gates(TILES - 1)
            x1T_copy(CHUNKS - 1)
            q_high(CHUNKS - 1)
            ret_high(CHUNKS - 1)
            act.wait_ge(q["rt"], 2)
            nc.scalar.activation(pe_[:], pe_[:], ACT.Exp).then_inc(q["ract"], 1)

            def expert(i, j):
                e = 2 * i + j
                act.wait_ge(q["xtr_ready"], e + 1)
                for h in range(HD):
                    nc.scalar.copy(xeT[j][:, h, :], bank[h][:, 0:CAP]).then_inc(q["xeT_ready"], 1)
                for f in range(0, FK, 2):
                    act.wait_ge(q["h_mm"], FK * e + f + 1)
                    nc.scalar.activation(hT[:, f, :], bank[2 + f % 4][:, 0:CAP], ACT.Relu,
                                         bias=b1t[:, bass.ds(e * FK + f, 1)]).then_inc(q["h_even"], 1)
                act.wait_ge(q["y_mm"], e + 1)
                for h in range(HD):
                    nc.scalar.activation(yT[:, h, :], bank[6 + h][:, 0:CAP], ACT.Identity,
                                         bias=b2t[:, bass.ds(e * HD + h, 1)]).then_inc(q["yT_ready"], 1)

            with act.Fori(0, E // 2) as i:
                for j in range(2):
                    expert(i, j)

        @block.tensor
        def _(pe):
            def mm(out_, lhsT, rhs, start=True, stop=True):
                return nc.tensor.matmul(out_, lhsT, rhs, start=start, stop=stop, skip_group_check=True)

            def in_a(n, j):
                pe.wait_ge(q[f"xin{j}"], 16 * ((n - j) // 2 + 1) if isinstance(n, int) else 8 * n + (16 - 8 * j))
                mm(RZ[j][:, 0:NW], bzq[:, 0:RNN], bst[:, 0:NW], True, False)
                mm(NS[j][:, 0:NW], bzq[:, 0:RNN], bst[:, NW:2 * NW], True, False)
                in_half(j, 0)

            def in_half(j, h):
                for i in range(3):
                    if i < 2:
                        o = RZ[j][:, 0:NW].rearrange("p (s i b) -> p i s b", i=2, b=B)[:, i]
                    else:
                        o = NS[j][:, 0:NW].rearrange("p (s b two) -> p two s b", two=2, b=B)[:, 1]
                    mm(o, wih[:, h, i * RNN:(i + 1) * RNN], xin_t[j][:, h, :].rearrange("p (s b) -> p s b", b=B), False, False)
                return mm(RZ[j][0:SSM, NW:NW + P], bw[:, h, :], xin_t[j][:, h, :], False, False)

            def in_b(j):
                in_half(j, 1).then_inc(q["in_done"], 1)

            def rec(g, j, s):
                t = CH * g + ST * j + s
                pj, ps = prev(j, s)
                rz = [RZ[j][:, s * 32 + i * 16:s * 32 + (i + 1) * 16] for i in range(2)]
                hn = ev(NS[j][:, s * 32:s * 32 + 32])
                def parts(i, h, n):
                    for k in range(n):
                        last = mm((rz + [hn])[i], whp[k][:, i * RNN:(i + 1) * RNN], h, False, False)
                    return last

                pe.wait_ge(q["hs_done"], t + 1)
                pe.wait_ge(q["h1_done"], t + 1)
                parts(0, od(h1[:]), 3)
                parts(1, od(h1[:]), 3)
                mm(RZ[j][0:SSM, NW + s * B:NW + (s + 1) * B], at_w[:], hsb[pj][0:SSM, ps * B:(ps + 1) * B], False, False)
                pe.wait_ge(q["h2_done"], t + 1)
                parts(0, h2[:], 2)
                parts(1, h2[:], 2).then_inc(q["rz_ready"], 1)
                parts(2, od(h1[:]), 3)
                parts(2, h2[:], 2).then_inc(q["ns_ready"], 1)

            def fin_a(n, j):
                pe.wait_ge(q[f"xfin{j}"], 16 * ((n - j) // 2 + 1) if isinstance(n, int) else 8 * n + (16 - 8 * j))
                if not isinstance(n, int) or n >= 1:
                    pe.wait_ge(q["fuse_b"], n)
                mm(FB[:, 0:D], hsb[j][:], cwe[:], True, False)
                for h in range(HD):
                    mm(FB[:, 0:D], xfin_t[j][:, h, :], dw[:, h, :], False, h == 1)

            def fin_b(n, j):
                mm(FB[:, D:2 * D], od(hist[j][:]), pw[:], False, False)
                mm(FB[:, D:2 * D], ones16[:], bzq[:, RNN:RNN + D], False, True)
                for h in range(HD):
                    last = mm(SC[:, 256:258], xfin_t[j][:, h, :], gw[:, h, :], h == 0, h == 1)
                last.then_inc(q["fin_ready"], 1)

            def x1_tr(c):
                pe.wait_ge(q["x1_ready"], 2 * c + 2)
                for j in range(2):
                    for h in range(HD):
                        last = nc.tensor.transpose(TB[:, h * 256 + j * P:h * 256 + (j + 1) * P], x1[j][:, h * P:(h + 1) * P], ident)
                last.then_inc(q["x1tr_ready"], 1)

            def q_proj(c, o):
                if o == 0:
                    pe.wait_ge(q["x1T_ready"], 2 * c + 2)
                for h in range(HD):
                    last = mm(TB[:, o * 256:(o + 1) * 256], wq[:, h, o * P:(o + 1) * P], x1T[:, h, :], h == 0, h == 1)
                if o == 1:
                    last.then_inc(q["q_ready"], 1)

            def scores(c, part, gates_left=None):
                if part == 0:
                    pe.wait_ge(q["gx_ready"], gates_left or 4 * c + 6)
                    pe.wait_ge(q["ql_ready"], 2 * c + 2)
                for b in range(part * B // 2, (part + 1) * B // 2):
                    for i, (x, y, h) in enumerate((x, y, h) for x, y in PAIRS for h in range(HD)):
                        last = mm(SC[:, b * CH:(b + 1) * CH], kp[x][:, h, b * N:(b + 1) * N], qp[y][:, h, b, :], i == 0, i == 5)
                if part == 1:
                    last.then_inc(q["sc_ready"], 1)

            def mix(c, part):
                if part == 0:
                    pe.wait_ge(q["rl_ready"], c + 1)
                for b in range(part * B // 2, (part + 1) * B // 2):
                    for h in range(HD):
                        for i, (x, y) in enumerate(PAIRS):
                            last = mm(QB[:, h * 256:(h + 1) * 256].rearrange("p (t b) -> p t b", b=B)[:, :, b],
                                      vp[x][:, b, h * P:(h + 1) * P], rp[y][:, b, :], i == 0, i == 2)
                if part == 1:
                    last.then_inc(q["pv_ready"], 1)

            def back(c):
                pe.wait_ge(q["res_ready"], 2 * c + 2)
                for j in range(2):
                    for h in range(HD):
                        nc.tensor.transpose(QB[:, j * 256 + h * P:j * 256 + (h + 1) * P], sT[:, h, j * P:(j + 1) * P], ident)
                for j in range(2):
                    for h in range(HD):
                        last = mm(SC[:, 264 + j * 8:272 + j * 8], sT[:, h, j * P:(j + 1) * P], rgc[:, h, :], h == 0, h == 1)
                last.then_inc(q["back_ready"], 1)

            def k_mm(u):
                i, o = u // 2, u % 2
                pe.wait_ge(q[f"ctx_load{i}"], 16)
                if i >= 1:
                    pe.wait_ge(q["k_mul"], 4 * i - 2 + 2 * o)
                for h in range(HD):
                    last = mm((QB, TB)[o][:], wk[:, h, o * P:(o + 1) * P], ctxb[:, h, bass.ts(i, 512)], h == 0, h == 1)
                last.then_inc(q["k_mm"], 1)

            def v_mm(b):
                if b == 0:
                    pe.wait_ge(q["k_mul"], 16)
                else:
                    pe.wait_ge(q["v_copy"], b)
                for h in range(HD):
                    last = mm(QB[:, 0:D], ctxb[:, h, b * N:(b + 1) * N], wv[:, h, :], h == 0, h == 1)
                last.then_inc(q["v_mm"], 1)

            def sums():
                pe.wait_ge(q["wsqs"], 3)
                pe.wait_ge(q["cstat"], 2)
                pe.wait_ge(q["w_late"], 64)
                pe.wait_ge(q["gx_ready"], 2)
                mm(SC[:, 0:4], ones[:], sq[:, 0:4], True, False)
                mm(SC[:, 3:4], ones[:], sq[:, 4:5], False, True)
                for h in range(HD):
                    last = mm(SC[:, 8:8 + E], ones[:], rgw[:, h, :], h == 0, h == 1)
                last.then_inc(q["nsum"], 1)

            def iteration(g, A, M, has_next):
                for s in range(CH):
                    rec(g, s // ST, s % ST)
                    if A and s == 0:
                        fin_a(2 * g - 1, 1)
                    if A and s == 1:
                        if M:
                            pe.wait_ge(q["ret_ready"], g - 1)
                        else:
                            pe.wait_ge(q["gcent"], 1)
                            pe.wait_ge(q["nrm_done"], 1)
                        fin_b(2 * g - 1, 1)
                    if s == 2:
                        in_a(2 * g + 1, 1)
                    if M and s == 3:
                        mix(g - 2, 0)
                    if M and s == 4:
                        mix(g - 2, 1)
                    if s == 5:
                        in_b(1)
                    if s == 7:
                        if M:
                            pe.wait_ge(q["gx_ready"], 4 * g)
                            back(g - 2)
                        if A:
                            x1_tr(g - 1)
                    if s == 8:
                        if not A:
                            pe.wait_ge(q["w_fin"], 16 * 5)
                        fin_a(2 * g, 0)
                    if A and s in (9, 10):
                        q_proj(g - 1, s - 9)
                    if s == 11:
                        if M:
                            pe.wait_ge(q["x2_ready"], 2 * g - 2)
                        fin_b(2 * g, 0)
                    if has_next and s == 12:
                        in_a(2 * g + 2, 0)
                    if has_next and s == 13:
                        in_b(0)
                    if not A:
                        if s == 0:
                            pe.wait_ge(q["w_k"], 16)
                        if s == V_STEP:
                            pe.wait_ge(q["w_att"], 32)
                        if s < V_STEP and s % 3 != 2:
                            k_mm(s // 3 * 2 + s % 3)
                        if s >= V_STEP:
                            v_mm(s - V_STEP)
                        if s == 14:
                            sums()
                    elif not M:
                        if s + CH - V_STEP < B:
                            v_mm(s + CH - V_STEP)
                        if s == 13:
                            pe.wait_ge(q["kv_lo"], 16)
                    if A and s >= 14:
                        scores(g - 1, s - 14)

            pe.wait_ge(q["w_rec"], 16 * 5)
            pe.wait_ge(q["init_v"], INIT_V)
            pe.wait_ge(q["init_p"], INIT_P)
            pe.wait_ge(q["bsplit"], 4)
            in_a(0, 0)
            in_b(0)
            pe.wait_ge(q["wsplit"], 4)
            iteration(0, False, False, True)
            iteration(1, True, False, True)
            with pe.Fori(2, CHUNKS - 1) as g:
                iteration(g, True, True, True)
            iteration(CHUNKS - 1, True, True, False)
            c = CHUNKS - 1
            pe.wait_ge(q["hs_done"], N + 1)
            pe.wait_ge(q["h2_done"], N + 1)
            fin_a(TILES - 1, 1)
            pe.wait_ge(q["ret_ready"], c)
            fin_b(TILES - 1, 1)
            mix(c - 1, 0)
            mix(c - 1, 1)
            x1_tr(c)
            pe.wait_ge(q["gx_ready"], 4 * c + 4)
            back(c - 1)
            q_proj(c, 0)
            q_proj(c, 1)
            pe.wait_ge(q["x2_ready"], 2 * c)
            scores(c, 0, 2 * TILES)
            scores(c, 1)
            mix(c, 0)
            mix(c, 1)
            pe.wait_ge(q["ret_ready"], c + 1)
            back(c)
            pe.wait_ge(q["rt"], RT_CUM)
            flat = [x[:].rearrange("p e k -> p (e k)") for x in (pre, msk, suf)]
            for i, name in enumerate(("le", "diag", "lt")):
                last = mm(bank[0][:, 0:E * TILES], con(name), flat[i], i == 0, i == 2)
            last.then_inc(q["rmm"], 1)
            pe.wait_ge(q["rt"], RT_SLOT)

            def expert(i, j, first):
                e = 2 * i + j
                pe.wait_ge(q[f"xe{j}"], 32 * i + 32)
                if not first:
                    pe.wait_ge(q["xeT_ready"], 2 * e)
                for c3 in range(3):
                    m = min(P, CAP - c3 * P)
                    for h in range(HD):
                        last = nc.tensor.transpose(bank[h][:, c3 * P:c3 * P + m], xe[j][0:m, c3, h * P:(h + 1) * P], ident[0:m, 0:m])
                last.then_inc(q["xtr_ready"], 1)
                pe.wait_ge(q["xeT_ready"], 2 * e + 2)
                pe.wait_ge(q[f"w1l{j}"], 16 * i + 16)
                for f in range(FK):
                    if f >= 4:
                        pe.wait_ge(q["h_odd" if f % 2 else "h_even"], FK // 2 * e + (f - 4) // 2 + 1)
                    for h in range(HD):
                        last = mm(bank[2 + f % 4][:, 0:CAP], w1t[j][:, h, f * P:(f + 1) * P], xeT[j][:, h, :], h == 0, h == 1)
                    last.then_inc(q["h_mm"], 1)
                pe.wait_ge(q["h_even"], FK // 2 * (e + 1))
                pe.wait_ge(q["h_odd"], FK // 2 * (e + 1))
                pe.wait_ge(q[f"w2l{j}"], 16 * i + 16)
                if not first:
                    pe.wait_ge(q["yt_ready"], e)
                for h in range(HD):
                    for f in range(FK):
                        last = mm(bank[6 + h][:, 0:CAP], w2t[j][:, f, h * P:(h + 1) * P], hT[:, f, :], f == 0, f == FK - 1)
                last.then_inc(q["y_mm"], 1)
                pe.wait_ge(q["yT_ready"], 2 * e + 2)
                for c3 in range(3):
                    m = min(P, CAP - c3 * P)
                    for h in range(HD):
                        w = c3 * D + h * P
                        last = nc.tensor.transpose(bank[6 + w // 512][0:m, w % 512:w % 512 + P], yT[:, h, c3 * P:c3 * P + m], ident)
                last.then_inc(q["ytr_ready"], 1)

            expert(0, 0, True)
            expert(0, 1, False)
            with pe.Fori(1, E // 2) as i:
                for j in range(2):
                    expert(i, j, False)

        @block.vector
        def _(dve):
            def rec(g, j, s):
                t = CH * g + ST * j + s
                pj, ps = prev(j, s)
                dve.wait_ge(q["ns_ready"], t + 1)
                dve.wait_ge(q["r_ready"], t + 1)
                nc.vector.tensor_tensor_scan(ub[:], rzb[:, 0:2 * B], NS[j][:, s * 32:s * 32 + 32], 0.0,
                                             ALU.mult, ALU.add).then_inc(q["npre_ready"], 1)
                nc.vector.tensor_scalar(ev(mb[:]), od(rzb[:, 2 * B:4 * B]), -1.0, 1.0, ALU.mult, ALU.add).then_inc(q["zh_ready"], 1)
                nc.vector.tensor_tensor(od(mb[:]), od(rzb[:, 2 * B:4 * B]), h_of(pj, ps), ALU.mult).then_inc(q["zh_ready"], 1)
                dve.wait_ge(q["zh_ready"], 2 * t + 2)
                dve.wait_ge(q["n_ready"], t + 1)
                nc.vector.tensor_tensor_scan(h1[:], nb[:], mb[:], 0.0, ALU.mult, ALU.add).then_inc(q["h1_done"], 1)
                nc.vector.tensor_tensor_scan(hist[j][:, s * 32:(s + 1) * 32], nb[:], mb[:], 0.0, ALU.mult, ALU.add).then_inc(q["hist_done"], 1)
                dve.wait_ge(q["h1_done"], t + 2)
                dve.wait_ge(q["hist_done"], t + 1)
                nc.vector.tensor_tensor(h2[:], h_of(j, s), od(h1[:]), ALU.subtract).then_inc(q["h2_done"], 1)
                dve.wait_ge(q["sg_ready"], t + 1)
                nc.vector.scalar_tensor_tensor(hsb[j][0:SSM, s * B:(s + 1) * B], RZ[j][0:SSM, NW + s * B:NW + (s + 1) * B], bb[:], sgb[:],
                                               ALU.add, ALU.mult).then_inc(q["hs_done"], 1)

            def fuse(n, j, part):
                if part == 0:
                    dve.wait_ge(q["gx_ready"], 2 * n + 2)
                    dve.wait_ge(q[f"xres{j}"], 16 * ((n - j) // 2 + 1) if isinstance(n, int) else 8 * n + (16 - 8 * j))
                    nc.vector.scalar_tensor_tensor(s1a[:], FB[:, 0:D], gxs[:, 0:1], xres[j][:], ALU.mult, ALU.add).then_inc(q["fuse_a"], 1)
                else:
                    dve.wait_ge(q["fuse_a"], n + 1)
                    nc.vector.scalar_tensor_tensor(s1b[:], FB[:, D:2 * D], gxs[:, 1:2], s1a[:], ALU.mult, ALU.add).then_inc(q["fuse_b"], 1)

            def stats_1(n):
                dve.wait_ge(q["fuse_b"], n + 1)
                nc.vector.bn_stats(st1[:], s1b[:]).then_inc(q["stat1"], 1)
                dve.wait_ge(q["init_v"], INIT_V)
                dve.wait_ge(q["stat1"], n + 1)
                nc.vector.bn_aggr(mv1[:], st1[:]).then_inc(q["var1"], 1)

            def norm_1(n, j):
                dve.wait_ge(q["rstd1"], n + 1)
                nc.vector.tensor_scalar(x1[j][:], s1b[:], mv1[:, 0:1], rs1[:], ALU.subtract, ALU.mult).then_inc(q["x1_ready"], 1)

            def rotate(c, o):
                dve.wait_ge(q["q_ready"], c + 1)
                for i, w in ((0, 0), (3, 1)) if o == 0 else ((2, 0), (1, 1)):
                    tab = cq[:, bass.ds(c * CH + w * N, CH)].unsqueeze(2).to_broadcast([P, CH, B])
                    last = nc.vector.tensor_tensor(tm[:, i, :].rearrange("p (t b) -> p t b", b=B),
                                                   TB[:, o * 256:(o + 1) * 256].rearrange("p (t b) -> p t b", b=B), tab, ALU.mult)
                if o == 1:
                    last.then_inc(q["qmul_ready"], 1)

            def decay(c):
                dve.wait_ge(q["sc_ready"], c + 1)
                m = con("mask")[:, bass.ts(c, CH)].unsqueeze(1).to_broadcast([P, B, CH])
                nc.vector.tensor_tensor(ret[:], SC[:, 0:B * CH].rearrange("p (b t) -> p b t", t=CH), m,
                                        ALU.mult).then_inc(q["ret_ready"], 1)

            def residual(c, h):
                dve.wait_ge(q["pv_ready"], c + 1)
                nc.vector.scalar_tensor_tensor(sT[:, h, :], QB[:, h * 256:(h + 1) * 256], und[:, 2:3], x1T[:, h, :],
                                               ALU.mult, ALU.add).then_inc(q["res_ready"], 1)

            def stats_2(c, j):
                dve.wait_ge(q["back_ready"], c + 1)
                last = nc.vector.bn_stats(st2[:, j, :], QB[:, j * 256:(j + 1) * 256])
                if j == 1:
                    last.then_inc(q["stat2"], 1)
                    dve.wait_ge(q["init_v"], INIT_V)
                    dve.wait_ge(q["stat2"], c + 1)
                    for i in range(2):
                        last = nc.vector.bn_aggr(mv2[:, i, :], st2[:, i, :])
                    last.then_inc(q["var2"], 1)

            def norm_2(c):
                dve.wait_ge(q["rstd2"], c + 1)
                for j in range(2):
                    nc.vector.scalar_tensor_tensor(lg[:, bass.ds(2 * c + j, 1), :].rearrange("p o e -> p (o e)"), SC[:, 264 + j * 8:272 + j * 8], rs2[:, j:j + 1],
                                                   rgbt[:], ALU.mult, ALU.add)
                    nc.vector.tensor_scalar(x2[:, bass.ds(2 * c + j, 1), :].rearrange("p o d -> p (o d)"), QB[:, j * 256:(j + 1) * 256], mv2[:, j, 0:1],
                                            rs2[:, j:j + 1], ALU.subtract, ALU.mult).then_inc(q["x2_ready"], 1)

            def k_rotate(u):
                i, o = u // 2, u % 2
                if u == 0:
                    dve.wait_ge(q["c_load"], 16)
                dve.wait_ge(q["k_mm"], u + 1)
                if i >= 1:
                    dve.wait_ge(q["k_rot"], 2 * i)
                for n, name in ((0, "cosk"), (3, "sink")) if o == 0 else ((2, "cosk"), (1, "sink")):
                    nc.vector.tensor_tensor(ktm[:, n, :].rearrange("p (b t) -> p b t", t=N),
                                            (QB, TB)[o][:].rearrange("p (b t) -> p b t", t=N),
                                            con(name).unsqueeze(1).to_broadcast([P, 4, N]), ALU.mult).then_inc(q["k_mul"], 1)

            def c_max(i):
                dve.wait_ge(q[f"ctx_load{i}"], 16)
                nc.vector.tensor_reduce(cmx[:, i * HD:(i + 1) * HD], ctxb[:, :, bass.ts(i, 512)], AX.X, ALU.max,
                                        apply_absolute_value=True).then_inc(q["cmax"], 1)

            def c_square():
                dve.wait_ge(q["cmax"], 4)
                nc.vector.tensor_reduce(cm1[:], cmx[:, 0:4 * HD].rearrange("p (i h) -> p h i", h=HD), AX.X, ALU.max).then_inc(q["cstat"], 1)
                dve.wait_ge(q["cstat"], 1)
                nc.vector.tensor_tensor(sq[:, 3:3 + HD], cm1[:], cm1[:], ALU.mult).then_inc(q["cstat"], 1)

            def norms():
                dve.wait_ge(q["nsum"], 1)
                for h in range(HD):
                    last = nc.vector.scalar_tensor_tensor(rgc[:, h, :], SC[:, 8:8 + E], -1.0 / D, rgw[:, h, :], ALU.mult, ALU.add)
                last.then_inc(q["gcent"], 1)
                nc.vector.tensor_scalar(nrm[:], SC[:, 0:4], TINY, None, ALU.max).then_inc(q["nrm_done"], 1)

            def scales():
                dve.wait_ge(q["inv_done"], 1)
                nc.vector.tensor_scalar(scl[:, 0:1], inv[:, 0:1], Q_UP, None, ALU.mult)
                nc.vector.tensor_scalar(scl[:, 1:3], inv[:, 1:3], inv[:, 3:4], K_UP, ALU.mult, ALU.mult).then_inc(q["scl_done"], 1)
                dve.wait_ge(q["scl_done"], 1)
                nc.vector.tensor_scalar(cq[:], cst[:, CC["cosq"][0]:CC["sinq"][1]], scl[:, 0:1], None, ALU.mult).then_inc(q["scl_done"], 1)
                nc.vector.tensor_scalar(und[:, 0:1], scl[:, 0:1], scl[:, 1:2], scl[:, 2:3], ALU.mult, ALU.mult).then_inc(q["scl_done"], 1)
                dve.wait_ge(q["scl_done"], 3)
                nc.vector.reciprocal(und[:, 1:2], und[:, 0:1]).then_inc(q["scl_done"], 1)
                dve.wait_ge(q["scl_done"], 4)
                nc.vector.tensor_scalar(und[:, 2:3], und[:, 1:2], 1.0 / RET_DOWN, None, ALU.mult).then_inc(q["scl_done"], 1)

            def k_low(i):
                dve.wait_ge(q["kv_hi"], i + 1)
                w = bass.ts(i % 4, 512)
                nc.vector.scalar_tensor_tensor(kp[1][:, i // 4, w], kT[:, i // 4, w], scl[:, 1:2], kp[0][:, i // 4, w],
                                               ALU.mult, ALU.subtract).then_inc(q["kv_lo"], 1)

            def v_low(i):
                dve.wait_ge(q["kv_hi"], 8 + i + 1)
                w = slice(2 * i, 2 * i + 2)
                nc.vector.scalar_tensor_tensor(vp[1][:, w, :], vt[:, w, :], scl[:, 2:3], vp[0][:, w, :],
                                               ALU.mult, ALU.subtract).then_inc(q["kv_lo"], 1)

            def iteration(g, A, M):
                for s in range(CH):
                    rec(g, s // ST, s % ST)
                    if M and s == 0:
                        decay(g - 2)
                    if A:
                        if s == 1:
                            norm_1(2 * g - 2, 0)
                        if s == 2:
                            fuse(2 * g - 1, 1, 0)
                        if s == 3:
                            fuse(2 * g - 1, 1, 1)
                        if s == 4:
                            stats_1(2 * g - 1)
                        if s == 5:
                            norm_1(2 * g - 1, 1)
                    if M:
                        if s in (5, 6):
                            residual(g - 2, s - 5)
                        if s in (8, 9):
                            stats_2(g - 2, s - 8)
                        if s == 10:
                            norm_2(g - 2)
                    if A and s in (11, 12):
                        rotate(g - 1, s - 11)
                    if s == 13:
                        fuse(2 * g, 0, 0)
                    if s == 14:
                        fuse(2 * g, 0, 1)
                    if s == 15:
                        stats_1(2 * g)
                    if not A:
                        if s < 12 and s % 3 != 0:
                            k_rotate(s // 3 * 2 + s % 3 - 1)
                        if s in (3, 6, 9, 12):
                            c_max(s // 3 - 1)
                        if s == 12:
                            c_square()
                        if s == 15:
                            norms()
                    elif not M:
                        if s == 0:
                            scales()
                        if 2 <= s < 10:
                            k_low(s - 2)
                        if 9 <= s < 13:
                            v_low(2 * s - 18)
                            v_low(2 * s - 17)

            nc.vector.memset(rzb[:], 0.0).then_inc(q["init_v"], 1)
            nc.vector.memset(nb[:], 0.0).then_inc(q["init_v"], 1)
            nc.vector.memset(hist[1][:], 0.0).then_inc(q["init_v"], 1)
            nc.vector.memset(hsb[1][0:SSM, :], 0.0).then_inc(q["init_v"], 1)
            for j in range(2):
                nc.vector.memset(hsb[j][SSM:SSM + 2, :], 1.0).then_inc(q["init_v"], 1)
            nc.vector.memset(c1[:], 0.0).then_inc(q["init_v"], 1)
            nc.vector.memset(ones16[:], 1.0).then_inc(q["init_v"], 1)
            dve.wait_ge(q["w_hh"], 32)
            nc.vector.tensor_copy(bzp[:], bz[:]).then_inc(q["bsplit"], 1)
            nc.vector.tensor_copy(whp[0][:], whh[:]).then_inc(q["wsplit"], 1)
            dve.wait_ge(q["bsplit"], 1)
            nc.vector.tensor_tensor(bzr[:], bz[:], bzp[:], ALU.subtract).then_inc(q["bsplit"], 1)
            dve.wait_ge(q["wsplit"], 1)
            nc.vector.tensor_tensor(whr[:], whh[:], whp[0][:], ALU.subtract).then_inc(q["wsplit"], 1)
            dve.wait_ge(q["bsplit"], 2)
            nc.vector.tensor_copy(bzq[0:32, :], bzp[0:32, :])
            nc.vector.tensor_copy(bzq[32:64, :], bzr[32:64, :])
            nc.vector.tensor_copy(bzq[64:96, :], bzr[64:96, :]).then_inc(q["bsplit"], 1)
            dve.wait_ge(q["bsplit"], 3)
            nc.vector.tensor_tensor(bzq[64:96, :], bzr[64:96, :], bzq[64:96, :], ALU.subtract).then_inc(q["bsplit"], 1)
            dve.wait_ge(q["wsplit"], 2)
            nc.vector.tensor_copy(whp[1][:], whr[:]).then_inc(q["wsplit"], 1)
            dve.wait_ge(q["wsplit"], 3)
            nc.vector.tensor_tensor(whp[2][:], whr[:], whp[1][:], ALU.subtract).then_inc(q["wsplit"], 1)
            dve.wait_ge(q["init_p"], INIT_P)
            nc.vector.memset(h1[:], 0.0).then_inc(q["h1_done"], 1)
            nc.vector.memset(h2[:], 0.0).then_inc(q["h2_done"], 1)
            nc.vector.memset(mb[:], 0.0).then_inc(q["hs_done"], 1)
            iteration(0, False, False)
            iteration(1, True, False)
            with dve.Fori(2, CHUNKS) as g:
                iteration(g, True, True)
            n, c = TILES - 1, CHUNKS - 1
            decay(c - 1)
            norm_1(n - 1, 0)
            fuse(n, 1, 0)
            fuse(n, 1, 1)
            stats_1(n)
            norm_1(n, 1)
            residual(c - 1, 0)
            residual(c - 1, 1)
            stats_2(c - 1, 0)
            stats_2(c - 1, 1)
            norm_2(c - 1)
            rotate(c, 0)
            rotate(c, 1)
            decay(c)
            residual(c, 0)
            residual(c, 1)
            stats_2(c, 0)
            stats_2(c, 1)
            norm_2(c)

            step = [0]

            def then(ins):
                step[0] += 1
                ins.then_inc(q["rt"], 1)
                dve.wait_ge(q["rt"], step[0])

            def bk(ap):
                return ap.unsqueeze(2).to_broadcast([P, TILES, E])

            dve.wait_ge(q["x2_ready"], TILES)
            then(nc.vector.tensor_reduce(mx[:], lg[:], AX.X, ALU.max))
            then(nc.vector.tensor_tensor(pe_[:], lg[:], bk(mx[:]), ALU.subtract))
            dve.wait_ge(q["ract"], 1)
            then(nc.vector.tensor_reduce(mx[:], pe_[:], AX.X, ALU.add))
            then(nc.vector.reciprocal(mx[:], mx[:]))
            then(nc.vector.tensor_tensor(pe_[:], pe_[:], bk(mx[:]), ALU.mult))
            for k in range(TILES):
                last = nc.vector.max(top[:, k, :], pe_[:, k, :])
            then(last)
            for k in range(TILES):
                last = nc.vector.max_index(topi[:, k, :], top[:, k, :], pe_[:, k, :])
            then(last)
            then(nc.vector.tensor_copy(topf[:], topi[:, :, 0:2]))
            for j in range(2):
                last = nc.vector.tensor_tensor(oh[j][:], topf[:, :, j].unsqueeze(1).to_broadcast([P, E, TILES]),
                                               con("iota").unsqueeze(2).to_broadcast([P, E, TILES]), ALU.is_equal)
            then(last)
            then(nc.vector.tensor_tensor(msk[:], oh[0][:], oh[1][:], ALU.add))
            then(nc.vector.tensor_tensor_scan(cum[:].rearrange("p e k -> p (e k)"), con("keep"), msk[:].rearrange("p e k -> p (e k)"),
                                              0.0, ALU.mult, ALU.add))
            nc.vector.tensor_tensor(pre[:], cum[:], msk[:], ALU.subtract)
            then(nc.vector.tensor_tensor(suf[:], cum[:, :, TILES - 1:TILES].to_broadcast([P, E, TILES]), cum[:], ALU.subtract))
            assert step[0] == RT_CUM, step[0]
            then(nc.vector.tensor_tensor(wsum[:], top[:, :, 0], top[:, :, 1], ALU.add))
            then(nc.vector.reciprocal(wsum[:], wsum[:]))
            for j in range(2):
                nc.vector.tensor_tensor(wt[:, j, :], top[:, :, j], wsum[:], ALU.mult)
            dve.wait_ge(q["rmm"], 1)
            R = bank[0][:, 0:E * TILES].rearrange("p (e k) -> p e k", k=TILES)
            then(nc.vector.tensor_scalar(ov[:], R, float(CAP), 2.0 * SLOTS, ALU.is_gt, ALU.mult))
            then(nc.vector.tensor_tensor(rk[:], R, con("slot0").rearrange("p (e k) -> p e k", k=TILES), ALU.add))
            then(nc.vector.tensor_tensor(rk[:], rk[:], ov[:], ALU.add))
            for j in range(2):
                last = nc.vector.tensor_tensor(oh[j][:], oh[j][:], rk[:], ALU.mult)
            then(last)
            for j in range(2):
                last = nc.vector.tensor_reduce(slf[:, j, :], oh[j][:].rearrange("p e k -> p k e"), AX.X, ALU.add)
            then(last)
            then(nc.vector.tensor_scalar(slu[:], slf[:], float(SLOTS), None, ALU.min))
            assert step[0] == RT_SLOT, step[0]

            def expert(i, j, first):
                e = 2 * i + j
                for f in range(1, FK, 2):
                    dve.wait_ge(q["h_mm"], FK * e + f + 1)
                    nc.vector.tensor_scalar(hT[:, f, :], bank[2 + f % 4][:, 0:CAP], b1t[:, bass.ds(e * FK + f, 1)], 0.0,
                                            ALU.add, ALU.max).then_inc(q["h_odd"], 1)
                dve.wait_ge(q["ytr_ready"], e + 1)
                if not first:
                    dve.wait_ge(q[f"yst{j}"], 32 * i)
                nc.vector.tensor_copy(yt[j][:, 0:2, :], bank[6][:].rearrange("p (c d) -> p c d", c=2))
                nc.vector.tensor_copy(yt[j][0:CAP - 2 * P, 2, :], bank[7][0:CAP - 2 * P, 0:D]).then_inc(q["yt_ready"], 1)

            expert(0, 0, True)
            expert(0, 1, True)
            with dve.Fori(1, E // 2) as i:
                for j in range(2):
                    expert(i, j, False)

            for k in range(TILES):
                r = k % RG
                dve.wait_ge(q[f"ga{r}"], 32 * (k // RG + 1))
                nc.vector.scalar_tensor_tensor(c1[:], yg[r][0][:], wt[:, 0, k:k + 1], x2[:, k, :], ALU.mult, ALU.add).then_inc(q["c_a"], 1)
                dve.wait_ge(q["c_a"], k + 1)
                nc.vector.scalar_tensor_tensor(c2[:], yg[r][1][:], wt[:, 1, k:k + 1], c1[:], ALU.mult, ALU.add).then_inc(q["c_b"], 1)
                dve.wait_ge(q["c_b"], k + 1)
                nc.vector.bn_stats(st3[:], c2[:]).then_inc(q["stat3"], 1)
                dve.wait_ge(q["stat3"], k + 1)
                nc.vector.bn_aggr(mv3[k % 2][:], st3[:]).then_inc(q["var3"], 1)
                dve.wait_ge(q["rstd3"], k + 1)
                if k >= RG:
                    dve.wait_ge(q[f"ost{r}"], 16 * (k // RG))
                nc.vector.tensor_scalar(ot[r][:], c2[:], mv3[k % 2][:, 0:1], rs3[k % 2][:], ALU.subtract, ALU.mult).then_inc(q["o_ready"], 1)


INIT_V, INIT_P = 8, 3
RT_CUM = 12
RT_SLOT = 20


def _constants():
    import numpy as np
    f = np.float32
    c = np.zeros((P, CW), f)

    def put(name, a):
        c[:a.shape[0], CC[name][0]:CC[name][1]] = a

    put("ident", np.eye(P, dtype=f))
    d = D
    base = ((np.arange(0, d, 2, dtype=f) + f(0.4 * d)) / f(1.4 * d)).astype(f)
    pos = np.arange(N, dtype=f)
    freqs = (f(1.0) / np.power(f(10000.0), np.arange(d // 2, dtype=f) / f(d // 2))).astype(f)
    ang = (pos[:, None] * freqs[None, :]).astype(f).astype(np.float64)
    scale = base[None, :].astype(np.float64) ** (pos[:, None] / 512.0)
    put("cosq", (np.cos(ang) * scale).T)
    put("sinq", (np.sin(ang) * scale).T)
    put("cosk", (np.cos(ang) / scale).T)
    put("sink", (np.sin(ang) / scale).T)
    u, v = np.arange(N)[None, :], np.arange(N)[:, None]
    put("mask", np.where(u >= v, 0.96875 ** np.maximum(u - v, 0).astype(np.float64), 0.0) * RET_DOWN)
    tl, b = np.arange(P) // B, np.arange(P) % B
    put("le", (b[:, None] <= b[None, :]).astype(f))
    put("diag", ((b[:, None] < b[None, :]) | ((b[:, None] == b[None, :]) & (tl[:, None] <= tl[None, :]))).astype(f))
    put("lt", (b[:, None] < b[None, :]).astype(f))
    put("slot0", np.tile(np.repeat(np.arange(E) * CAP - 1.0, TILES), (P, 1)))
    put("keep", np.tile(np.tile((np.arange(TILES) > 0).astype(f), E), (P, 1)))
    put("iota", np.tile(np.arange(E, dtype=f), (P, 1)))
    return c


def _bias_selection():
    import numpy as np
    sel = np.zeros((3, 32, 512), np.float16)
    rz = sel[:, :, 0:256].reshape(3, 32, ST, 2, B)
    rz[:, 0, :, 0], rz[:, 3, :, 0], rz[:, 1, :, 1], rz[:, 4, :, 1] = 1, 1, 1, 1
    hn = sel[:, :, 256:].reshape(3, 32, ST, B, 2)
    hn[:, 5, :, :, 0], hn[:, 2, :, :, 1] = 1, 1
    return sel.reshape(3 * 32, 512)


def kernel(**inputs):
    import numpy as np
    import concourse.bacc as _bacc
    from concourse.bass_utils import run_bass_kernel_spmd as _run

    a = {k: np.asarray(v) for k, v in inputs.items()}
    p = "L0_attn_"
    order = np.concatenate([np.arange(0, D, 2), np.arange(1, D, 2)])
    b_rows = np.zeros((3, 32, RNN + D), np.float32)
    b_rows[:, 0:6, 0:RNN] = np.concatenate([a[p + "b_ih"].reshape(3, RNN), a[p + "b_hh"].reshape(3, RNN)])
    b_rows[:, 0, RNN:] = a[p + "proj_b"]
    arrays = {
        "xtok": a["x"].transpose(1, 0, 2).reshape(S, D),
        "xT": a["x"].transpose(2, 1, 0).reshape(D, S),
        "ctxT": a["ctx_1024"].transpose(2, 0, 1).reshape(D, S),
        "consts": _constants(),
        "AT": a[p + "A"].T,
        "BwT": a[p + "Bw"].T,
        "Bb": a[p + "Bb"].reshape(SSM, 1),
        "CwE": np.concatenate([a[p + "Cw"].T, a[p + "Cb"][None], a[p + "Db"][None]]),
        "DwT": a[p + "Dw"].T,
        "W_ihT": a[p + "W_ih"].T,
        "b_rows": b_rows.reshape(3 * 32, RNN + D),
        "bsel": _bias_selection(),
        "W_hhT": a[p + "W_hh"].T,
        "projT": a[p + "proj_w"].T,
        "gateT": a[p + "gate_w"].T,
        "gate_b": a[p + "gate_b"].reshape(1, 2),
        "WqT": a["L0_xattn_Wq"][order].T,
        "WkT": a["L0_xattn_Wk"][order].T,
        "WvT": a["L0_xattn_Wv"].T,
        "rgwT": a["L0_ffn_gate_w"],
        "rgb": a["L0_ffn_gate_b"].reshape(1, E),
        "w1": a["L0_ffn_w1"],
        "b1": a["L0_ffn_b1"].reshape(E, FK, P).transpose(2, 0, 1).reshape(P, E * FK),
        "w2": a["L0_ffn_w2"],
        "b2": a["L0_ffn_b2"].reshape(E, HD, P).transpose(2, 0, 1).reshape(P, E * HD),
    }
    nc = _bacc.Bacc("TRN2", target_bir_lowering=False, num_devices=1)
    feeds, args = {}, []
    for name, v in arrays.items():
        v = np.ascontiguousarray(v)
        feeds[f"in_{name}"] = v
        args.append(nc.dram_tensor(f"in_{name}", v.shape, mybir.dt.from_np(v.dtype), kind="ExternalInput").ap())
    args.append(nc.dram_tensor("out_tok", (S, D), F32, kind="ExternalOutput").ap())
    mk_decoder_kernel(nc, *args)
    r = _run(nc, [feeds], core_ids=[0])
    got = r.results[0]["out_tok"]
    return np.ascontiguousarray(got.reshape(N, B, D).transpose(1, 0, 2))
```

```python
from contextlib import ExitStack

import concourse.bass as bass
from concourse import mybir

F32 = mybir.dt.float32
U32 = mybir.dt.uint32
F16 = mybir.dt.float16
BF16 = mybir.dt.bfloat16
ALU = mybir.AluOpType
ACT = mybir.ActivationFunctionType
AX = mybir.AxisListType

B, N, D = 16, 128, 256
SSM, RNN = 64, 128
FF, E = 1024, 8
S = B * N
CAP = int(1.25 * S / E)
CT = -(-CAP // 128)
P = 128
ST = P // B
TILES = S // P
CH = 2 * ST
CHUNKS = N // CH
HD = D // P
FK = FF // P
EPS = 1e-5

Q_UP, K_UP, V_UP = 2.0 ** 7, 2.0 ** 12, 2.0 ** 12
W_UP = 2.0 ** 11
TINY = 1e-24
PAIRS = ((0, 0), (1, 0), (0, 1))
V_FIRST = (1, 3, 9, 11)
V_EARLY = len(V_FIRST)
V_SLOTS = (2, 4, 6, 7, 9, 11)
PIECES = ("k0", "k1", "k2", "k3", "k4", "k5", "v0", "v1", "k6", "v2", "k7", "v3", "v4", "v5", "v6", "v7")
HI_STEP = (1, 1, 2, 2, 3, 3, 4, 5, 5, 6, 8, 8, 9, 10, 12, 13)
LO_STEP = (2, 3, 4, 5, 6, 6, 7, 7, 8, 8, 9, 9, 10, 13, 13, 14)
RET_DOWN = 2.0 ** -8

CC = {}
_at = 0
for _name, _w in (("ident", P), ("cosq", N), ("sinq", N), ("cosk", N), ("sink", N), ("mask", N),
                  ("le", P), ("diag", P), ("lt", P), ("slot0", E * TILES), ("keep", E * TILES),
                  ("iota", E), ("tok", TILES)):
    CC[_name] = (_at, _at + _w)
    _at += _w
CW = _at


def mk_decoder_kernel(nc, xtok, xT, ctxT, consts, AbE, BwT, CwE, DwT, W_ihT, b_rows, bsel, iota, W_hhT, projT,
                      gateT, gate_b, WqT, WkT, WvT, rgwT, rgb, w1, b1, w2, b2, out):
    x2_d = nc.dram_tensor("x2_d", (S, D), F32, kind="Internal").ap()
    ybuf = nc.dram_tensor("ybuf", (2 * S, D), F32, kind="Internal").ap()

    with ExitStack() as ctx:
        def sb(name, shape, dt=F32):
            return ctx.enter_context(nc.sbuf_tensor(name, shape, dt))

        def sem(name):
            return ctx.enter_context(nc.semaphore(name))

        cst = sb("cst", [P, CW])

        def con(name):
            return cst[:, CC[name][0]:CC[name][1]]

        ident = con("ident")
        whh = sb("whh", [RNN, 3 * RNN])
        whp = [sb(f"whp{i}", [RNN, 3 * RNN], BF16) for i in range(3)]
        wih = sb("wih", [P, HD, 3 * RNN])
        at_w = sb("at_w", [SSM + 2, SSM])
        bw = sb("bw", [P, HD, SSM])
        cwe = sb("cwe", [SSM + 2, D])
        dw = sb("dw", [P, HD, D])
        pw = sb("pw", [RNN, D])
        bz = sb("bz", [3 * 32, RNN + D])
        bzp = sb("bzp", [3 * 32, RNN + D], BF16)
        bzq = sb("bzq", [3 * 32, RNN + D], BF16)
        bst = sb("bst", [3 * 32, 512], F16)
        iota16 = sb("iota16", [P, P + E * CT], F16)
        ones16 = sb("ones16", [3 * 32, P], F16)
        gw = sb("gw", [P, HD, 2])
        gb = sb("gb", [P, 2])
        wq = sb("wq", [P, HD, D])
        wk = sb("wk", [P, HD, D])
        wv = sb("wv", [P, HD, D])
        rgw = sb("rgw", [P, HD, E])
        rgi = sb("rgi", [P, HD, P + E])
        rgbt = sb("rgbt", [P, E])
        b1t = sb("b1t", [P, E * FK])
        b2t = sb("b2t", [P, E * HD])
        ones = sb("ones", [P, P])
        mhalf = sb("mhalf", [P, 4])
        epst = sb("epst", [P, 2])
        xin_t = [sb(f"xin_t{j}", [P, HD, P]) for j in range(2)]
        xfin_t = [sb(f"xfin_t{j}", [P, HD, P]) for j in range(2)]
        xres = [sb(f"xres{j}", [P, D]) for j in range(2)]
        hist = [sb(f"hist{j}", [RNN, ST * 2 * B]) for j in range(2)]
        hsb = [sb(f"hsb{j}", [SSM + 2, P]) for j in range(2)]
        rzb = sb("rzb", [RNN, 4 * B])
        h1 = sb("h1", [RNN, 2 * B], F16)
        h2 = sb("h2", [RNN, B], F16)
        nb = sb("nb", [RNN, 2 * B])
        ub = sb("ub", [RNN, 2 * B])
        mb = sb("mb", [RNN, 2 * B])
        sgb = sb("sgb", [SSM, B])
        arena = [sb(f"arena{i}", [P, 4096]) for i in range(3)]
        arena3 = sb("arena3", [P, 2048])

        def view(a, at, *dims):
            w = 1
            for d_ in dims:
                w *= d_
            ap = a[:, at:at + w]
            return ap if len(dims) == 1 else ap.rearrange("p (a b) -> p a b", a=dims[0])

        ctxb = view(arena[0], 0, HD, S)
        kT = view(arena[1], 0, HD, S)
        vt = view(arena[2], 0, B, D)
        ktm = view(arena3, 0, 4, 512)
        kp = [sb(f"kp{i}", [P, HD, S], F16) for i in range(2)]
        vp = [sb(f"vp{i}", [P, B, D], F16) for i in range(2)]
        sq = sb("sq", [P, 3 + HD * B])
        nrm = sb("nrm", [P, 4])
        inv = sb("inv", [P, 4])
        scl = sb("scl", [P, 3])
        und = sb("und", [P, 3])
        cq = sb("cq", [P, 2 * N])
        gxs = sb("gxs", [P, 2])
        s1a = sb("s1a", [P, D])
        s1b = sb("s1b", [P, D])
        st1 = sb("st1", [P, 6])
        mv1 = sb("mv1", [P, 2])
        ve1 = sb("ve1", [P, 1])
        rs1 = sb("rs1", [P, 1])
        x1 = [sb(f"x1_{j}", [P, D]) for j in range(2)]
        x1T = sb("x1T", [P, HD, 2 * P])
        x1R = sb("x1R", [P, HD, 2 * P])
        tm = sb("tm", [P, 4, 2 * P])
        wsq = tm[:, 0:HD, :]
        qr = sb("qr", [P, HD, 2 * P])
        qp = [sb(f"qp{i}", [P, HD, B, CH], F16) for i in range(2)]
        ret = sb("ret", [P, B, CH])
        rp = [sb(f"rp{i}", [P, B, CH], F16) for i in range(2)]
        sT = sb("sT", [P, HD, 2 * P])
        whr = tm[:, 2:4, :].rearrange("p a b -> p (a b)")[:, 0:3 * RNN]
        bzr = qr[:].rearrange("p a b -> p (a b)")[0:3 * 32, 0:RNN + D]
        st2 = sb("st2", [P, 2, HD, 6])
        mv2 = sb("mv2", [P, 2, 2])
        ve2 = sb("ve2", [P, 2])
        rs2 = sb("rs2", [P, 2])
        x2 = sb("x2", [P, TILES, D])
        lg = sb("lg", [P, TILES, E])
        mx = sb("mx", [P, TILES])
        pe_ = sb("pe_", [P, TILES, E])
        top = sb("top", [P, TILES, 8])
        topi = sb("topi", [P, TILES, 8], U32)
        topf = sb("topf", [P, TILES, 2])
        oh = [sb(f"oh{j}", [P, E, TILES]) for j in range(2)]
        msk = sb("msk", [P, E, TILES])
        cum = sb("cum", [P, E, TILES])
        pre = sb("pre", [P, E, TILES])
        suf = sb("suf", [P, E, TILES])
        rk = sb("rk", [P, E, TILES])
        ov = sb("ov", [P, E, TILES])
        slf = sb("slf", [P, 2, TILES])
        slu = sb("slu", [P, 2, TILES], U32)
        lo = sb("lo", [P, 2, TILES], F16)
        hi = sb("hi", [P, 2, TILES], F16)
        v1 = sb("v1", [P, E * CT])
        v2 = sb("v2", [P, E * CT])
        gix = sb("gix", [P, E * CT], U32)
        six = sb("six", [P, E * CT], U32)
        lo1 = vp[0][:].rearrange("p b d -> p (b d)").rearrange("p (n c) -> p n c", c=P)
        hi1, hit = (vp[1][:].rearrange("p b d -> p (b d)")[:, i * S:i * S + 2 * TILES * E * CT].rearrange("p (n c) -> p n c", c=E * CT)
                    for i in range(2))
        wt = sb("wt", [P, 2, TILES])
        wsum = sb("wsum", [P, TILES])
        wbuf = sb("wbuf", [P, 4 * HD * FF])
        w1t = [view(wbuf, 2 * j * HD * FF, HD, FF) for j in range(2)]
        w2t = [view(wbuf, (2 * j + 1) * HD * FF, FK, D) for j in range(2)]
        wparts = [[arena[1][:, i * 2048:(i + 1) * 2048].bitcast(F16) for i in range(2)],
                  [kp[i][:].rearrange("p h c -> p (h c)") for i in range(2)]]
        w1p = [[w[:, 0:HD * FF].rearrange("p (h f) -> p h f", h=HD) for w in ws] for ws in wparts]
        w2p = [[w[:, HD * FF:].rearrange("p (k d) -> p k d", k=FK) for w in ws] for ws in wparts]
        b1s = [sb(f"b1s{j}", [P, FK]) for j in range(2)]
        wsum2 = [sb(f"wsum2_{j}", [P, 2, 3]) for j in range(2)]
        wtot = [sb(f"wtot{j}", [P, 2]) for j in range(2)]
        wnrm = [sb(f"wnrm{j}", [P, 2]) for j in range(2)]
        winv = [sb(f"winv{j}", [P, 2]) for j in range(2)]
        wscl = [sb(f"wscl{j}", [P, 2]) for j in range(2)]
        wprod = [sb(f"wprod{j}", [P, 1]) for j in range(2)]
        wund = [sb(f"wund{j}", [P, 1]) for j in range(2)]
        wjunk = [arena3[:, 1536:2048].bitcast(BF16), arena[0][:, 3584:4096].bitcast(BF16)]
        hp = [arena[0][:, i * FK * CAP // 2:(i + 1) * FK * CAP // 2].bitcast(F16).rearrange("p (f c) -> p f c", f=FK) for i in range(2)]
        h32 = view(arena[2], 6 * D + 2 * HD * CAP, 4, CAP)
        yT = view(arena[0], FK * CAP, HD, CAP)

        def quarter(a1, a2, p):
            return a1[:, :, p * FF // 2:(p + 1) * FF // 2] if p < 2 else a2[:, (p - 2) * FK // 2:(p - 1) * FK // 2, :]

        yg = [view(wbuf, c * 4 * D, 4, D) for c in range(CHUNKS)]
        ca = [view(arena[1], k * D, D) for k in range(4)]
        cb = [view(arena[1], (4 + k) * D, D) for k in range(4)]
        ot = [view(arena[1], (8 + 2 * r) * D, 2, D) for r in range(3)]
        xe = [view(arena[2], j * 3 * D, 3, D) for j in range(2)]
        xp = [[arena[2][:, 6 * D + (2 * j + i) * HD * CAP // 2:6 * D + (2 * j + i + 1) * HD * CAP // 2].bitcast(F16)
               .rearrange("p (h c) -> p h c", h=HD) for i in range(2)] for j in range(2)]
        yt = [view(arena3, j * 3 * D, 3, D) for j in range(2)]
        zero = sb("zero", [P, D])
        st3 = sb("st3", [P, 2, 6])
        mv3 = sb("mv3", [P, CHUNKS, 2, 2])
        ve3 = sb("ve3", [P, 2])
        rs3 = sb("rs3", [P, CHUNKS, 2])
        ng3 = sb("ng3", [P, CHUNKS, 2])
        nm3 = sb("nm3", [P, CHUNKS, 2])

        bank = [ctx.enter_context(nc.psum_tensor(f"bank{i}", [P, 512], F32)) for i in range(8)]
        RZ = bank[0:2]
        NS = bank[2:4]
        FB = bank[4]
        QB = bank[5]
        TB = bank[6]
        SC = bank[7]
        NW = 2 * ST * B

        names = ("w_hh w_k w_v w_rec w_fin w_att w_late c_load ctx_load0 ctx_load1 ctx_load2 ctx_load3 xin0 xin1 xfin0 xfin1 xres0 xres1 "
                 "init_v init_p wsplit bsplit k_mm k_mul k_rot v_mm v_copy wsqs csqs nsum cguard nrm_done inv_done scl_done gcent "
                 "kv_hi kv_lo "
                 "in_done rz_ready ns_ready r_ready sg_ready npre_ready n_ready zh_ready h1_done hist_done h2_done hs_done "
                 "fin_ready gx_ready fuse_a fuse_b stat1 var1 eps1 rstd1 x1_ready x1tr_ready x1T_ready x1R_ready "
                 "q_ready qmul_ready qr_ready qh_ready ql_ready sc_ready ret_ready rh_ready rl_ready pv_ready res_ready back_ready "
                 "stat2 var2 eps2 rstd2 lg_ready x2_ready rt ract rmm "
                 "zrow x2_st hi_ready hi1_ready hit_ready ws_ready ix_ready imm imm_read gix_ready xe0 xe1 w1l0 w1l1 w2l0 w2l1 xtr_ready xhi_ready xlo_ready h_mm h32_ready h_hi h_lo y_mm wsq_ready wnsum wnrm_ready winv_ready wscl_ready w_hi w_lo yT_ready ytr_ready yt_ready yst0 yst1 "
                 "yl0 yl1 yl2 yl3 yl4 yl5 yl6 yl7 c_w c_even c_odd c_b stat3 var3 eps3 neg3 pow3 rstd3 o_ready ost0 ost1 ost2")
        q = {n: sem(n) for n in names.split()}

        def ev(ap):
            return ap.rearrange("p (c two) -> p c two", two=2)[:, :, 0]

        def od(ap):
            return ap.rearrange("p (c two) -> p c two", two=2)[:, :, 1]

        def k_products(i):
            return ktm if i % 2 == 0 else x2[:].rearrange("p k d -> p (k d)")[:, 0:2048].rearrange("p (a b) -> p a b", a=4)

        def v_bank(b):
            return TB if b < V_EARLY else (QB, SC)[b % 2]

        def h_of(j, s):
            return od(hist[j][:, s * 2 * B:(s + 1) * 2 * B])

        def prev(j, s):
            return (j, s - 1) if s else (1 - j, ST - 1)

        def halves(bk):
            return bk[:, 0:2 * (P + E)].rearrange("p (h c) -> p h c", h=2)[:, :, 0:P]

        xT_d = xT.rearrange("(h p) c -> p h c", p=P)
        ctxT_d = ctxT.rearrange("(h p) c -> p h c", p=P)
        w1_d = w1.rearrange("e (h p) f -> p e h f", p=P)
        w2_d = w2.rearrange("e (k p) d -> p e k d", p=P)

        block = ctx.enter_context(nc.Block())

        @block.sync
        def _(sp):
            def load_in(k, j, first=False):
                if not first:
                    sp.wait_ge(q["in_done"], k - 1)
                sp.dma_start(xin_t[j][:], xT_d[:, :, bass.ts(k, P)]).then_inc(q[f"xin{j}"], 16)

            def load_fin(k, j, first=False):
                if not first:
                    sp.wait_ge(q["fuse_b"], k - 1)
                sp.dma_start(xfin_t[j][:], xT_d[:, :, bass.ts(k, P)]).then_inc(q[f"xfin{j}"], 16)
                sp.dma_start(xres[j][:], xtok[bass.ts(k, P), :]).then_inc(q[f"xres{j}"], 16)

            load_in(0, 0, True)
            sp.dma_start(whh[:], W_hhT).then_inc(q["w_hh"], 16)
            sp.dma_start(bz[:], b_rows).then_inc(q["w_hh"], 16)
            sp.dma_start(wih[:], W_ihT.rearrange("(h p) r -> p h r", p=P)).then_inc(q["w_rec"], 16)
            sp.dma_start(bst[:], bsel).then_inc(q["w_rec"], 16)
            sp.dma_start(at_w[:], AbE).then_inc(q["w_rec"], 16)
            sp.dma_start(bw[:], BwT.rearrange("(h p) r -> p h r", p=P)).then_inc(q["w_rec"], 16)
            load_in(1, 1, True)
            sp.dma_start(wk[:], WkT.rearrange("(h p) r -> p h r", p=P)).then_inc(q["w_k"], 16)
            for i in range(4):
                sp.dma_start(ctxb[:, :, bass.ts(i, 512)], ctxT_d[:, :, bass.ts(i, 512)]).then_inc(q[f"ctx_load{i}"], 16)
                if i == 0:
                    sp.dma_start(wv[:], WvT.rearrange("(h p) r -> p h r", p=P)).then_inc(q["w_v"], 16)
                    sp.dma_start(cst[:], consts).then_inc(q["c_load"], 16)
                if i == 1:
                    sp.dma_start(dw[:], DwT.rearrange("(h p) r -> p h r", p=P)).then_inc(q["w_fin"], 16)
                    sp.dma_start(pw[:], projT).then_inc(q["w_fin"], 16)
                    sp.dma_start(cwe[:], CwE).then_inc(q["w_fin"], 16)
                    sp.dma_start(gw[:], gateT.rearrange("(h p) r -> p h r", p=P)).then_inc(q["w_fin"], 16)
                    sp.dma_start(gb[:], gate_b.to_broadcast([P, 2])).then_inc(q["w_fin"], 16)
                    load_fin(0, 0, True)
            sp.dma_start(wq[:], WqT.rearrange("(h p) r -> p h r", p=P)).then_inc(q["w_att"], 16)
            sp.dma_start(rgw[:], rgwT.rearrange("(h p) r -> p h r", p=P)).then_inc(q["w_late"], 16)
            sp.dma_start(iota16[:], iota).then_inc(q["w_late"], 16)
            sp.dma_start(rgbt[:], rgb.to_broadcast([P, E])).then_inc(q["w_late"], 16)
            load_fin(1, 1, True)
            sp.dma_start(b1t[:], b1).then_inc(q["w_late"], 16)
            sp.dma_start(b2t[:], b2).then_inc(q["w_late"], 16)
            for e in range(2):
                sp.dma_start(w1t[e], w1_d[:, e]).then_inc(q[f"w1l{e}"], 16)
                sp.dma_start(w2t[e], w2_d[:, e]).then_inc(q[f"w2l{e}"], 16)
            def store_x2(c):
                sp.wait_ge(q["x2_ready"], 2 * c + 3)
                sp.dma_start(x2_d[bass.ds(2 * c * P, 2 * P), :].rearrange("(k p) d -> p k d", p=P), x2[:, bass.ds(2 * c, 2), :]).then_inc(q["x2_st"], 16)

            def inputs(g):
                load_in(2 * g + 2, 0)
                load_fin(2 * g + 2, 0)
                load_in(2 * g + 3, 1)
                load_fin(2 * g + 3, 1)

            inputs(0)
            inputs(1)
            with sp.Fori(2, CHUNKS - 1) as g:
                inputs(g)
                store_x2(g - 2)
            for c in range(CHUNKS - 3, CHUNKS):
                store_x2(c)
            with sp.Fori(0, E // 2 - 1) as i:
                for j in range(2):
                    e = 2 * i + j
                    sp.wait_ge(q["w_lo"], 4 * e + 2)
                    sp.dma_start(w1t[j], w1_d[:, e + 2]).then_inc(q[f"w1l{j}"], 16)
                    sp.wait_ge(q["w_lo"], 4 * e + 4)
                    sp.dma_start(w2t[j], w2_d[:, e + 2]).then_inc(q[f"w2l{j}"], 16)
            for j in range(2):
                sp.wait_ge(q[f"yst{j}"], 16 * CT * (E // 2))
            y_v = ybuf.rearrange("(j k p) d -> p j k d", j=2, p=P)
            for c in range(CHUNKS):
                for j in range(2):
                    sp.dma_start(yg[c][:, 2 * j:2 * j + 2, :], y_v[:, j, 2 * c:2 * c + 2, :]).then_inc(q[f"yl{c}"], 16)
            for c in range(CHUNKS):
                sp.wait_ge(q["o_ready"], c + 1)
                sp.dma_start(out[2 * c * P:2 * (c + 1) * P, :].rearrange("(k p) d -> p k d", p=P), ot[c % 3]).then_inc(q[f"ost{c % 3}"], 16)
            for r in range(3):
                sp.wait_ge(q[f"ost{r}"], 16 * len(range(r, CHUNKS, 3)))

        @block.gpsimd
        def _(pool):
            def rot_k(i):
                pool.wait_ge(q["k_mul"], 4 * (i + 1))
                t = k_products(i)
                pool.tensor_tensor(kT[:, 0, bass.ts(i, 512)], t[:, 0, :], t[:, 1, :], ALU.subtract).then_inc(q["k_rot"], 1)
                pool.tensor_tensor(kT[:, 1, bass.ts(i, 512)], t[:, 2, :], t[:, 3, :], ALU.add).then_inc(q["k_rot"], 1)

            def rstd(var, eps, out_, ready, done, scratch, n):
                pool.wait_ge(var, n)
                pool.tensor_tensor(scratch[0], scratch[1], epst[:, 0:scratch[0].shape[-1]], ALU.add).then_inc(eps, 1)
                pool.wait_ge(eps, n)
                pool.tensor_tensor(out_, scratch[0], mhalf[:, 0:scratch[0].shape[-1]], ALU.pow).then_inc(done, 1)

            def rstd_1(n):
                rstd(q["var1"], q["eps1"], rs1[:], None, q["rstd1"], (ve1[:], mv1[:, 1:2]), n + 1)

            def rot_q(c):
                for h, op in enumerate((ALU.subtract, ALU.add)):
                    pool.wait_ge(q["qmul_ready"], 2 * c + h + 1)
                    pool.tensor_tensor(qr[:, h, :], tm[:, 2 * h, :], tm[:, 2 * h + 1, :], op).then_inc(q["qr_ready"], 1)

            def q_low(c):
                for h in range(HD):
                    pool.wait_ge(q["qh_ready"], 2 * c + h + 1)
                    pool.tensor_tensor(qp[1][:, h].rearrange("p b t -> p t b"), qr[:, h, :].rearrange("p (t b) -> p t b", b=B),
                                       qp[0][:, h].rearrange("p b t -> p t b"), ALU.subtract).then_inc(q["ql_ready"], 1)

            def ret_low(c):
                pool.wait_ge(q["rh_ready"], c + 1)
                pool.tensor_tensor(rp[1][:], ret[:], rp[0][:], ALU.subtract).then_inc(q["rl_ready"], 1)

            def rstd_2(c):
                rstd(q["var2"], q["eps2"], rs2[:], None, q["rstd2"], (ve2[:], mv2[:, :, 1]), c + 1)

            def iteration(g, A, M):
                if A:
                    rstd_1(2 * g - 2)
                    if not M:
                        rot_k(3)
                    rstd_1(2 * g - 1)
                if A and not M:
                    for i in range(8):
                        pool.dma_start(ybuf[i * 4 * P:(i + 1) * 4 * P, :].rearrange("(k p) d -> p k d", p=P),
                                       zero[:].unsqueeze(1).to_broadcast([P, 4, D])).then_inc(q["zrow"], 16)
                if M:
                    ret_low(g - 2)
                if A:
                    rot_q(g - 1)
                if M:
                    rstd_2(g - 2)
                if A:
                    q_low(g - 1)

            pool.memset(ones[:], 1.0).then_inc(q["init_p"], 1)
            pool.memset(mhalf[:], -0.5).then_inc(q["init_p"], 1)
            pool.memset(epst[:], EPS).then_inc(q["init_p"], 1)
            pool.wait_ge(q["init_v"], INIT_V)
            pool.wait_ge(q["init_p"], INIT_P)
            for i in range(3):
                rot_k(i)
            iteration(0, False, False)
            pool.wait_ge(q["nrm_done"], 1)
            pool.tensor_tensor(inv[:], nrm[:], mhalf[:], ALU.pow).then_inc(q["inv_done"], 1)
            iteration(1, True, False)
            with pool.Fori(2, CHUNKS) as g:
                iteration(g, True, True)
            rstd_1(TILES - 2)
            rstd_1(TILES - 1)
            ret_low(CHUNKS - 2)
            rot_q(CHUNKS - 1)
            rstd_2(CHUNKS - 2)
            rstd_2(CHUNKS - 1)
            for j in range(2):
                w = slice(j * TILES, (j + 1) * TILES)
                pool.wait_ge(q["hi1_ready"], j + 1)
                pool.tensor_tensor(hit[:, w, :], hi1[:, w, :], con("tok").unsqueeze(2).to_broadcast([P, TILES, E * CT]),
                                   ALU.mult).then_inc(q["hit_ready"], 1)

            def norms(e):
                pool.wait_ge(q["wnrm_ready"], 2 * e + 2)
                pool.tensor_tensor(winv[e % 2][:], wnrm[e % 2][:], mhalf[:, 0:2], ALU.pow).then_inc(q["winv_ready"], 1)

            norms(0)
            pool.wait_ge(q["x2_st"], 16 * CHUNKS)
            pool.wait_ge(q["gix_ready"], 1)

            def slots(e):
                for c in range(CT):
                    yield c, min(P, CAP - c * P), slice(e * CT + c, e * CT + c + 1)

            def gather(e):
                if e >= 2:
                    pool.wait_ge(q["xtr_ready"], e - 1)
                for c, m, col in slots(e):
                    pool.indirect_dma_start(
                        xe[e % 2][0:m, c, :], None, x2_d[:, :], bass.IndirectOffsetOnAxis(ap=gix[0:m, col], axis=0),
                        bounds_check=S - 1, oob_is_err=False).then_inc(q[f"xe{e % 2}"], 16)

            def scatter(e):
                pool.wait_ge(q["yt_ready"], 2 * e + 2)
                for c, m, col in slots(e):
                    pool.indirect_dma_start(
                        ybuf[:, :], bass.IndirectOffsetOnAxis(ap=six[0:m, col], axis=0), yt[e % 2][0:m, c, :], None,
                        bounds_check=2 * S - 1, oob_is_err=False).then_inc(q[f"yst{e % 2}"], 16)

            gather(0)
            gather(1)
            pool.wait_ge(q["gix_ready"], 2)
            pool.wait_ge(q["zrow"], 16 * 8)
            for e in range(E):
                if e + 1 < E:
                    norms(e + 1)
                if e + 2 < E:
                    gather(e + 2)
                if e >= 1:
                    scatter(e - 1)
            scatter(E - 1)

            def first_choice(c):
                pool.wait_ge(q["c_w"], c + 1)
                if c >= 2:
                    pool.wait_ge(q["c_b"], 2 * c - 3)
                pool.tensor_tensor(ca[2 * c % 4], yg[c][:, 0, :], x2[:, 2 * c, :], ALU.add).then_inc(q["c_even"], 1)

            def rstd_3(c):
                pool.wait_ge(q["var3"], c + 1)
                pool.tensor_tensor(ng3[:, c, :], zero[:, 0:2], mv3[:, c, :, 0], ALU.subtract).then_inc(q["neg3"], 1)
                pool.tensor_tensor(ve3[:], mv3[:, c, :, 1], epst[:, 0:2], ALU.add).then_inc(q["eps3"], 1)
                pool.wait_ge(q["eps3"], c + 1)
                pool.tensor_tensor(rs3[:, c, :], ve3[:], mhalf[:, 0:2], ALU.pow).then_inc(q["pow3"], 1)
                pool.wait_ge(q["neg3"], c + 1)
                pool.wait_ge(q["pow3"], c + 1)
                pool.tensor_tensor(nm3[:, c, :], ng3[:, c, :], rs3[:, c, :], ALU.mult).then_inc(q["rstd3"], 1)

            first_choice(0)
            for c in range(CHUNKS):
                if c + 1 < CHUNKS:
                    first_choice(c + 1)
                rstd_3(c)

        @block.scalar
        def _(act):
            def rec(g, j, s):
                t = CH * g + ST * j + s
                act.wait_ge(q["rz_ready"], t + 1)
                nc.scalar.activation(od(rzb[:]), RZ[j][:, s * 2 * B:(s + 1) * 2 * B], ACT.Sigmoid).then_inc(q["r_ready"], 1)
                nc.scalar.activation(sgb[:], RZ[j][0:SSM, NW + s * B:NW + (s + 1) * B], ACT.Sigmoid).then_inc(q["sg_ready"], 1)
                act.wait_ge(q["npre_ready"], t + 1)
                nc.scalar.activation(od(nb[:]), od(ub[:]), ACT.Tanh).then_inc(q["n_ready"], 1)

            def gates(n):
                act.wait_ge(q["fin_ready"], n + 1)
                for i in range(2):
                    nc.scalar.activation(gxs[:, i:i + 1], TB[:, i:i + 1], ACT.Sigmoid, bias=gb[:, i:i + 1]).then_inc(q["gx_ready"], 1)

            def x1T_copy(c):
                act.wait_ge(q["x1tr_ready"], c + 1)
                for h in range(HD):
                    nc.scalar.copy(x1T[:, h, :], TB[:, h * 256:(h + 1) * 256]).then_inc(q["x1T_ready"], 1)

            def x1R_copy(c, first=False):
                act.wait_ge(q["x1T_ready"], 2 * c + 2)
                if not first:
                    act.wait_ge(q["res_ready"], 2 * c)
                nc.scalar.copy(x1R[:], x1T[:]).then_inc(q["x1R_ready"], 1)

            def q_high(c):
                for h in range(HD):
                    act.wait_ge(q["qr_ready"], 2 * c + h + 1)
                    nc.scalar.copy(qp[0][:, h].rearrange("p b t -> p t b"),
                                   qr[:, h, :].rearrange("p (t b) -> p t b", b=B)).then_inc(q["qh_ready"], 1)

            def ret_high(c):
                act.wait_ge(q["ret_ready"], c + 1)
                nc.scalar.copy(rp[0][:], ret[:]).then_inc(q["rh_ready"], 1)

            def w_square(i):
                if i == 0:
                    act.wait_ge(q["w_k"], 16)
                    act.wait_ge(q["w_v"], 16)
                    act.wait_ge(q["w_att"], 16)
                    act.wait_ge(q["csqs"], HD * B)
                else:
                    act.wait_ge(q["wsqs"], i)
                nc.scalar.activation(wsq, (wq, wk, wv)[i][:], ACT.Square, accum_out=sq[:, i:i + 1]).then_inc(q["wsqs"], 1)

            def v_out(b):
                act.wait_ge(q["v_mm"], b + 1)
                nc.scalar.copy(vt[:, b, :], v_bank(b)[:, 0:D]).then_inc(q["v_copy"], 1)

            def c_square(b):
                act.wait_ge(q[f"ctx_load{b // 4}"], 16)
                for h in range(HD):
                    if b > 0:
                        act.wait_ge(q["csqs"], 2 * b - 1 + h)
                    nc.scalar.activation(tm[:, h, 0:N], ctxb[:, h, b * N:(b + 1) * N], ACT.Square,
                                         accum_out=sq[:, 3 + h * B + b:4 + h * B + b]).then_inc(q["csqs"], 1)

            def high(piece):
                i = int(piece[1:])
                if piece[0] == "k":
                    act.wait_ge(q["k_rot"], i + 1)
                    dst, src, k = kp[0][:, i % 2, bass.ts(i // 2, 512)], kT[:, i % 2, bass.ts(i // 2, 512)], 1
                else:
                    act.wait_ge(q["v_copy"], 2 * i + 2)
                    dst, src, k = vp[0][:, 2 * i:2 * i + 2, :], vt[:, 2 * i:2 * i + 2, :], 2
                nc.scalar.activation(dst, src, ACT.Copy, scale=scl[:, k:k + 1]).then_inc(q["kv_hi"], 1)

            def iteration(g, A, M):
                for s in range(CH):
                    rec(g, s // ST, s % ST)
                    if A and s == 1:
                        gates(2 * g - 1)
                    if M and s == 6:
                        ret_high(g - 2)
                    if A and s == 7:
                        x1T_copy(g - 1)
                    if A and s == 11:
                        x1R_copy(g - 1, not M)
                    if s == 13:
                        gates(2 * g)
                    if A and s == 14:
                        q_high(g - 1)
                    if not A:
                        if s in V_FIRST:
                            v_out(V_FIRST.index(s))
                        if 2 <= s < 10:
                            c_square(2 * s - 4)
                            c_square(2 * s - 3)
                        if 10 <= s < 13:
                            w_square(s - 10)
                    elif not M:
                        if s in V_SLOTS:
                            for b in range(2):
                                v_out(V_EARLY + 2 * V_SLOTS.index(s) + b)
                        if s == 1:
                            act.wait_ge(q["scl_done"], 1)
                        for n, piece in enumerate(PIECES):
                            if HI_STEP[n] == s:
                                high(piece)

            act.wait_ge(q["init_v"], INIT_V)
            act.wait_ge(q["init_p"], INIT_P)
            act.wait_ge(q["w_rec"], 16 * 4)
            iteration(0, False, False)
            iteration(1, True, False)
            with act.Fori(2, CHUNKS) as g:
                iteration(g, True, True)
            gates(TILES - 1)
            ret_high(CHUNKS - 2)
            x1T_copy(CHUNKS - 1)

            def squares(e, j, i):
                for p in range(4):
                    if p % 2 == 0:
                        act.wait_ge(q[f"w{p // 2 + 1}l{j}"], 16 * i + 16)
                    src = quarter(w1t[j], w2t[j], p)
                    if p > 1 or not (isinstance(e, int) and e == 0):
                        act.wait_ge(q["wsq_ready"], 5 * e + max(p - 1, 0))
                    nc.scalar.activation(wjunk[p % 2].rearrange("p (a b) -> p a b", a=src.shape[1]), src, ACT.Square,
                                         accum_out=wsum2[j][:, p // 2, p % 2:p % 2 + 1]).then_inc(q["wsq_ready"], 1)
                act.wait_ge(q["wsq_ready"], 5 * e + 3)
                nc.scalar.activation(wjunk[0][:, 0:FK], b1t[:, bass.ds(e * FK, FK)], ACT.Square,
                                     accum_out=wsum2[j][:, 0, 2:3]).then_inc(q["wsq_ready"], 1)

            def w_high(e, j, p):
                if p == 0:
                    act.wait_ge(q["wscl_ready"], 4 * e + 1)
                nc.scalar.activation(quarter(w1p[j][0], w2p[j][0], p), quarter(w1t[j], w2t[j], p), ACT.Copy,
                                     scale=wscl[j][:, p // 2:p // 2 + 1]).then_inc(q["w_hi"], 1)

            def exponentials(part, a, b):
                act.wait_ge(q["rt"], RT_EXP[part])
                nc.scalar.activation(pe_[:, a:b, :], pe_[:, a:b, :], ACT.Exp).then_inc(q["ract"], 1)

            exponentials(0, 0, TILES - 4)
            q_high(CHUNKS - 1)
            x1R_copy(CHUNKS - 1)
            ret_high(CHUNKS - 1)
            act.wait_ge(q["w_late"], 80)
            squares(0, 0, 0)
            exponentials(1, TILES - 4, TILES)
            squares(1, 1, 0)

            def rows_high(e, j):
                act.wait_ge(q["xtr_ready"], e + 1)
                for h in range(HD):
                    nc.scalar.copy(xp[j][0][:, h, :], bank[h][:, 0:CAP]).then_inc(q["xhi_ready"], 1)

            def hidden(e, j, f):
                act.wait_ge(q["h_mm"], FK * e + f + 1)
                if f == 0:
                    act.wait_ge(q["wscl_ready"], 4 * e + 4)
                if f >= 4:
                    act.wait_ge(q["h_lo"], FK * e + f - 3)
                nc.scalar.activation(h32[:, f % 4, :], bank[2 + f % 4][:, 0:CAP], ACT.Relu,
                                     bias=b1s[j][:, f:f + 1]).then_inc(q["h32_ready"], 1)

            def expert(i, j):
                e = 2 * i + j
                last = isinstance(e, int) and e == E - 1
                for f in range(FK):
                    hidden(e, j, f)
                    if f == 5 and not last:
                        rows_high(e + 1, 1 - j)
                    if f >= 6 and not last:
                        w_high(e + 1, 1 - j, f - 6)
                if not last:
                    w_high(e + 1, 1 - j, 2)
                    w_high(e + 1, 1 - j, 3)
                if not (isinstance(e, int) and e >= E - 2):
                    squares(e + 2, j, i + 1)
                act.wait_ge(q["y_mm"], e + 1)
                for h in range(HD):
                    nc.scalar.activation(yT[:, h, :], bank[6 + h][:, 0:CAP], ACT.Identity, scale=wund[j][:],
                                         bias=b2t[:, bass.ds(e * HD + h, 1)]).then_inc(q["yT_ready"], 1)

            for p in range(4):
                w_high(0, 0, p)
            rows_high(0, 0)
            with act.Fori(0, E // 2 - 1) as i:
                for j in range(2):
                    expert(i, j)
            expert(E // 2 - 1, 0)
            expert(E // 2 - 1, 1)

            def weighted(c):
                act.wait_ge(q[f"yl{c}"], 32)
                nc.scalar.activation(yg[c][:, 0, :], yg[c][:, 0, :], ACT.Copy, scale=wt[:, 0, 2 * c:2 * c + 1]).then_inc(q["c_w"], 1)

            weighted(0)
            weighted(1)
            for c in range(CHUNKS):
                if c + 2 < CHUNKS:
                    weighted(c + 2)
                act.wait_ge(q["rstd3"], c + 1)
                if c >= 3:
                    act.wait_ge(q[f"ost{c % 3}"], 16 * (c // 3))
                for i in range(2):
                    last = nc.scalar.activation(ot[c % 3][:, i, :], cb[(2 * c + i) % 4], ACT.Identity,
                                                bias=nm3[:, c, i:i + 1], scale=rs3[:, c, i:i + 1])
                last.then_inc(q["o_ready"], 1)

        @block.tensor
        def _(pe):
            def mm(out_, lhsT, rhs, start=True, stop=True):
                return nc.tensor.matmul(out_, lhsT, rhs, start=start, stop=stop, skip_group_check=True)

            def in_a(n, j):
                pe.wait_ge(q[f"xin{j}"], 16 * ((n - j) // 2 + 1) if isinstance(n, int) else 8 * n + (16 - 8 * j))
                mm(RZ[j][:, 0:NW], bzq[:, 0:RNN], bst[:, 0:NW], True, False)
                mm(NS[j][:, 0:NW], bzq[:, 0:RNN], bst[:, NW:2 * NW], True, False)
                in_half(j, 0)

            def in_half(j, h):
                for i in range(3):
                    if i < 2:
                        o = RZ[j][:, 0:NW].rearrange("p (s i b) -> p i s b", i=2, b=B)[:, i]
                    else:
                        o = NS[j][:, 0:NW].rearrange("p (s b two) -> p two s b", two=2, b=B)[:, 1]
                    mm(o, wih[:, h, i * RNN:(i + 1) * RNN], xin_t[j][:, h, :].rearrange("p (s b) -> p s b", b=B), False, False)
                return mm(RZ[j][0:SSM, NW:NW + P], bw[:, h, :], xin_t[j][:, h, :], False, False)

            def in_b(j):
                in_half(j, 1).then_inc(q["in_done"], 1)

            def rec(g, j, s):
                t = CH * g + ST * j + s
                pj, ps = prev(j, s)
                rz = [RZ[j][:, s * 32 + i * 16:s * 32 + (i + 1) * 16] for i in range(2)]
                hn = ev(NS[j][:, s * 32:s * 32 + 32])
                def parts(i, h, n):
                    for k in range(n):
                        last = mm((rz + [hn])[i], whp[k][:, i * RNN:(i + 1) * RNN], h, False, False)
                    return last

                pe.wait_ge(q["hs_done"], t + 1)
                mm(RZ[j][0:SSM, NW + s * B:NW + (s + 1) * B], at_w[:], hsb[pj][:, ps * B:(ps + 1) * B], False, False)
                pe.wait_ge(q["h1_done"], t + 1)
                parts(0, od(h1[:]), 3)
                parts(1, od(h1[:]), 3)
                parts(2, od(h1[:]), 3)
                pe.wait_ge(q["h2_done"], t + 1)
                parts(0, h2[:], 2)
                parts(1, h2[:], 2).then_inc(q["rz_ready"], 1)
                parts(2, h2[:], 2).then_inc(q["ns_ready"], 1)

            def fin_a(n, j):
                pe.wait_ge(q[f"xfin{j}"], 16 * ((n - j) // 2 + 1) if isinstance(n, int) else 8 * n + (16 - 8 * j))
                if not isinstance(n, int) or n >= 1:
                    pe.wait_ge(q["fuse_b"], n)
                mm(FB[:, 0:D], hsb[j][:], cwe[:], True, False)
                mm(FB[:, 0:D], xfin_t[j][:, 0, :], dw[:, 0, :], False, False)
                mm(FB[:, D:2 * D], ones16[:], bzq[:, RNN:RNN + D], False, False)

            def fin_b(n, j):
                mm(FB[:, 0:D], xfin_t[j][:, 1, :], dw[:, 1, :], False, True)
                mm(FB[:, D:2 * D], od(hist[j][:]), pw[:], False, True)
                for h in range(HD):
                    last = mm(TB[:, 0:2], xfin_t[j][:, h, :], gw[:, h, :], h == 0, h == 1)
                last.then_inc(q["fin_ready"], 1)

            def x1_tr(c):
                pe.wait_ge(q["x1_ready"], 2 * c + 2)
                for j in range(2):
                    for h in range(HD):
                        last = nc.tensor.transpose(TB[:, h * 256 + j * P:h * 256 + (j + 1) * P], x1[j][:, h * P:(h + 1) * P], ident)
                last.then_inc(q["x1tr_ready"], 1)

            def q_proj(c, o):
                if o == 0:
                    pe.wait_ge(q["x1T_ready"], 2 * c + 2)
                for h in range(HD):
                    last = mm(TB[:, o * 256:(o + 1) * 256], wq[:, h, o * P:(o + 1) * P], x1T[:, h, :], h == 0, h == 1)
                if o == 1:
                    last.then_inc(q["q_ready"], 1)

            def scores(c, part, drain=False):
                bk = NS[0] if drain else SC
                if part == 0 and not drain:
                    pe.wait_ge(q["x2_ready"], 2 * c + 1)
                if part == 0:
                    pe.wait_ge(q["ql_ready"], 2 * c + 2)
                for b in range(part * B // 2, (part + 1) * B // 2):
                    for i, (x, y, h) in enumerate((x, y, h) for x, y in PAIRS for h in range(HD)):
                        last = mm(bk[:, b * CH:(b + 1) * CH], kp[x][:, h, b * N:(b + 1) * N], qp[y][:, h, b, :], i == 0, i == 5)
                if part == 1:
                    last.then_inc(q["sc_ready"], 1)

            def mix(c, part, drain=False):
                bk = NS[1] if drain else QB
                if part == 0:
                    pe.wait_ge(q["rl_ready"], c + 1)
                for b in range(part * B // 2, (part + 1) * B // 2):
                    for h in range(HD):
                        for i, (x, y) in enumerate(PAIRS):
                            last = mm(bk[:, h * 256:(h + 1) * 256].rearrange("p (t b) -> p t b", b=B)[:, :, b],
                                      vp[x][:, b, h * P:(h + 1) * P], rp[y][:, b, :], i == 0, i == 2)
                if part == 1:
                    last.then_inc(q["pv_ready"], 1)

            def back(c):
                pe.wait_ge(q["res_ready"], 2 * c + 2)
                for j, bk in enumerate((QB, SC)):
                    for h in range(HD):
                        last = mm(bk[:, h * P:h * P + P + E], sT[:, h, j * P:(j + 1) * P], rgi[:, h, :], h == 0, h == 1)
                last.then_inc(q["back_ready"], 1)

            def k_mm(u):
                i, o = u // 2, u % 2
                pe.wait_ge(q[f"ctx_load{i}"], 16)
                if i >= 1:
                    pe.wait_ge(q["k_mul"], 4 * i - 2 + 2 * o)
                for h in range(HD):
                    last = mm((QB, SC)[o][:], wk[:, h, o * P:(o + 1) * P], ctxb[:, h, bass.ts(i, 512)], h == 0, h == 1)
                last.then_inc(q["k_mm"], 1)

            def v_mm(b):
                if b == V_EARLY:
                    pe.wait_ge(q["k_mul"], 14)
                elif b == V_EARLY + 1:
                    pe.wait_ge(q["k_mul"], 16)
                elif b > 0:
                    pe.wait_ge(q["v_copy"], b if b < V_EARLY else b - 1)
                for h in range(HD):
                    last = mm(v_bank(b)[:, 0:D], ctxb[:, h, b * N:(b + 1) * N], wv[:, h, :], h == 0, h == 1)
                last.then_inc(q["v_mm"], 1)

            def sums():
                pe.wait_ge(q["wsqs"], 3)
                pe.wait_ge(q["csqs"], HD * B)
                pe.wait_ge(q["w_late"], 80)
                pe.wait_ge(q["gx_ready"], 2)
                mm(TB[:, 64:67], ones[:], sq[:, 0:3])
                for h in range(HD):
                    mm(TB[:, 96:96 + B], ones[:], sq[:, 3 + h * B:3 + (h + 1) * B], h == 0, h == 1)
                for h in range(HD):
                    last = mm(TB[:, 72:72 + E], ones[:], rgw[:, h, :], h == 0, h == 1)
                last.then_inc(q["nsum"], 1)

            def iteration(g, A, M, has_next):
                for s in range(CH):
                    rec(g, s // ST, s % ST)
                    if A and s == 0:
                        fin_a(2 * g - 1, 1)
                    if A and s == 1:
                        pe.wait_ge(q["gx_ready"], 4 * g - 2)
                        if not M:
                            pe.wait_ge(q["gcent"], 1)
                            pe.wait_ge(q["nrm_done"], 1)
                        fin_b(2 * g - 1, 1)
                    if M and s in (2, 4):
                        scores(g - 2, (s - 2) // 2)
                    if s == 3:
                        in_a(2 * g + 1, 1)
                    if s == 5:
                        in_b(1)
                    if A and s == 6:
                        pe.wait_ge(q["gx_ready"], 4 * g)
                        x1_tr(g - 1)
                    if M and s in (7, 9):
                        mix(g - 2, (s - 7) // 2)
                    if A and s in (8, 10):
                        q_proj(g - 1, (s - 8) // 2)
                    if M and s == 11:
                        back(g - 2)
                    if s == 12:
                        if not A:
                            pe.wait_ge(q["w_fin"], 16 * 5)
                        fin_a(2 * g, 0)
                    if s == 13:
                        if A:
                            pe.wait_ge(q["qmul_ready"], 2 * g)
                        else:
                            pe.wait_ge(q["v_copy"], V_EARLY)
                        fin_b(2 * g, 0)
                    if has_next and s == 14:
                        in_a(2 * g + 2, 0)
                    if has_next and s == 15:
                        in_b(0)
                    if not A:
                        if s == 0:
                            pe.wait_ge(q["w_k"], 16)
                        if s == 1:
                            pe.wait_ge(q["w_v"], 16)
                        if s % 2 == 0:
                            k_mm(s // 2)
                        if s in V_FIRST:
                            v_mm(V_FIRST.index(s))
                        if s == 15:
                            sums()
                    elif not M:
                        if s in V_SLOTS:
                            for b in range(2):
                                v_mm(V_EARLY + 2 * V_SLOTS.index(s) + b)
                        if s == 15:
                            pe.wait_ge(q["kv_lo"], 16)

            pe.wait_ge(q["w_rec"], 16 * 4)
            pe.wait_ge(q["init_v"], INIT_V)
            pe.wait_ge(q["init_p"], INIT_P)
            pe.wait_ge(q["bsplit"], 4)
            in_a(0, 0)
            in_b(0)
            pe.wait_ge(q["wsplit"], 4)
            iteration(0, False, False, True)
            iteration(1, True, False, True)
            with pe.Fori(2, CHUNKS - 1) as g:
                iteration(g, True, True, True)
            iteration(CHUNKS - 1, True, True, False)
            c = CHUNKS - 1
            pe.wait_ge(q["hs_done"], N + 1)
            pe.wait_ge(q["h2_done"], N + 1)
            fin_a(TILES - 1, 1)
            pe.wait_ge(q["gx_ready"], 2 * TILES - 2)
            fin_b(TILES - 1, 1)
            scores(c - 1, 0)
            scores(c - 1, 1)
            pe.wait_ge(q["gx_ready"], 2 * TILES)
            x1_tr(c)
            mix(c - 1, 0)
            q_proj(c, 0)
            q_proj(c, 1)
            mix(c - 1, 1)
            scores(c, 0, True)
            scores(c, 1, True)
            back(c - 1)
            mix(c, 0, True)
            mix(c, 1, True)
            pe.wait_ge(q["x2_ready"], 2 * c + 1)
            back(c)
            pe.wait_ge(q["rt"], RT_CUM)
            flat = [x[:].rearrange("p e k -> p (e k)") for x in (pre, msk, suf)]
            for i, name in enumerate(("le", "diag", "lt")):
                last = mm(bank[0][:, 0:E * TILES], con(name), flat[i], i == 0, i == 2)
            last.then_inc(q["rmm"], 1)

            def norms(e, j, bk=1):
                pe.wait_ge(q["wsq_ready"], 5 * e + 5)
                mm(bank[bk][:, 384:390], ones[:], wsum2[j][:].rearrange("p w k -> p (w k)")).then_inc(q["wnsum"], 1)

            norms(0, 0, 6)
            ps = bank[1]
            for n in range(2 * TILES):
                if n % TILES == 0:
                    pe.wait_ge(q["hit_ready"], n // TILES + 1)
                if n % 8 == 0:
                    pe.wait_ge(q["ix_ready"], n // 8 + 1)
                mm(ps[:, 0:E * CT], lo1[:, n, :], hit[:, n, :], n == 0, False)
                if n >= TILES:
                    last = mm(ps[:, 64:64 + E * CT], lo1[:, n, :], hi1[:, n, :], False, n == 2 * TILES - 1)
            last.then_inc(q["imm"], 1)

            def rows_T(e, j, i, free=True):
                pe.wait_ge(q[f"xe{j}"], 16 * CT * (i + 1))
                if free:
                    pe.wait_ge(q["yt_ready"], 2 * e - 4)
                if not (isinstance(e, int) and e == 0):
                    pe.wait_ge(q["wnrm_ready"], 2 * e + 1)
                for c in range(CT):
                    m = min(P, CAP - c * P)
                    for h in range(HD):
                        last = nc.tensor.transpose(bank[h][:, c * P:c * P + m], xe[j][0:m, c, h * P:(h + 1) * P], ident[0:m, 0:m])
                last.then_inc(q["xtr_ready"], 1)

            def hidden(e, j, f):
                if f >= 4:
                    pe.wait_ge(q["h32_ready"], FK * e + f - 3)
                if f % 4 == 0:
                    pe.wait_ge(q["w_lo"], 4 * e + f // 4 + 1)
                for h in range(HD):
                    for n, (a, b) in enumerate(PAIRS):
                        last = mm(bank[2 + f % 4][:, 0:CAP], w1p[j][a][:, h, f * P:(f + 1) * P], xp[j][b][:, h, :],
                                  h == n == 0, h == 1 and n == 2)
                last.then_inc(q["h_mm"], 1)

            def results_T(e):
                pe.wait_ge(q["yT_ready"], 2 * e + 2)
                for c in range(CT):
                    m = min(P, CAP - c * P)
                    for h in range(HD):
                        w = c * D + h * P
                        last = nc.tensor.transpose(bank[w // 512][0:m, w % 512:w % 512 + P], yT[:, h, c * P:c * P + m], ident)
                last.then_inc(q["ytr_ready"], 1)

            def expert(i, j, first=False, last_=False):
                e = 2 * i + j
                pe.wait_ge(q["xlo_ready"], 2 * e + 2)
                for f in range(FK):
                    hidden(e, j, f)
                    if f == 1 and not last_:
                        if not (first or isinstance(e, int) and e < 2):
                            pe.wait_ge(q["yt_ready"], 2 * e - 2)
                        norms(e + 1, 1 - j)
                    if f == 4 and not last_:
                        rows_T(e + 1, 1 - j, i + j, not (first or isinstance(e, int) and e < 2))
                if not first:
                    pe.wait_ge(q["yT_ready"], 2 * e)
                for f in range(FK):
                    pe.wait_ge(q["h_lo"], FK * e + f + 1)
                    if f % 4 == 0:
                        pe.wait_ge(q["w_lo"], 4 * e + f // 4 + 3)
                    for h in range(HD):
                        for n, (a, b) in enumerate(PAIRS):
                            last = mm(bank[6 + h][:, 0:CAP], w2p[j][a][:, f, h * P:(h + 1) * P], hp[b][:, f, :],
                                      f == n == 0, f == FK - 1 and n == 2)
                    if f == 3 and not first:
                        if not last_:
                            pe.wait_ge(q["xlo_ready"], 2 * e + 4)
                        else:
                            pe.wait_ge(q["yt_ready"], 2 * e - 2)
                        results_T(e - 1)
                last.then_inc(q["y_mm"], 1)

            pe.wait_ge(q["imm_read"], 1)
            rows_T(0, 0, 0, False)
            expert(0, 0, True)
            expert(0, 1)
            with pe.Fori(1, E // 2 - 1) as i:
                for j in range(2):
                    expert(i, j)
            expert(E // 2 - 1, 0)
            expert(E // 2 - 1, 1, last_=True)
            pe.wait_ge(q["yt_ready"], 2 * E - 2)
            results_T(E - 1)

        @block.vector
        def _(dve):
            def rec(g, j, s):
                t = CH * g + ST * j + s
                pj, ps = prev(j, s)
                dve.wait_ge(q["ns_ready"], t + 1)
                dve.wait_ge(q["r_ready"], t + 1)
                nc.vector.tensor_tensor_scan(ub[:], rzb[:, 0:2 * B], NS[j][:, s * 32:s * 32 + 32], 0.0,
                                             ALU.mult, ALU.add).then_inc(q["npre_ready"], 1)
                nc.vector.tensor_scalar(ev(mb[:]), od(rzb[:, 2 * B:4 * B]), -1.0, 1.0, ALU.mult, ALU.add)
                nc.vector.tensor_tensor(od(mb[:]), od(rzb[:, 2 * B:4 * B]), h_of(pj, ps), ALU.mult).then_inc(q["zh_ready"], 1)
                dve.wait_ge(q["sg_ready"], t + 1)
                nc.vector.tensor_tensor(hsb[j][0:SSM, s * B:(s + 1) * B], RZ[j][0:SSM, NW + s * B:NW + (s + 1) * B], sgb[:],
                                        ALU.mult).then_inc(q["hs_done"], 1)
                dve.wait_ge(q["zh_ready"], t + 1)
                dve.wait_ge(q["n_ready"], t + 1)
                nc.vector.tensor_tensor_scan(h1[:], nb[:], mb[:], 0.0, ALU.mult, ALU.add).then_inc(q["h1_done"], 1)
                nc.vector.tensor_tensor_scan(hist[j][:, s * 32:(s + 1) * 32], nb[:], mb[:], 0.0, ALU.mult, ALU.add).then_inc(q["hist_done"], 1)
                dve.wait_ge(q["hist_done"], t + 1)
                nc.vector.tensor_tensor(h2[:], h_of(j, s), od(h1[:]), ALU.subtract).then_inc(q["h2_done"], 1)

            def fuse(n, j, part):
                if part == 0:
                    dve.wait_ge(q["gx_ready"], 2 * n + 2)
                    dve.wait_ge(q[f"xres{j}"], 16 * ((n - j) // 2 + 1) if isinstance(n, int) else 8 * n + (16 - 8 * j))
                    nc.vector.scalar_tensor_tensor(s1a[:], FB[:, 0:D], gxs[:, 0:1], xres[j][:], ALU.mult, ALU.add).then_inc(q["fuse_a"], 1)
                else:
                    dve.wait_ge(q["fuse_a"], n + 1)
                    nc.vector.scalar_tensor_tensor(s1b[:], FB[:, D:2 * D], gxs[:, 1:2], s1a[:], ALU.mult, ALU.add).then_inc(q["fuse_b"], 1)

            def stats_1(n):
                dve.wait_ge(q["fuse_b"], n + 1)
                nc.vector.bn_stats(st1[:], s1b[:]).then_inc(q["stat1"], 1)
                dve.wait_ge(q["init_v"], INIT_V)
                dve.wait_ge(q["stat1"], n + 1)
                nc.vector.bn_aggr(mv1[:], st1[:]).then_inc(q["var1"], 1)

            def norm_1(n, j):
                dve.wait_ge(q["rstd1"], n + 1)
                nc.vector.tensor_scalar(x1[j][:], s1b[:], mv1[:, 0:1], rs1[:], ALU.subtract, ALU.mult).then_inc(q["x1_ready"], 1)

            def rotate(c, h):
                dve.wait_ge(q["q_ready"], c + 1)
                for i, (half, w) in enumerate(((0, 0), (1, 1)) if h == 0 else ((1, 0), (0, 1))):
                    tab = cq[:, bass.ds(c * CH + w * N, CH)].unsqueeze(2).to_broadcast([P, CH, B])
                    last = nc.vector.tensor_tensor(tm[:, 2 * h + i, :].rearrange("p (t b) -> p t b", b=B),
                                                   TB[:, half * 256:(half + 1) * 256].rearrange("p (t b) -> p t b", b=B), tab, ALU.mult)
                last.then_inc(q["qmul_ready"], 1)

            def q_low(c):
                for h in range(HD):
                    dve.wait_ge(q["qh_ready"], 2 * c + h + 1)
                    nc.vector.tensor_tensor(qp[1][:, h].rearrange("p b t -> p t b"), qr[:, h, :].rearrange("p (t b) -> p t b", b=B),
                                            qp[0][:, h].rearrange("p b t -> p t b"), ALU.subtract).then_inc(q["ql_ready"], 1)

            def ret_low(c):
                dve.wait_ge(q["rh_ready"], c + 1)
                nc.vector.tensor_tensor(rp[1][:], ret[:], rp[0][:], ALU.subtract).then_inc(q["rl_ready"], 1)

            def decay(c, bk=SC):
                dve.wait_ge(q["sc_ready"], c + 1)
                m = con("mask")[:, bass.ts(c, CH)].unsqueeze(1).to_broadcast([P, B, CH])
                nc.vector.tensor_tensor(ret[:], bk[:, 0:B * CH].rearrange("p (b t) -> p b t", t=CH), m,
                                        ALU.mult).then_inc(q["ret_ready"], 1)

            def residual(c, h, bk=QB):
                if h == 0:
                    dve.wait_ge(q["x1R_ready"], c + 1)
                    dve.wait_ge(q["pv_ready"], c + 1)
                nc.vector.scalar_tensor_tensor(sT[:, h, :], bk[:, h * 256:(h + 1) * 256], und[:, 2:3], x1R[:, h, :],
                                               ALU.mult, ALU.add).then_inc(q["res_ready"], 1)

            def stats_2(c):
                dve.wait_ge(q["back_ready"], c + 1)
                for i, bk in enumerate((QB, SC)):
                    for h in range(HD):
                        last = nc.vector.bn_stats(st2[:, i, h, :], halves(bk)[:, h, :])
                last.then_inc(q["stat2"], 1)

            def var_2(c):
                dve.wait_ge(q["init_v"], INIT_V)
                dve.wait_ge(q["stat2"], c + 1)
                for i in range(2):
                    last = nc.vector.bn_aggr(mv2[:, i, :], st2[:, i, :, :])
                last.then_inc(q["var2"], 1)

            def logits(c, j):
                if j == 0:
                    dve.wait_ge(q["rstd2"], c + 1)
                bk = (QB, SC)[j]
                nc.vector.scalar_tensor_tensor(lg[:, bass.ds(2 * c + j, 1), :].rearrange("p o e -> p (o e)"), bk[:, P:P + E], rs2[:, j:j + 1],
                                               rgbt[:], ALU.mult, ALU.add).then_inc(q["lg_ready"], 1)

            def norm_2(c, j):
                bk = (QB, SC)[j]
                nc.vector.tensor_scalar(x2[:, bass.ds(2 * c + j, 1), :].rearrange("p o (h d) -> p (o h) d", h=HD), halves(bk), mv2[:, j, 0:1],
                                        rs2[:, j:j + 1], ALU.subtract, ALU.mult).then_inc(q["x2_ready"], 1)

            def k_rotate(m):
                i, o = m // 4, m % 4 // 2
                if m == 0:
                    dve.wait_ge(q["c_load"], 16)
                if m % 2 == 0:
                    dve.wait_ge(q["k_mm"], m // 2 + 1)
                if m % 4 == 0 and i >= 2:
                    dve.wait_ge(q["k_rot"], 2 * i - 2)
                n, name = ((0, "cosk"), (3, "sink"), (2, "cosk"), (1, "sink"))[m % 4]
                nc.vector.tensor_tensor(k_products(i)[:, n, :].rearrange("p (b t) -> p b t", t=N),
                                        (QB, SC)[o][:].rearrange("p (b t) -> p b t", t=N),
                                        con(name).unsqueeze(1).to_broadcast([P, 4, N]), ALU.mult).then_inc(q["k_mul"], 1)

            def norms():
                dve.wait_ge(q["nsum"], 1)
                for h in range(HD):
                    nc.vector.scalar_tensor_tensor(rgi[:, h, (1 - h) * P:(1 - h) * P + E], TB[:, 72:72 + E], -1.0 / D, rgw[:, h, :], ALU.mult, ALU.add)
                    last = nc.vector.tensor_copy(rgi[:, h, h * E:h * E + P], ident)
                last.then_inc(q["gcent"], 1)
                nc.vector.tensor_reduce(nrm[:, 3:4], TB[:, 96:96 + B], AX.X, ALU.max).then_inc(q["cguard"], 1)
                nc.vector.tensor_copy(nrm[:, 0:3], TB[:, 64:67]).then_inc(q["cguard"], 1)
                dve.wait_ge(q["cguard"], 2)
                nc.vector.tensor_scalar(nrm[:], nrm[:], TINY, None, ALU.max).then_inc(q["nrm_done"], 1)

            def scales():
                dve.wait_ge(q["inv_done"], 1)
                nc.vector.tensor_scalar(scl[:, 0:1], inv[:, 0:1], Q_UP, None, ALU.mult)
                nc.vector.tensor_scalar(scl[:, 1:3], inv[:, 1:3], inv[:, 3:4], K_UP, ALU.mult, ALU.mult).then_inc(q["scl_done"], 1)

            def tables():
                dve.wait_ge(q["scl_done"], 1)
                nc.vector.tensor_scalar(cq[:], cst[:, CC["cosq"][0]:CC["sinq"][1]], scl[:, 0:1], None, ALU.mult).then_inc(q["scl_done"], 1)
                nc.vector.tensor_scalar(und[:, 0:1], scl[:, 0:1], scl[:, 1:2], scl[:, 2:3], ALU.mult, ALU.mult).then_inc(q["scl_done"], 1)
                dve.wait_ge(q["scl_done"], 3)
                nc.vector.reciprocal(und[:, 1:2], und[:, 0:1]).then_inc(q["scl_done"], 1)
                dve.wait_ge(q["scl_done"], 4)
                nc.vector.tensor_scalar(und[:, 2:3], und[:, 1:2], 1.0 / RET_DOWN, None, ALU.mult).then_inc(q["scl_done"], 1)

            def low(n):
                i = int(PIECES[n][1:])
                dve.wait_ge(q["kv_hi"], n + 1)
                if PIECES[n][0] == "k":
                    w = bass.ts(i // 2, 512)
                    dst, src, first, k = kp[1][:, i % 2, w], kT[:, i % 2, w], kp[0][:, i % 2, w], 1
                else:
                    w = slice(2 * i, 2 * i + 2)
                    dst, src, first, k = vp[1][:, w, :], vt[:, w, :], vp[0][:, w, :], 2
                nc.vector.scalar_tensor_tensor(dst, src, scl[:, k:k + 1], first, ALU.mult, ALU.subtract).then_inc(q["kv_lo"], 1)

            def iteration(g, A, M):
                for s in range(CH):
                    rec(g, s // ST, s % ST)
                    if A:
                        if s == 0:
                            stats_1(2 * g - 2)
                        if s == 1:
                            norm_1(2 * g - 2, 0)
                        if s == 2:
                            fuse(2 * g - 1, 1, 0)
                        if s == 3:
                            fuse(2 * g - 1, 1, 1)
                    if A:
                        if s == 4:
                            stats_1(2 * g - 1)
                        if s == 5:
                            norm_1(2 * g - 1, 1)
                    if M:
                        if s == 5:
                            decay(g - 2)
                        if s == 10:
                            residual(g - 2, 0)
                            residual(g - 2, 1)
                    if A and s in (11, 12):
                        rotate(g - 1, s - 11)
                    if M:
                        if s == 13:
                            stats_2(g - 2)
                            var_2(g - 2)
                    if s in (14, 15):
                        fuse(2 * g, 0, s - 14)
                        if M:
                            logits(g - 2, s - 14)
                            norm_2(g - 2, s - 14)
                    if not A:
                        if s >= 1:
                            k_rotate(s - 1)
                        if s == 15:
                            norms()
                    elif not M:
                        if s == 0:
                            k_rotate(15)
                        if s == 1:
                            scales()
                        if s == 10:
                            tables()
                        for n in range(len(PIECES)):
                            if LO_STEP[n] == s:
                                low(n)

            nc.vector.memset(rzb[:], 0.0).then_inc(q["init_v"], 1)
            nc.vector.memset(nb[:], 0.0).then_inc(q["init_v"], 1)
            nc.vector.memset(hist[1][:], 0.0).then_inc(q["init_v"], 1)
            nc.vector.memset(hsb[1][0:SSM, :], 0.0).then_inc(q["init_v"], 1)
            for j in range(2):
                nc.vector.memset(hsb[j][SSM:SSM + 2, :], 1.0).then_inc(q["init_v"], 1)
            nc.vector.memset(zero[:], 0.0).then_inc(q["init_v"], 1)
            for j in range(2):
                nc.vector.memset(wsum2[j][:], 0.0).then_inc(q["init_v"], 1)
            nc.vector.memset(ones16[:], 1.0).then_inc(q["init_v"], 1)
            dve.wait_ge(q["w_hh"], 32)
            nc.vector.tensor_copy(bzp[:], bz[:]).then_inc(q["bsplit"], 1)
            nc.vector.tensor_copy(whp[0][:], whh[:]).then_inc(q["wsplit"], 1)
            dve.wait_ge(q["bsplit"], 1)
            nc.vector.tensor_tensor(bzr, bz[:], bzp[:], ALU.subtract).then_inc(q["bsplit"], 1)
            dve.wait_ge(q["wsplit"], 1)
            nc.vector.tensor_tensor(whr, whh[:], whp[0][:], ALU.subtract).then_inc(q["wsplit"], 1)
            dve.wait_ge(q["bsplit"], 2)
            nc.vector.tensor_copy(bzq[0:32, :], bzp[0:32, :])
            nc.vector.tensor_copy(bzq[32:64, :], bzr[32:64, :])
            nc.vector.tensor_copy(bzq[64:96, :], bzr[64:96, :]).then_inc(q["bsplit"], 1)
            dve.wait_ge(q["bsplit"], 3)
            nc.vector.tensor_tensor(bzq[64:96, :], bzr[64:96, :], bzq[64:96, :], ALU.subtract).then_inc(q["bsplit"], 1)
            dve.wait_ge(q["wsplit"], 2)
            nc.vector.tensor_copy(whp[1][:], whr).then_inc(q["wsplit"], 1)
            dve.wait_ge(q["wsplit"], 3)
            nc.vector.tensor_tensor(whp[2][:], whr, whp[1][:], ALU.subtract).then_inc(q["wsplit"], 1)
            dve.wait_ge(q["init_p"], INIT_P)
            nc.vector.memset(h1[:], 0.0).then_inc(q["h1_done"], 1)
            nc.vector.memset(h2[:], 0.0).then_inc(q["h2_done"], 1)
            nc.vector.memset(mb[:], 0.0).then_inc(q["hs_done"], 1)
            nc.vector.memset(st2[:], 0.0).then_inc(q["x2_ready"], 1)
            iteration(0, False, False)
            iteration(1, True, False)
            with dve.Fori(2, CHUNKS) as g:
                iteration(g, True, True)
            n, c = TILES - 1, CHUNKS - 1
            stats_1(n - 1)
            norm_1(n - 1, 0)
            fuse(n, 1, 0)
            fuse(n, 1, 1)
            decay(c - 1)
            stats_1(n)
            norm_1(n, 1)

            step = [0]

            def then(ins):
                step[0] += 1
                ins.then_inc(q["rt"], 1)
                dve.wait_ge(q["rt"], step[0])

            def soften(a, b, part):
                def bk(ap):
                    return ap.unsqueeze(2).to_broadcast([P, b - a, E])

                t = slice(a, b)
                dve.wait_ge(q["lg_ready"], b)
                then(nc.vector.tensor_reduce(mx[:, t], lg[:, t, :], AX.X, ALU.max))
                then(nc.vector.tensor_tensor(pe_[:, t, :], lg[:, t, :], bk(mx[:, t]), ALU.subtract))
                assert step[0] == RT_EXP[part], step[0]
                dve.wait_ge(q["ract"], part + 1)
                then(nc.vector.tensor_reduce(mx[:, t], pe_[:, t, :], AX.X, ALU.add))
                then(nc.vector.reciprocal(mx[:, t], mx[:, t]))
                then(nc.vector.tensor_tensor(pe_[:, t, :], pe_[:, t, :], bk(mx[:, t]), ALU.mult))

            def choose(a, b):
                for k in range(a, b):
                    last = nc.vector.max(top[:, k, :], pe_[:, k, :])
                then(last)
                for k in range(a, b):
                    last = nc.vector.max_index(topi[:, k, :], top[:, k, :], pe_[:, k, :])
                then(last)

            soften(0, TILES - 4, 0)
            rotate(c, 0)
            rotate(c, 1)
            q_low(c)
            residual(c - 1, 0)
            residual(c - 1, 1)
            choose(0, TILES - 4)
            decay(c, NS[0])
            ret_low(c)
            stats_2(c - 1)
            var_2(c - 1)
            for j in range(2):
                logits(c - 1, j)
                norm_2(c - 1, j)
            residual(c, 0, NS[1])
            residual(c, 1, NS[1])
            stats_2(c)
            var_2(c)
            logits(c, 0)
            logits(c, 1)
            soften(TILES - 4, TILES, 1)
            choose(TILES - 4, TILES)
            then(nc.vector.tensor_copy(topf[:], topi[:, :, 0:2]))
            for j in range(2):
                last = nc.vector.tensor_tensor(oh[j][:], topf[:, :, j].unsqueeze(1).to_broadcast([P, E, TILES]),
                                               con("iota").unsqueeze(2).to_broadcast([P, E, TILES]), ALU.is_equal)
            then(last)
            then(nc.vector.tensor_tensor(msk[:], oh[0][:], oh[1][:], ALU.add))
            then(nc.vector.tensor_tensor_scan(cum[:].rearrange("p e k -> p (e k)"), con("keep"), msk[:].rearrange("p e k -> p (e k)"),
                                              0.0, ALU.mult, ALU.add))
            nc.vector.tensor_tensor(pre[:], cum[:], msk[:], ALU.subtract)
            then(nc.vector.tensor_tensor(suf[:], cum[:, :, TILES - 1:TILES].to_broadcast([P, E, TILES]), cum[:], ALU.subtract))
            assert step[0] == RT_CUM, step[0]
            norm_2(c, 0)
            norm_2(c, 1)
            dve.wait_ge(q["rmm"], 1)
            R = bank[0][:, 0:E * TILES].rearrange("p (e k) -> p e k", k=TILES)
            nc.vector.tensor_scalar(ov[:], R, float(CAP), 4.0 * E * CT * P, ALU.is_gt, ALU.mult)
            then(nc.vector.tensor_tensor(rk[:], R, con("slot0").rearrange("p (e k) -> p e k", k=TILES), ALU.add))
            then(nc.vector.tensor_tensor(rk[:], rk[:], ov[:], ALU.add))
            for j in range(2):
                last = nc.vector.tensor_tensor(oh[j][:], oh[j][:], rk[:], ALU.mult)
            then(last)
            for j in range(2):
                last = nc.vector.tensor_reduce(slf[:, j, :], oh[j][:].rearrange("p e k -> p k e"), AX.X, ALU.add)
            then(last)
            then(nc.vector.tensor_copy(slu[:], slf[:]))
            then(nc.vector.tensor_scalar(slu[:], slu[:], P - 1, None, ALU.bitwise_and))
            then(nc.vector.tensor_copy(lo[:], slu[:]))
            nc.vector.tensor_tensor(hi[:], slf[:], lo[:], ALU.subtract).then_inc(q["hi_ready"], 1)
            dve.wait_ge(q["hi_ready"], 1)
            for j in range(2):
                w = slice(j * TILES, (j + 1) * TILES)
                nc.vector.tensor_tensor(hi1[:, w, :], hi[:, j, :].unsqueeze(2).to_broadcast([P, TILES, E * CT]),
                                        iota16[:, P:].unsqueeze(1).to_broadcast([P, TILES, E * CT]), ALU.is_equal).then_inc(q["hi1_ready"], 1)
            flat_lo = lo[:].rearrange("p j k -> p (j k)")
            for n in range(0, 2 * TILES, 8):
                nc.vector.tensor_tensor(lo1[:, n:n + 8, :], flat_lo[:, n:n + 8].unsqueeze(2).to_broadcast([P, 8, P]),
                                        iota16[:, 0:P].unsqueeze(1).to_broadcast([P, 8, P]), ALU.is_equal).then_inc(q["ix_ready"], 1)

            def norms(e, j, bk=1):
                dve.wait_ge(q["wnsum"], e + 1)
                nc.vector.tensor_reduce(wtot[j][:], bank[bk][:, 384:390].rearrange("p (w k) -> p w k", w=2), AX.X, ALU.add).then_inc(q["wnrm_ready"], 1)
                dve.wait_ge(q["wnrm_ready"], 2 * e + 1)
                nc.vector.tensor_scalar(wnrm[j][:], wtot[j][:], TINY, None, ALU.max).then_inc(q["wnrm_ready"], 1)

            def scales(e, j):
                dve.wait_ge(q["winv_ready"], e + 1)
                nc.vector.tensor_scalar(wscl[j][:], winv[j][:], W_UP, None, ALU.mult).then_inc(q["wscl_ready"], 1)
                dve.wait_ge(q["wscl_ready"], 4 * e + 1)
                nc.vector.tensor_scalar(b1s[j][:], b1t[:, bass.ds(e * FK, FK)], wscl[j][:, 0:1], None, ALU.mult).then_inc(q["wscl_ready"], 1)
                nc.vector.tensor_tensor(wprod[j][:], wscl[j][:, 0:1], wscl[j][:, 1:2], ALU.mult).then_inc(q["wscl_ready"], 1)
                dve.wait_ge(q["wscl_ready"], 4 * e + 3)
                nc.vector.reciprocal(wund[j][:], wprod[j][:]).then_inc(q["wscl_ready"], 1)

            def w_low(e, j, p):
                dve.wait_ge(q["w_hi"], 4 * e + p + 1)
                nc.vector.scalar_tensor_tensor(quarter(w1p[j][1], w2p[j][1], p), quarter(w1t[j], w2t[j], p), wscl[j][:, p // 2:p // 2 + 1],
                                               quarter(w1p[j][0], w2p[j][0], p), ALU.mult, ALU.subtract).then_inc(q["w_lo"], 1)

            norms(0, 0, 6)
            dve.wait_ge(q["imm"], 1)
            then(nc.vector.tensor_copy(v1[:], bank[1][:, 0:E * CT]))
            nc.vector.tensor_copy(v2[:], bank[1][:, 64:64 + E * CT]).then_inc(q["imm_read"], 1)
            nc.vector.tensor_scalar(gix[:], v1[:], -1.0, 0.0, ALU.add, ALU.max).then_inc(q["gix_ready"], 1)
            dve.wait_ge(q["imm_read"], 1)
            then(nc.vector.scalar_tensor_tensor(v2[:], v2[:], float(S), v1[:], ALU.mult, ALU.add))
            then(nc.vector.tensor_scalar(v1[:], v1[:], 0.0, 4.0 * S, ALU.is_equal, ALU.mult))
            nc.vector.scalar_tensor_tensor(six[:], v2[:], -1.0, v1[:], ALU.add, ALU.add).then_inc(q["gix_ready"], 1)

            nc.vector.tensor_tensor(wsum[:], top[:, :, 0], top[:, :, 1], ALU.add).then_inc(q["ws_ready"], 1)
            dve.wait_ge(q["ws_ready"], 1)
            nc.vector.reciprocal(wsum[:], wsum[:]).then_inc(q["ws_ready"], 1)
            dve.wait_ge(q["ws_ready"], 2)
            for j in range(2):
                nc.vector.tensor_tensor(wt[:, j, :], top[:, :, j], wsum[:], ALU.mult)
            def rows_low(e, j):
                for h in range(HD):
                    dve.wait_ge(q["xhi_ready"], 2 * e + h + 1)
                    nc.vector.tensor_tensor(xp[j][1][:, h, :], bank[h][:, 0:CAP], xp[j][0][:, h, :], ALU.subtract).then_inc(q["xlo_ready"], 1)

            def h_high(e, f):
                dve.wait_ge(q["h32_ready"], FK * e + f + 1)
                nc.vector.tensor_copy(hp[0][:, f, :], h32[:, f % 4, :]).then_inc(q["h_hi"], 1)

            def h_low(e, f):
                dve.wait_ge(q["h_hi"], FK * e + f + 1)
                nc.vector.tensor_tensor(hp[1][:, f, :], h32[:, f % 4, :], hp[0][:, f, :], ALU.subtract).then_inc(q["h_lo"], 1)

            def results(e, j, stored):
                dve.wait_ge(q["ytr_ready"], e + 1)
                if stored is not None:
                    dve.wait_ge(q[f"yst{j}"], stored)
                nc.vector.tensor_copy(yt[j][:, 0:2, :], bank[0][:].rearrange("p (c d) -> p c d", c=2)).then_inc(q["yt_ready"], 1)
                nc.vector.tensor_copy(yt[j][0:CAP - 2 * P, 2, :], bank[1][0:CAP - 2 * P, 0:D]).then_inc(q["yt_ready"], 1)

            def expert(i, j, last=False):
                e = 2 * i + j
                for f in range(FK):
                    h_high(e, f)
                    if f == 1 and not last:
                        norms(e + 1, 1 - j)
                    if f >= 1:
                        h_low(e, f - 1)
                    if f == 4 and not last:
                        scales(e + 1, 1 - j)
                    if f == 6 and not last:
                        rows_low(e + 1, 1 - j)
                h_low(e, FK - 1)
                for p in range(4):
                    if not last:
                        w_low(e + 1, 1 - j, p)
                    if p == 3 and not (isinstance(e, int) and e == 0):
                        pi = i if j else i - 1
                        results(e - 1, 1 - j, None if isinstance(e, int) and e < 3 else 16 * CT * pi)

            scales(0, 0)
            for p in range(3):
                w_low(0, 0, p)
            rows_low(0, 0)
            w_low(0, 0, 3)
            expert(0, 0)
            expert(0, 1)
            expert(1, 0)
            expert(1, 1)
            with dve.Fori(2, E // 2 - 1) as i:
                for j in range(2):
                    expert(i, j)
            expert(E // 2 - 1, 0)
            expert(E // 2 - 1, 1, True)
            results(E - 1, 1, 16 * CT * (E // 2 - 1))

            for c in range(CHUNKS):
                dve.wait_ge(q[f"yl{c}"], 32)
                k = 2 * c + 1
                nc.vector.scalar_tensor_tensor(ca[k % 4], yg[c][:, 1, :], wt[:, 0, k:k + 1], x2[:, k, :], ALU.mult, ALU.add).then_inc(q["c_odd"], 1)
                for i in range(2):
                    k = 2 * c + i
                    dve.wait_ge(q["c_odd" if i else "c_even"], c + 1)
                    if c >= 2:
                        dve.wait_ge(q["o_ready"], c - 1)
                    nc.vector.scalar_tensor_tensor(cb[k % 4], yg[c][:, 2 + i, :], wt[:, 1, k:k + 1], ca[k % 4], ALU.mult, ALU.add).then_inc(q["c_b"], 1)
                for i in range(2):
                    k = 2 * c + i
                    dve.wait_ge(q["c_b"], k + 1)
                    last = nc.vector.bn_stats(st3[:, i, :], cb[k % 4])
                last.then_inc(q["stat3"], 1)
                dve.wait_ge(q["stat3"], c + 1)
                for i in range(2):
                    last = nc.vector.bn_aggr(mv3[:, c, i, :], st3[:, i, :])
                last.then_inc(q["var3"], 1)


INIT_V, INIT_P = 10, 3
RT_EXP = (2, 9)
RT_CUM = 19


def _constants():
    import numpy as np
    f = np.float32
    c = np.zeros((P, CW), f)

    def put(name, a):
        c[:a.shape[0], CC[name][0]:CC[name][1]] = a

    put("ident", np.eye(P, dtype=f))
    d = D
    base = ((np.arange(0, d, 2, dtype=f) + f(0.4 * d)) / f(1.4 * d)).astype(f)
    pos = np.arange(N, dtype=f)
    freqs = (f(1.0) / np.power(f(10000.0), np.arange(d // 2, dtype=f) / f(d // 2))).astype(f)
    ang = (pos[:, None] * freqs[None, :]).astype(f).astype(np.float64)
    scale = base[None, :].astype(np.float64) ** (pos[:, None] / 512.0)
    put("cosq", (np.cos(ang) * scale).T)
    put("sinq", (np.sin(ang) * scale).T)
    put("cosk", (np.cos(ang) / scale).T)
    put("sink", (np.sin(ang) / scale).T)
    u, v = np.arange(N)[None, :], np.arange(N)[:, None]
    put("mask", np.where(u >= v, 0.96875 ** np.maximum(u - v, 0).astype(np.float64), 0.0) * RET_DOWN)
    tl, b = np.arange(P) // B, np.arange(P) % B
    put("le", (b[:, None] <= b[None, :]).astype(f))
    put("diag", ((b[:, None] < b[None, :]) | ((b[:, None] == b[None, :]) & (tl[:, None] <= tl[None, :]))).astype(f))
    put("lt", (b[:, None] < b[None, :]).astype(f))
    put("slot0", np.tile(np.repeat(np.arange(E) * CT * P - 1.0, TILES), (P, 1)))
    put("keep", np.tile(np.tile((np.arange(TILES) > 0).astype(f), E), (P, 1)))
    put("iota", np.tile(np.arange(E, dtype=f), (P, 1)))
    put("tok", np.arange(TILES)[None, :] * P + np.arange(P)[:, None] + 1.0)
    return c


def _bias_selection():
    import numpy as np
    sel = np.zeros((3, 32, 512), np.float16)
    rz = sel[:, :, 0:256].reshape(3, 32, ST, 2, B)
    rz[:, 0, :, 0], rz[:, 3, :, 0], rz[:, 1, :, 1], rz[:, 4, :, 1] = 1, 1, 1, 1
    hn = sel[:, :, 256:].reshape(3, 32, ST, B, 2)
    hn[:, 5, :, :, 0], hn[:, 2, :, :, 1] = 1, 1
    return sel.reshape(3 * 32, 512)


def kernel(**inputs):
    import numpy as np
    import concourse.bacc as _bacc
    from concourse.bass_utils import run_bass_kernel_spmd as _run

    a = {k: np.asarray(v) for k, v in inputs.items()}
    p = "L0_attn_"
    order = np.concatenate([np.arange(0, D, 2), np.arange(1, D, 2)])
    b_rows = np.zeros((3, 32, RNN + D), np.float32)
    b_rows[:, 0:6, 0:RNN] = np.concatenate([a[p + "b_ih"].reshape(3, RNN), a[p + "b_hh"].reshape(3, RNN)])
    b_rows[:, 0, RNN:] = a[p + "proj_b"]
    arrays = {
        "xtok": a["x"].transpose(1, 0, 2).reshape(S, D),
        "xT": a["x"].transpose(2, 1, 0).reshape(D, S),
        "ctxT": a["ctx_1024"].transpose(2, 0, 1).reshape(D, S),
        "consts": _constants(),
        "AbE": np.concatenate([a[p + "A"].T, a[p + "Bb"][None], np.zeros((1, SSM), np.float32)]),
        "BwT": a[p + "Bw"].T,
        "CwE": np.concatenate([a[p + "Cw"].T, a[p + "Cb"][None], a[p + "Db"][None]]),
        "DwT": a[p + "Dw"].T,
        "W_ihT": a[p + "W_ih"].T,
        "b_rows": b_rows.reshape(3 * 32, RNN + D),
        "bsel": _bias_selection(),
        "iota": np.tile(np.concatenate([np.arange(P), np.arange(E * CT) * P]).astype(np.float16), (P, 1)),
        "W_hhT": a[p + "W_hh"].T,
        "projT": a[p + "proj_w"].T,
        "gateT": a[p + "gate_w"].T,
        "gate_b": a[p + "gate_b"].reshape(1, 2),
        "WqT": a["L0_xattn_Wq"][order].T,
        "WkT": a["L0_xattn_Wk"][order].T,
        "WvT": a["L0_xattn_Wv"].T,
        "rgwT": a["L0_ffn_gate_w"],
        "rgb": a["L0_ffn_gate_b"].reshape(1, E),
        "w1": a["L0_ffn_w1"],
        "b1": a["L0_ffn_b1"].reshape(E, FK, P).transpose(2, 0, 1).reshape(P, E * FK),
        "w2": a["L0_ffn_w2"],
        "b2": a["L0_ffn_b2"].reshape(E, HD, P).transpose(2, 0, 1).reshape(P, E * HD),
    }
    nc = _bacc.Bacc("TRN2", target_bir_lowering=False, num_devices=1)
    feeds, args = {}, []
    for name, v in arrays.items():
        v = np.ascontiguousarray(v)
        feeds[f"in_{name}"] = v
        args.append(nc.dram_tensor(f"in_{name}", v.shape, mybir.dt.from_np(v.dtype), kind="ExternalInput").ap())
    args.append(nc.dram_tensor("out_tok", (S, D), F32, kind="ExternalOutput").ap())
    mk_decoder_kernel(nc, *args)
    r = _run(nc, [feeds], core_ids=[0])
    got = r.results[0]["out_tok"]
    return np.ascontiguousarray(got.reshape(N, B, D).transpose(1, 0, 2))
```
